# Optimizing a Trainium2 kernel written in Bass

```python
import numpy as np
import jax
import jax.numpy as jnp

def _softmax(x, axis=-1):
    return jax.nn.softmax(x, axis=axis)

def _gelu(x):
    return jax.nn.gelu(x, approximate=True)

def _silu(x):
    return jax.nn.silu(x)

def _sigmoid(x):
    return jax.nn.sigmoid(x)

def _layernorm(x, axis=-1, eps=1e-05):
    m = jnp.mean(x, axis=axis, keepdims=True)
    v = jnp.var(x, axis=axis, keepdims=True)
    return (x - m) / jnp.sqrt(v + eps)

def _scatter_add(tgt, idx, src, axis=0):
    return tgt.at[idx].add(src)

def _segment_sum(src, seg, n):
    return jax.ops.segment_sum(src, seg, n)
kernel_name = 'mk_seq_postln_d4_jaxref_r8_1dd683'

def setup_inputs(seed: int=0):
    np.random.seed(seed)
    _w = jnp.asarray

    def _L0_attn_setup():
        import jax, jax.numpy as jnp
        import numpy as np
        B, S, H, N, D = (2, 256, 128, 16, 64)
        PAD = -30000.0
        key = jax.random.key(seed)
        kx, kqkv, kout, krpe = jax.random.split(key, 4)
        x = jax.random.normal(kx, (B, S, H), jnp.float32)
        qkv = jax.random.normal(kqkv, (H, 3, N, D), jnp.float32) * H ** (-0.5)
        out_w = jax.random.normal(kout, (N, D, H), jnp.float32) * (N * D) ** (-0.5)
        rpe_bias = jax.random.normal(krpe, (N, S), jnp.float32) * 0.02
        return {'x': x, 'qkv': qkv, 'out_w': out_w, 'rpe_bias': rpe_bias}
    _L0_attn_in = _L0_attn_setup()

    def _L0_ffn_setup():
        import jax, jax.numpy as jnp
        import numpy as np
        key = jax.random.key(seed)
        ks = jax.random.split(key, 5)
        B, Sq, M, E, H = (4, 256, 128, 8, 512)
        x = jax.random.normal(ks[0], (B, Sq, M), dtype=jnp.float32)
        wg = jax.random.normal(ks[1], (M, E), dtype=jnp.float32) * (1.0 / np.sqrt(M))
        w1 = jax.random.normal(ks[2], (E, M, H), dtype=jnp.float32) * (1.0 / np.sqrt(M))
        b1 = jnp.zeros((E, H), dtype=jnp.float32)
        w2 = jax.random.normal(ks[3], (E, H, M), dtype=jnp.float32) * (1.0 / np.sqrt(H))
        b2 = jnp.zeros((E, M), dtype=jnp.float32)
        return {'x': x, 'wg': wg, 'w1': w1, 'b1': b1, 'w2': w2, 'b2': b2}
    _L0_ffn_in = _L0_ffn_setup()

    def _L1_attn_setup():
        import jax, jax.numpy as jnp
        import numpy as np
        B, S, H = (2, 256, 128)
        NQ, NKV, HD, RANK = (16, 4, 64, 8)
        THETA = 10000.0
        LORA_SCALE = 16 / RANK
        ATTN_SCALE = 1.0 / np.sqrt(HD)

        def _lora_proj(x, W, A, Bm):
            return x @ W.T + x @ A.T @ Bm.T * LORA_SCALE

        def _rope(x, cos_h, sin_h):
            x1, x2 = (x[..., ::2], x[..., 1::2])
            return jnp.concatenate([x1 * cos_h - x2 * sin_h, x1 * sin_h + x2 * cos_h], axis=-1)

        def _forward(x, Wq, Wk, Wv, Wo, qA, qB, kA, kB, vA, vB, oA, oB):
            b, s, _ = x.shape
            q = _lora_proj(x, Wq, qA, qB).reshape(b, s, NQ, HD).transpose(0, 2, 1, 3)
            k = _lora_proj(x, Wk, kA, kB).reshape(b, s, NKV, HD).transpose(0, 2, 1, 3)
            v = _lora_proj(x, Wv, vA, vB).reshape(b, s, NKV, HD).transpose(0, 2, 1, 3)
            inv_freq = 1.0 / THETA ** (jnp.arange(0, HD, 2, dtype=jnp.float32) / HD)
            freqs = jnp.arange(s, dtype=jnp.float32)[:, None] * inv_freq[None, :]
            cos_h = jnp.cos(freqs)[None, None]
            sin_h = jnp.sin(freqs)[None, None]
            q = _rope(q, cos_h, sin_h)
            k = _rope(k, cos_h, sin_h)
            rep = NQ // NKV
            k = jnp.repeat(k, rep, axis=1)
            v = jnp.repeat(v, rep, axis=1)
            attn = jax.nn.softmax(jnp.einsum('bhqd,bhkd->bhqk', q, k) * ATTN_SCALE, axis=-1)
            out = jnp.einsum('bhqk,bhkd->bhqd', attn, v)
            out = out.transpose(0, 2, 1, 3).reshape(b, s, NQ * HD)
            return _lora_proj(out, Wo, oA, oB)
        key = jax.random.key(seed)
        ks = jax.random.split(key, 14)
        n = lambda k, shape, s: jax.random.normal(k, shape, jnp.float32) * s
        return {'x': n(ks[0], (B, S, H), 1.0), 'Wq': n(ks[1], (NQ * HD, H), 0.02), 'Wk': n(ks[2], (NKV * HD, H), 0.02), 'Wv': n(ks[3], (NKV * HD, H), 0.02), 'Wo': n(ks[4], (H, NQ * HD), 0.02), 'qA': n(ks[5], (RANK, H), 0.05), 'qB': n(ks[6], (NQ * HD, RANK), 0.05), 'kA': n(ks[7], (RANK, H), 0.05), 'kB': n(ks[8], (NKV * HD, RANK), 0.05), 'vA': n(ks[9], (RANK, H), 0.05), 'vB': n(ks[10], (NKV * HD, RANK), 0.05), 'oA': n(ks[11], (RANK, NQ * HD), 0.05), 'oB': n(ks[12], (H, RANK), 0.05)}
    _L1_attn_in = _L1_attn_setup()

    def _L1_ffn_setup():
        import jax, jax.numpy as jnp
        import numpy as np
        from jax.scipy.linalg import expm
        B, S, D, E, K, NROT = (2, 256, 128, 8, 2, 3)
        EPS = 1e-05

        def _gelu(x):
            return jax.nn.gelu(x, approximate=False)

        def _forward(x, ln_gamma, ln_beta, abel_w, abel_b, moe_gate_w, moe_gate_b, ew1, eb1, ew2, eb2, gens, gc_w, gc_b):
            residual = x
            mu = jnp.mean(x, axis=-1, keepdims=True)
            var = jnp.mean((x - mu) ** 2, axis=-1, keepdims=True)
            xn = (x - mu) * jax.lax.rsqrt(var + EPS) * ln_gamma + ln_beta
            abel_out = _gelu(xn @ abel_w + abel_b)
            logits = xn @ moe_gate_w + moe_gate_b
            topw, topi = jax.lax.top_k(logits, K)
            topw = jax.nn.softmax(topw, axis=-1)
            w_dense = jnp.sum(jax.nn.one_hot(topi, E, dtype=xn.dtype) * topw[..., None], axis=-2)
            h = _gelu(jnp.einsum('bsd,edh->ebsh', xn, ew1) + eb1[:, None, None, :])
            eo = jnp.einsum('ebsh,ehd->ebsd', h, ew2) + eb2[:, None, None, :]
            moe_out = jnp.einsum('ebsd,bse->bsd', eo, w_dense)
            for i in range(NROT):
                moe_out = moe_out @ expm(gens[i])
            combined = jnp.concatenate([abel_out, moe_out], axis=-1)
            gate = jax.nn.sigmoid(combined @ gc_w + gc_b)
            mixed = abel_out * (1.0 - gate) + moe_out * gate
            return residual + mixed
        key = jax.random.key(seed)
        ks = jax.random.split(key, 16)
        sc = 0.02
        x = jax.random.normal(ks[0], (B, S, D), jnp.float32)
        ln_gamma = 1.0 + sc * jax.random.normal(ks[1], (D,), jnp.float32)
        ln_beta = sc * jax.random.normal(ks[2], (D,), jnp.float32)
        abel_w = sc * jax.random.normal(ks[3], (D, D), jnp.float32)
        abel_b = sc * jax.random.normal(ks[4], (D,), jnp.float32)
        moe_gate_w = sc * jax.random.normal(ks[5], (D, E), jnp.float32)
        moe_gate_b = sc * jax.random.normal(ks[6], (E,), jnp.float32)
        ew1 = sc * jax.random.normal(ks[7], (E, D, 2 * D), jnp.float32)
        eb1 = sc * jax.random.normal(ks[8], (E, 2 * D), jnp.float32)
        ew2 = sc * jax.random.normal(ks[9], (E, 2 * D, D), jnp.float32)
        eb2 = sc * jax.random.normal(ks[10], (E, D), jnp.float32)
        g = sc * jax.random.normal(ks[11], (NROT, D, D), jnp.float32)
        gens = 0.5 * (g - jnp.swapaxes(g, -1, -2))
        gc_w = sc * jax.random.normal(ks[12], (2 * D, 1), jnp.float32)
        gc_b = sc * jax.random.normal(ks[13], (1,), jnp.float32)
        return dict(x=x, ln_gamma=ln_gamma, ln_beta=ln_beta, abel_w=abel_w, abel_b=abel_b, moe_gate_w=moe_gate_w, moe_gate_b=moe_gate_b, ew1=ew1, eb1=eb1, ew2=ew2, eb2=eb2, gens=gens, gc_w=gc_w, gc_b=gc_b)
    _L1_ffn_in = _L1_ffn_setup()

    def _L2_attn_setup():
        import jax, jax.numpy as jnp
        import numpy as np
        D = 128
        H = 16
        KVH = 4
        HD = D // H
        LAT = 32
        WIN = 32
        B, S = (1, 256)
        BASE_G, BASE_L = (1000000.0, 10000.0)
        EPS = 1e-06

        def rmsnorm(x, w):
            return x * jax.lax.rsqrt(jnp.mean(x * x, axis=-1, keepdims=True) + EPS) * w

        def qk_norm(x):
            return x * jax.lax.rsqrt(jnp.mean(x * x, axis=-1, keepdims=True) + EPS)

        def rope(x, base):
            s, hd = (x.shape[-2], x.shape[-1])
            inv_freq = 1.0 / base ** (jnp.arange(0, hd, 2, dtype=jnp.float32) / hd)
            freqs = jnp.arange(s, dtype=jnp.float32)[:, None] * inv_freq[None, :]
            cos, sin = (jnp.cos(freqs), jnp.sin(freqs))
            xe, xo = (x[..., ::2], x[..., 1::2])
            out = jnp.stack([xe * cos - xo * sin, xe * sin + xo * cos], axis=-1)
            return out.reshape(x.shape)

        def split_heads(x, n_heads):
            b, s, _ = x.shape
            return x.reshape(b, s, n_heads, HD).transpose(0, 2, 1, 3)

        def repeat_kv(x):
            return jnp.repeat(x, H // KVH, axis=1)

        def sdpa(q, k, v, mask):
            scores = jnp.einsum('bhqd,bhkd->bhqk', q, k) / np.sqrt(HD).astype(np.float32)
            scores = jnp.where(mask, scores, jnp.float32(-1e+30))
            probs = jax.nn.softmax(scores, axis=-1)
            return jnp.einsum('bhqk,bhkd->bhqd', probs, v)

        def merge_heads(x):
            b, h, s, hd = x.shape
            return x.transpose(0, 2, 1, 3).reshape(b, s, h * hd)

        def global_latent_attn(x, wq, w_kv_down, w_k_up, w_v_up, wo):
            q = split_heads(x @ wq, H)
            latent = x @ w_kv_down
            k = split_heads(latent @ w_k_up, KVH)
            v = split_heads(latent @ w_v_up, KVH)
            q, k = (rope(q, BASE_G), rope(k, BASE_G))
            q, k = (qk_norm(q), qk_norm(k))
            k, v = (repeat_kv(k), repeat_kv(v))
            i = jnp.arange(x.shape[1])
            causal = i[:, None] >= i[None, :]
            return merge_heads(sdpa(q, k, v, causal)) @ wo

        def local_gqa_attn(x, wq, wk, wv, wo):
            q = split_heads(x @ wq, H)
            k = split_heads(x @ wk, KVH)
            v = split_heads(x @ wv, KVH)
            q, k = (rope(q, BASE_L), rope(k, BASE_L))
            q, k = (qk_norm(q), qk_norm(k))
            k, v = (repeat_kv(k), repeat_kv(v))
            i = jnp.arange(x.shape[1])
            diff = i[:, None] - i[None, :]
            mask = (diff >= 0) & (diff < WIN)
            return merge_heads(sdpa(q, k, v, mask)) @ wo
        key = jax.random.key(seed)
        ks = jax.random.split(key, 12)
        std = 0.02
        return {'hidden': jax.random.normal(ks[0], (B, S, D), dtype=jnp.float32), 'norm1_w': jnp.ones((D,), jnp.float32), 'norm2_w': jnp.ones((D,), jnp.float32), 'g_wq': jax.random.normal(ks[1], (D, H * HD), jnp.float32) * std, 'g_kv_down': jax.random.normal(ks[2], (D, LAT), jnp.float32) * std, 'g_k_up': jax.random.normal(ks[3], (LAT, KVH * HD), jnp.float32) * std, 'g_v_up': jax.random.normal(ks[4], (LAT, KVH * HD), jnp.float32) * std, 'g_wo': jax.random.normal(ks[5], (D, D), jnp.float32) * std, 'l_wq': jax.random.normal(ks[6], (D, H * HD), jnp.float32) * std, 'l_wk': jax.random.normal(ks[7], (D, KVH * HD), jnp.float32) * std, 'l_wv': jax.random.normal(ks[8], (D, KVH * HD), jnp.float32) * std, 'l_wo': jax.random.normal(ks[9], (D, D), jnp.float32) * std}
    _L2_attn_in = _L2_attn_setup()

    def _L2_ffn_setup():
        import jax, jax.numpy as jnp
        import numpy as np
        N_EXPERTS = 8
        TOP_K = 2
        D_MODEL = 128
        HIDDEN = 512
        ROUTED_H = 128
        BATCH, SEQ = (2, 512)
        key = jax.random.key(seed)
        ks = jax.random.split(key, 8)
        std = 0.02
        return {'x': jax.random.normal(ks[0], (BATCH, SEQ, D_MODEL), dtype=jnp.float32), 'w12': std * jax.random.normal(ks[1], (N_EXPERTS, 2 * ROUTED_H, D_MODEL), dtype=jnp.float32), 'w3': std * jax.random.normal(ks[2], (N_EXPERTS, D_MODEL, ROUTED_H), dtype=jnp.float32), 'shared_w1': std * jax.random.normal(ks[3], (HIDDEN, D_MODEL), dtype=jnp.float32), 'shared_w2': std * jax.random.normal(ks[4], (HIDDEN, D_MODEL), dtype=jnp.float32), 'shared_w3': std * jax.random.normal(ks[5], (D_MODEL, HIDDEN), dtype=jnp.float32), 'router_w': std * jax.random.normal(ks[6], (N_EXPERTS, D_MODEL), dtype=jnp.float32), 'expert_bias': jnp.zeros((N_EXPERTS,), dtype=jnp.float32)}
    _L2_ffn_in = _L2_ffn_setup()

    def _L3_attn_setup():
        import math
        import jax, jax.numpy as jnp
        import numpy as np
        B, S, D, H, DH = (2, 256, 128, 16, 64)
        INNER = H * DH

        def _l2norm(t):
            n = jnp.linalg.norm(t, axis=-1, keepdims=True)
            return t / jnp.maximum(n, 1e-12)
        key = jax.random.key(seed)
        k0, k1, k2, k3 = jax.random.split(key, 4)
        x = jax.random.normal(k0, (B, S, D), dtype=jnp.float32)
        w_q = jax.random.normal(k1, (D, INNER), dtype=jnp.float32) * 0.02
        w_kv = jax.random.normal(k2, (D, 2 * INNER), dtype=jnp.float32) * 0.02
        w_out = jax.random.normal(k3, (INNER, D), dtype=jnp.float32) * 0.02
        b_out = jnp.zeros((D,), dtype=jnp.float32)
        scale_init = -math.log(math.log2(S ** 2 - S))
        scale = jnp.full((1, H, 1, 1), scale_init, dtype=jnp.float32)
        return {'x': x, 'w_q': w_q, 'w_kv': w_kv, 'w_out': w_out, 'b_out': b_out, 'scale': scale}
    _L3_attn_in = _L3_attn_setup()

    def _L3_ffn_setup():
        import jax, jax.numpy as jnp
        import numpy as np
        LN_EPS = 1e-05

        def _layernorm(x, g, b):
            m = jnp.mean(x, axis=-1, keepdims=True)
            v = jnp.mean(jnp.square(x - m), axis=-1, keepdims=True)
            return (x - m) * jax.lax.rsqrt(v + LN_EPS) * g + b
        K_TOP = 2
        key = jax.random.key(seed)
        ks = jax.random.split(key, 4)
        B, N, D, E = (8, 256, 128, 4)
        s = 0.02
        return {'x': jax.random.normal(ks[0], (B, N, D), dtype=jnp.float32), 'gate_W': jax.random.normal(ks[1], (D, E), dtype=jnp.float32) * s, 'gate_b': jnp.zeros((E,), jnp.float32), 'W1': jax.random.normal(ks[2], (E, D, D), dtype=jnp.float32) * s, 'b1': jnp.zeros((E, D), jnp.float32), 'g1': jnp.ones((E, D), jnp.float32), 'be1': jnp.zeros((E, D), jnp.float32), 'W2': jax.random.normal(ks[3], (E, D, D), dtype=jnp.float32) * s, 'b2': jnp.zeros((E, D), jnp.float32), 'g2': jnp.ones((E, D), jnp.float32), 'be2': jnp.zeros((E, D), jnp.float32)}
    _L3_ffn_in = _L3_ffn_setup()
    _d = {'L0_attn_x': _L0_attn_in['x'], 'L0_attn_qkv': _L0_attn_in['qkv'], 'L0_attn_out_w': _L0_attn_in['out_w'], 'L0_attn_rpe_bias': _L0_attn_in['rpe_bias'], 'L0_ffn_wg': _L0_ffn_in['wg'], 'L0_ffn_w1': _L0_ffn_in['w1'], 'L0_ffn_b1': _L0_ffn_in['b1'], 'L0_ffn_w2': _L0_ffn_in['w2'], 'L0_ffn_b2': _L0_ffn_in['b2'], 'L1_attn_Wq': _L1_attn_in['Wq'], 'L1_attn_Wk': _L1_attn_in['Wk'], 'L1_attn_Wv': _L1_attn_in['Wv'], 'L1_attn_Wo': _L1_attn_in['Wo'], 'L1_attn_qA': _L1_attn_in['qA'], 'L1_attn_qB': _L1_attn_in['qB'], 'L1_attn_kA': _L1_attn_in['kA'], 'L1_attn_kB': _L1_attn_in['kB'], 'L1_attn_vA': _L1_attn_in['vA'], 'L1_attn_vB': _L1_attn_in['vB'], 'L1_attn_oA': _L1_attn_in['oA'], 'L1_attn_oB': _L1_attn_in['oB'], 'L1_ffn_ln_gamma': _L1_ffn_in['ln_gamma'], 'L1_ffn_ln_beta': _L1_ffn_in['ln_beta'], 'L1_ffn_abel_w': _L1_ffn_in['abel_w'], 'L1_ffn_abel_b': _L1_ffn_in['abel_b'], 'L1_ffn_moe_gate_w': _L1_ffn_in['moe_gate_w'], 'L1_ffn_moe_gate_b': _L1_ffn_in['moe_gate_b'], 'L1_ffn_ew1': _L1_ffn_in['ew1'], 'L1_ffn_eb1': _L1_ffn_in['eb1'], 'L1_ffn_ew2': _L1_ffn_in['ew2'], 'L1_ffn_eb2': _L1_ffn_in['eb2'], 'L1_ffn_gens': _L1_ffn_in['gens'], 'L1_ffn_gc_w': _L1_ffn_in['gc_w'], 'L1_ffn_gc_b': _L1_ffn_in['gc_b'], 'L2_attn_norm1_w': _L2_attn_in['norm1_w'], 'L2_attn_norm2_w': _L2_attn_in['norm2_w'], 'L2_attn_g_wq': _L2_attn_in['g_wq'], 'L2_attn_g_kv_down': _L2_attn_in['g_kv_down'], 'L2_attn_g_k_up': _L2_attn_in['g_k_up'], 'L2_attn_g_v_up': _L2_attn_in['g_v_up'], 'L2_attn_g_wo': _L2_attn_in['g_wo'], 'L2_attn_l_wq': _L2_attn_in['l_wq'], 'L2_attn_l_wk': _L2_attn_in['l_wk'], 'L2_attn_l_wv': _L2_attn_in['l_wv'], 'L2_attn_l_wo': _L2_attn_in['l_wo'], 'L2_ffn_w12': _L2_ffn_in['w12'], 'L2_ffn_w3': _L2_ffn_in['w3'], 'L2_ffn_shared_w1': _L2_ffn_in['shared_w1'], 'L2_ffn_shared_w2': _L2_ffn_in['shared_w2'], 'L2_ffn_shared_w3': _L2_ffn_in['shared_w3'], 'L2_ffn_router_w': _L2_ffn_in['router_w'], 'L2_ffn_expert_bias': _L2_ffn_in['expert_bias'], 'L3_attn_w_q': _L3_attn_in['w_q'], 'L3_attn_w_kv': _L3_attn_in['w_kv'], 'L3_attn_w_out': _L3_attn_in['w_out'], 'L3_attn_b_out': _L3_attn_in['b_out'], 'L3_attn_scale': _L3_attn_in['scale'], 'L3_ffn_gate_W': _L3_ffn_in['gate_W'], 'L3_ffn_gate_b': _L3_ffn_in['gate_b'], 'L3_ffn_W1': _L3_ffn_in['W1'], 'L3_ffn_b1': _L3_ffn_in['b1'], 'L3_ffn_g1': _L3_ffn_in['g1'], 'L3_ffn_be1': _L3_ffn_in['be1'], 'L3_ffn_W2': _L3_ffn_in['W2'], 'L3_ffn_b2': _L3_ffn_in['b2'], 'L3_ffn_g2': _L3_ffn_in['g2'], 'L3_ffn_be2': _L3_ffn_in['be2']}
    _x0 = _d['L0_attn_x']
    _d['L0_attn_x'] = jax.random.normal(jax.random.fold_in(jax.random.key(seed), 1), (16, 256, 128), dtype=_x0.dtype)
    del _x0
    return _d

def reference(L0_attn_x, L0_attn_qkv, L0_attn_out_w, L0_attn_rpe_bias, L0_ffn_wg, L0_ffn_w1, L0_ffn_b1, L0_ffn_w2, L0_ffn_b2, L1_attn_Wq, L1_attn_Wk, L1_attn_Wv, L1_attn_Wo, L1_attn_qA, L1_attn_qB, L1_attn_kA, L1_attn_kB, L1_attn_vA, L1_attn_vB, L1_attn_oA, L1_attn_oB, L1_ffn_ln_gamma, L1_ffn_ln_beta, L1_ffn_abel_w, L1_ffn_abel_b, L1_ffn_moe_gate_w, L1_ffn_moe_gate_b, L1_ffn_ew1, L1_ffn_eb1, L1_ffn_ew2, L1_ffn_eb2, L1_ffn_gens, L1_ffn_gc_w, L1_ffn_gc_b, L2_attn_norm1_w, L2_attn_norm2_w, L2_attn_g_wq, L2_attn_g_kv_down, L2_attn_g_k_up, L2_attn_g_v_up, L2_attn_g_wo, L2_attn_l_wq, L2_attn_l_wk, L2_attn_l_wv, L2_attn_l_wo, L2_ffn_w12, L2_ffn_w3, L2_ffn_shared_w1, L2_ffn_shared_w2, L2_ffn_shared_w3, L2_ffn_router_w, L2_ffn_expert_bias, L3_attn_w_q, L3_attn_w_kv, L3_attn_w_out, L3_attn_b_out, L3_attn_scale, L3_ffn_gate_W, L3_ffn_gate_b, L3_ffn_W1, L3_ffn_b1, L3_ffn_g1, L3_ffn_be1, L3_ffn_W2, L3_ffn_b2, L3_ffn_g2, L3_ffn_be2):

    def _L0_attn_ref(x, qkv, out_w, rpe_bias):
        import jax, jax.numpy as jnp
        import numpy as np
        B, S, H, N, D = (2, 256, 128, 16, 64)
        PAD = -30000.0
        q, k, v = jnp.einsum('bsx,xMnd->Mbnsd', x, qkv)
        s = x.shape[1]
        a = jnp.einsum('bnsd,bntd->bnst', q, k) * q.shape[-1] ** (-0.5)
        cum = jnp.cumsum(rpe_bias[:, :s], axis=-1)
        rel = jnp.arange(s)[:, None] - jnp.arange(s)[None, :]
        bias = jnp.where(rel >= 0, cum[:, jnp.clip(rel, 0)], PAD)
        a = jax.nn.softmax(a + bias, axis=-1)
        mix = jnp.einsum('bnst,bntd->bnsd', a, v)
        return jnp.einsum('bnsd,ndx->bsx', mix, out_w)

    def _L0_ffn_ref(x, wg, w1, b1, w2, b2):
        import jax, jax.numpy as jnp
        import numpy as np
        B, Sq, M = x.shape
        E = wg.shape[1]
        S = B * Sq
        C = S // E
        xt = x.reshape(S, M)
        gates = jax.nn.softmax(xt @ wg, axis=-1)
        expert_idx = jnp.argmax(gates, axis=-1)
        mask1 = jax.nn.one_hot(expert_idx, E, dtype=xt.dtype)
        locations = jnp.cumsum(mask1, axis=0) - 1.0
        pos = jnp.sum(locations * mask1, axis=1).astype(jnp.int32)
        keep = (pos < C).astype(xt.dtype)
        gate_val = jnp.sum(gates * mask1, axis=1) * keep
        slot = expert_idx.astype(jnp.int32) * C + jnp.clip(pos, 0, C - 1)
        disp = jnp.zeros((E * C, M), dtype=xt.dtype).at[slot].add(xt * keep[:, None])
        disp = disp.reshape(E, C, M)
        h = jax.nn.relu(jnp.einsum('ecm,emh->ech', disp, w1) + b1[:, None, :])
        eo = jnp.einsum('ech,ehm->ecm', h, w2) + b2[:, None, :]
        out = eo.reshape(E * C, M)[slot] * gate_val[:, None]
        return out.reshape(B, Sq, M)

    def _L1_attn_ref(x, Wq, Wk, Wv, Wo, qA, qB, kA, kB, vA, vB, oA, oB):
        import jax, jax.numpy as jnp
        import numpy as np
        B, S, H = (2, 256, 128)
        NQ, NKV, HD, RANK = (16, 4, 64, 8)
        THETA = 10000.0
        LORA_SCALE = 16 / RANK
        ATTN_SCALE = 1.0 / np.sqrt(HD)

        def _lora_proj(x, W, A, Bm):
            return x @ W.T + x @ A.T @ Bm.T * LORA_SCALE

        def _rope(x, cos_h, sin_h):
            x1, x2 = (x[..., ::2], x[..., 1::2])
            return jnp.concatenate([x1 * cos_h - x2 * sin_h, x1 * sin_h + x2 * cos_h], axis=-1)

        def _forward(x, Wq, Wk, Wv, Wo, qA, qB, kA, kB, vA, vB, oA, oB):
            b, s, _ = x.shape
            q = _lora_proj(x, Wq, qA, qB).reshape(b, s, NQ, HD).transpose(0, 2, 1, 3)
            k = _lora_proj(x, Wk, kA, kB).reshape(b, s, NKV, HD).transpose(0, 2, 1, 3)
            v = _lora_proj(x, Wv, vA, vB).reshape(b, s, NKV, HD).transpose(0, 2, 1, 3)
            inv_freq = 1.0 / THETA ** (jnp.arange(0, HD, 2, dtype=jnp.float32) / HD)
            freqs = jnp.arange(s, dtype=jnp.float32)[:, None] * inv_freq[None, :]
            cos_h = jnp.cos(freqs)[None, None]
            sin_h = jnp.sin(freqs)[None, None]
            q = _rope(q, cos_h, sin_h)
            k = _rope(k, cos_h, sin_h)
            rep = NQ // NKV
            k = jnp.repeat(k, rep, axis=1)
            v = jnp.repeat(v, rep, axis=1)
            attn = jax.nn.softmax(jnp.einsum('bhqd,bhkd->bhqk', q, k) * ATTN_SCALE, axis=-1)
            out = jnp.einsum('bhqk,bhkd->bhqd', attn, v)
            out = out.transpose(0, 2, 1, 3).reshape(b, s, NQ * HD)
            return _lora_proj(out, Wo, oA, oB)
        return _forward(x, Wq, Wk, Wv, Wo, qA, qB, kA, kB, vA, vB, oA, oB)

    def _L1_ffn_ref(x, ln_gamma, ln_beta, abel_w, abel_b, moe_gate_w, moe_gate_b, ew1, eb1, ew2, eb2, gens, gc_w, gc_b):
        import jax, jax.numpy as jnp
        import numpy as np
        from jax.scipy.linalg import expm
        B, S, D, E, K, NROT = (2, 256, 128, 8, 2, 3)
        EPS = 1e-05

        def _gelu(x):
            return jax.nn.gelu(x, approximate=False)

        def _forward(x, ln_gamma, ln_beta, abel_w, abel_b, moe_gate_w, moe_gate_b, ew1, eb1, ew2, eb2, gens, gc_w, gc_b):
            residual = x
            mu = jnp.mean(x, axis=-1, keepdims=True)
            var = jnp.mean((x - mu) ** 2, axis=-1, keepdims=True)
            xn = (x - mu) * jax.lax.rsqrt(var + EPS) * ln_gamma + ln_beta
            abel_out = _gelu(xn @ abel_w + abel_b)
            logits = xn @ moe_gate_w + moe_gate_b
            topw, topi = jax.lax.top_k(logits, K)
            topw = jax.nn.softmax(topw, axis=-1)
            w_dense = jnp.sum(jax.nn.one_hot(topi, E, dtype=xn.dtype) * topw[..., None], axis=-2)
            h = _gelu(jnp.einsum('bsd,edh->ebsh', xn, ew1) + eb1[:, None, None, :])
            eo = jnp.einsum('ebsh,ehd->ebsd', h, ew2) + eb2[:, None, None, :]
            moe_out = jnp.einsum('ebsd,bse->bsd', eo, w_dense)
            for i in range(NROT):
                moe_out = moe_out @ expm(gens[i])
            combined = jnp.concatenate([abel_out, moe_out], axis=-1)
            gate = jax.nn.sigmoid(combined @ gc_w + gc_b)
            mixed = abel_out * (1.0 - gate) + moe_out * gate
            return residual + mixed
        return _forward(x, ln_gamma, ln_beta, abel_w, abel_b, moe_gate_w, moe_gate_b, ew1, eb1, ew2, eb2, gens, gc_w, gc_b)

    def _L2_attn_ref(hidden, norm1_w, norm2_w, g_wq, g_kv_down, g_k_up, g_v_up, g_wo, l_wq, l_wk, l_wv, l_wo):
        import jax, jax.numpy as jnp
        import numpy as np
        D = 128
        H = 16
        KVH = 4
        HD = D // H
        LAT = 32
        WIN = 32
        B, S = (1, 256)
        BASE_G, BASE_L = (1000000.0, 10000.0)
        EPS = 1e-06

        def rmsnorm(x, w):
            return x * jax.lax.rsqrt(jnp.mean(x * x, axis=-1, keepdims=True) + EPS) * w

        def qk_norm(x):
            return x * jax.lax.rsqrt(jnp.mean(x * x, axis=-1, keepdims=True) + EPS)

        def rope(x, base):
            s, hd = (x.shape[-2], x.shape[-1])
            inv_freq = 1.0 / base ** (jnp.arange(0, hd, 2, dtype=jnp.float32) / hd)
            freqs = jnp.arange(s, dtype=jnp.float32)[:, None] * inv_freq[None, :]
            cos, sin = (jnp.cos(freqs), jnp.sin(freqs))
            xe, xo = (x[..., ::2], x[..., 1::2])
            out = jnp.stack([xe * cos - xo * sin, xe * sin + xo * cos], axis=-1)
            return out.reshape(x.shape)

        def split_heads(x, n_heads):
            b, s, _ = x.shape
            return x.reshape(b, s, n_heads, HD).transpose(0, 2, 1, 3)

        def repeat_kv(x):
            return jnp.repeat(x, H // KVH, axis=1)

        def sdpa(q, k, v, mask):
            scores = jnp.einsum('bhqd,bhkd->bhqk', q, k) / np.sqrt(HD).astype(np.float32)
            scores = jnp.where(mask, scores, jnp.float32(-1e+30))
            probs = jax.nn.softmax(scores, axis=-1)
            return jnp.einsum('bhqk,bhkd->bhqd', probs, v)

        def merge_heads(x):
            b, h, s, hd = x.shape
            return x.transpose(0, 2, 1, 3).reshape(b, s, h * hd)

        def global_latent_attn(x, wq, w_kv_down, w_k_up, w_v_up, wo):
            q = split_heads(x @ wq, H)
            latent = x @ w_kv_down
            k = split_heads(latent @ w_k_up, KVH)
            v = split_heads(latent @ w_v_up, KVH)
            q, k = (rope(q, BASE_G), rope(k, BASE_G))
            q, k = (qk_norm(q), qk_norm(k))
            k, v = (repeat_kv(k), repeat_kv(v))
            i = jnp.arange(x.shape[1])
            causal = i[:, None] >= i[None, :]
            return merge_heads(sdpa(q, k, v, causal)) @ wo

        def local_gqa_attn(x, wq, wk, wv, wo):
            q = split_heads(x @ wq, H)
            k = split_heads(x @ wk, KVH)
            v = split_heads(x @ wv, KVH)
            q, k = (rope(q, BASE_L), rope(k, BASE_L))
            q, k = (qk_norm(q), qk_norm(k))
            k, v = (repeat_kv(k), repeat_kv(v))
            i = jnp.arange(x.shape[1])
            diff = i[:, None] - i[None, :]
            mask = (diff >= 0) & (diff < WIN)
            return merge_heads(sdpa(q, k, v, mask)) @ wo
        x = hidden
        x = x + global_latent_attn(rmsnorm(x, norm1_w), g_wq, g_kv_down, g_k_up, g_v_up, g_wo)
        x = x + local_gqa_attn(rmsnorm(x, norm2_w), l_wq, l_wk, l_wv, l_wo)
        return x

    def _L2_ffn_ref(x, w12, w3, shared_w1, shared_w2, shared_w3, router_w, expert_bias):
        import jax, jax.numpy as jnp
        import numpy as np
        N_EXPERTS = 8
        TOP_K = 2
        D_MODEL = 128
        HIDDEN = 512
        ROUTED_H = 128
        BATCH, SEQ = (2, 512)
        b, s, d = x.shape
        xf = x.reshape(-1, d)
        shared = jax.nn.silu(xf @ shared_w1.T) * (xf @ shared_w2.T) @ shared_w3.T
        scores = jax.nn.sigmoid(xf @ router_w.T)
        _, top_idx = jax.lax.top_k(scores + expert_bias, TOP_K)
        mask = jax.nn.one_hot(top_idx, N_EXPERTS, dtype=xf.dtype).sum(axis=-2)
        gates = scores * mask
        h12 = jnp.einsum('td,ehd->teh', xf, w12)
        h1, h2 = jnp.split(h12, 2, axis=-1)
        h = jax.nn.silu(h1) * h2 * gates[:, :, None]
        routed = jnp.einsum('teh,edh->td', h, w3)
        return (shared + routed).reshape(b, s, d)

    def _L3_attn_ref(x, w_q, w_kv, w_out, b_out, scale):
        import math
        import jax, jax.numpy as jnp
        import numpy as np
        B, S, D, H, DH = (2, 256, 128, 16, 64)
        INNER = H * DH

        def _l2norm(t):
            n = jnp.linalg.norm(t, axis=-1, keepdims=True)
            return t / jnp.maximum(n, 1e-12)
        b, s, _ = x.shape
        h = scale.shape[1]
        q = (x @ w_q).reshape(b, s, h, -1).transpose(0, 2, 1, 3)
        kv = x @ w_kv
        k, v = jnp.split(kv, 2, axis=-1)
        k = k.reshape(b, s, h, -1).transpose(0, 2, 1, 3)
        v = v.reshape(b, s, h, -1).transpose(0, 2, 1, 3)
        q = _l2norm(q) * jnp.exp(scale)
        k = _l2norm(k)
        sim = jnp.einsum('bhid,bhjd->bhij', q, k)
        attn = jax.nn.softmax(sim, axis=-1)
        out = jnp.einsum('bhij,bhjd->bhid', attn, v)
        out = out.transpose(0, 2, 1, 3).reshape(b, s, h * out.shape[-1])
        return out @ w_out + b_out

    def _L3_ffn_ref(x, gate_W, gate_b, W1, b1, g1, be1, W2, b2, g2, be2):
        import jax, jax.numpy as jnp
        import numpy as np
        LN_EPS = 1e-05

        def _layernorm(x, g, b):
            m = jnp.mean(x, axis=-1, keepdims=True)
            v = jnp.mean(jnp.square(x - m), axis=-1, keepdims=True)
            return (x - m) * jax.lax.rsqrt(v + LN_EPS) * g + b
        K_TOP = 2
        B, N, D = x.shape
        BN = B * N
        xf = x.reshape(BN, D)
        gate_scores = xf @ gate_W + gate_b
        topk_scores, topk_idx = jax.lax.top_k(gate_scores, K_TOP)
        weights = jax.nn.softmax(topk_scores, axis=-1)

        def expert(w1, bb1, gg1, bbe1, w2, bb2, gg2, bbe2):
            h = jax.nn.relu(_layernorm(xf @ w1 + bb1, gg1, bbe1))
            return _layernorm(h @ w2 + bb2, gg2, bbe2)
        all_out = jax.vmap(expert)(W1, b1, g1, be1, W2, b2, g2, be2)
        exp_out = all_out[topk_idx, jnp.arange(BN)[:, None]]
        out = jnp.sum(weights[..., None] * exp_out, axis=1)
        return (out + xf).reshape(B, N, D)
    x = L0_attn_x
    x = _layernorm(x + _L0_attn_ref(x, L0_attn_qkv, L0_attn_out_w, L0_attn_rpe_bias), axis=-1)
    x = _layernorm(x + _L0_ffn_ref(x, L0_ffn_wg, L0_ffn_w1, L0_ffn_b1, L0_ffn_w2, L0_ffn_b2), axis=-1)
    x = _layernorm(x + _L1_attn_ref(x, L1_attn_Wq, L1_attn_Wk, L1_attn_Wv, L1_attn_Wo, L1_attn_qA, L1_attn_qB, L1_attn_kA, L1_attn_kB, L1_attn_vA, L1_attn_vB, L1_attn_oA, L1_attn_oB), axis=-1)
    x = _layernorm(x + _L1_ffn_ref(x, L1_ffn_ln_gamma, L1_ffn_ln_beta, L1_ffn_abel_w, L1_ffn_abel_b, L1_ffn_moe_gate_w, L1_ffn_moe_gate_b, L1_ffn_ew1, L1_ffn_eb1, L1_ffn_ew2, L1_ffn_eb2, L1_ffn_gens, L1_ffn_gc_w, L1_ffn_gc_b), axis=-1)
    x = _layernorm(x + _L2_attn_ref(x, L2_attn_norm1_w, L2_attn_norm2_w, L2_attn_g_wq, L2_attn_g_kv_down, L2_attn_g_k_up, L2_attn_g_v_up, L2_attn_g_wo, L2_attn_l_wq, L2_attn_l_wk, L2_attn_l_wv, L2_attn_l_wo), axis=-1)
    x = _layernorm(x + _L2_ffn_ref(x, L2_ffn_w12, L2_ffn_w3, L2_ffn_shared_w1, L2_ffn_shared_w2, L2_ffn_shared_w3, L2_ffn_router_w, L2_ffn_expert_bias), axis=-1)
    x = _layernorm(x + _L3_attn_ref(x, L3_attn_w_q, L3_attn_w_kv, L3_attn_w_out, L3_attn_b_out, L3_attn_scale), axis=-1)
    x = _layernorm(x + _L3_ffn_ref(x, L3_ffn_gate_W, L3_ffn_gate_b, L3_ffn_W1, L3_ffn_b1, L3_ffn_g1, L3_ffn_be1, L3_ffn_W2, L3_ffn_b2, L3_ffn_g2, L3_ffn_be2), axis=-1)
    return x

_drawn_inputs = setup_inputs


def setup_inputs(seed=0):
    import zlib

    import numpy as np

    out = dict(_drawn_inputs(seed))
    spreads = {'L0_ffn_b1': (0.0, 0.1),
     'L0_ffn_b2': (0.0, 0.1),
     'L2_attn_norm1_w': (1.0, 0.6),
     'L2_attn_norm2_w': (1.0, 0.6),
     'L2_ffn_expert_bias': (0.0, 0.478),
     'L3_attn_b_out': (0.0, 0.1),
     'L3_attn_scale': (-2.772235631942749, 0.6),
     'L3_ffn_gate_b': (0.0, 0.1),
     'L3_ffn_b1': (0.0, 0.1),
     'L3_ffn_g1': (1.0, 0.2),
     'L3_ffn_be1': (0.0, 0.315),
     'L3_ffn_b2': (0.0, 0.1),
     'L3_ffn_g2': (1.0, 0.2),
     'L3_ffn_be2': (0.0, 0.1)}
    factors = {'L1_attn_Wq': 6.702,
     'L1_attn_Wk': 7.072,
     'L1_attn_qA': 8.0,
     'L1_attn_qB': 8.0,
     'L1_attn_kA': 8.0,
     'L1_attn_kB': 8.0,
     'L1_ffn_ln_gamma': 8.0,
     'L1_ffn_ln_beta': 8.0,
     'L1_ffn_abel_b': 5.128,
     'L1_ffn_moe_gate_w': 3.003,
     'L1_ffn_moe_gate_b': 8.0,
     'L1_ffn_ew1': 3.025,
     'L1_ffn_eb1': 8.0,
     'L1_ffn_ew2': 3.547,
     'L1_ffn_eb2': 3.873,
     'L1_ffn_gens': 4.649,
     'L1_ffn_gc_w': 8.0,
     'L2_attn_g_wq': 8.0,
     'L2_attn_g_kv_down': 8.0,
     'L2_attn_g_k_up': 8.0,
     'L2_attn_g_v_up': 8.0,
     'L2_attn_g_wo': 8.0,
     'L2_attn_l_wq': 3.673,
     'L2_attn_l_wk': 3.298,
     'L2_attn_l_wv': 2.788,
     'L2_ffn_w12': 3.726,
     'L2_ffn_w3': 4.128,
     'L2_ffn_router_w': 4.156,
     'L3_attn_w_q': 8.0}
    for name, (base, spread) in spreads.items():
        noise = np.random.default_rng([zlib.crc32(name.encode()), seed]).standard_normal(out[name].shape)
        drawn = base * np.exp(spread * noise) if base else spread * noise
        out[name] = jnp.asarray(drawn.astype(out[name].dtype))
    for name, factor in factors.items():
        out[name] = (out[name] * factor).astype(out[name].dtype)
    return out
```

```python
from contextlib import ExitStack

import numpy as np

import concourse.bass as bass
from concourse import mybir

F32 = mybir.dt.float32
U32 = mybir.dt.uint32
I32 = mybir.dt.int32
ALU = mybir.AluOpType
ACT = mybir.ActivationFunctionType
AX = mybir.AxisListType.X

P = 128
ALL_B, S = 16, 256
B = 2
T = B * S
GROUPS = ALL_B // B
ALL_T = ALL_B * S
NT = T // P
NE = 8
CAP = ALL_T // NE
SC = S // P
NH, HD = 16, 64
NCH = NH * HD // P
PAD = -30000.0
LN_EPS = 1e-5
RMS_EPS = 1e-6


def chunked(a):
    c = a.shape[0] // P
    return np.ascontiguousarray(a.reshape(c, P, -1).transpose(1, 0, 2).reshape(P, -1))


def on_all_partitions(v):
    return np.broadcast_to(v.reshape(1, -1), (P, v.size))


def constants():
    i = np.arange(P)
    c = {}
    c["ident"] = np.eye(P)
    c["flip"] = np.eye(P)[::-1]
    j, u = np.arange(S)[:, None], np.arange(S)[None, :]
    c["revtri"] = chunked((j <= S - 1 - u).astype(np.float32))
    c["upto"] = (i[:, None] <= i[None, :])
    c["ones"] = np.ones((P, P))
    c["slot0"] = np.broadcast_to(CAP * np.arange(8.0), (P, 8))
    c["rows32"] = (i[:, None] // 32 == np.arange(4)[None, :])
    c["iota8"] = np.broadcast_to(np.arange(8.0), (P, 8))
    c["desc8"] = np.broadcast_to(8 - np.arange(8.0), (P, 8))
    c["neghalf"] = np.full((P, P), -0.5)
    inv = 1.0 / 10000.0 ** (np.arange(0, HD, 2, dtype=np.float32) / np.float32(HD))
    ang = np.arange(S, dtype=np.float32)[None, :] * inv.astype(np.float32)[:, None]
    cos, sin = np.cos(ang), np.sin(ang)
    ch = np.tile(np.concatenate([cos, cos]), (2, B))
    sh = np.tile(np.concatenate([-sin, sin]), (2, B))
    c["rope_cos"], c["rope_sin"] = ch, sh
    for tag, base in (("g", 1000000.0), ("l", 10000.0)):
        inv = (1.0 / np.float32(base) ** (np.arange(0, 8, 2, dtype=np.float32) / np.float32(8))).astype(np.float32)
        ang = np.arange(S, dtype=np.float32)[:, None] * inv[None, :]
        for nm, f in (("cos", np.cos), ("sin", np.sin)):
            t = np.tile(f(ang), (B, 1)).reshape(NT, P, 4).transpose(1, 0, 2)
            c[f"{tag}_{nm}"] = t.reshape(P, -1)
    d = i[None, :] - i[:, None]
    c["causal"] = (d >= 0)
    c["near"] = (d >= 0) & (d < 32)
    c["near_prev"] = (d + P < 32)
    return {k: np.ascontiguousarray(v, dtype=np.float32) for k, v in c.items()}


def layout(w):
    rows = lambda a: a
    L = {}
    qkv = w["L0_attn_qkv"].reshape(P, 3, NH * HD)
    L["first"] = [("rpe", chunked(w["L0_attn_rpe_bias"].T)), ("wg", w["L0_ffn_wg"])]
    L["l0a"] = [("wq", qkv[:, 0]), ("wk", qkv[:, 1]), ("wv", qkv[:, 2]),
                ("wo", chunked(w["L0_attn_out_w"].reshape(NH * HD, P)))]
    w1 = w["L0_ffn_w1"]
    w2 = w["L0_ffn_w2"].reshape(NE, 4, P, P).transpose(0, 2, 1, 3).reshape(NE, P, 4 * P)
    b1 = w["L0_ffn_b1"].reshape(NE, 4, P).transpose(0, 2, 1)
    b2 = np.broadcast_to(w["L0_ffn_b2"][:, None, :], (NE, P, P))
    L["l0f"] = [("all", np.concatenate([w1, w2, b1, b2], axis=2).reshape(NE * P, -1))]
    L["gens"] = [("a", w["L1_ffn_gens"].transpose(1, 0, 2).reshape(P, -1)),
                 ("aT", w["L1_ffn_gens"].transpose(2, 0, 1).reshape(P, -1))]
    half = np.arange(0, HD, 2)
    fwd = np.concatenate([half, half + 1])
    bwd = np.concatenate([half + 1, half])

    def by_head(a, order, twice=False):
        h = a.reshape(-1, HD, a.shape[1])[:, order]
        if twice:
            h = np.repeat(h, 2, axis=0)
        return h.reshape(-1, a.shape[1]).T

    L["l1a"] = []
    for nm, tw in (("q", False), ("k", True)):
        for tag, order in (("", fwd), ("s", bwd)):
            L["l1a"].append((f"w{nm}{tag}", by_head(w[f"L1_attn_W{nm}"], order, tw)))
    L["l1a"].append(("wv", w["L1_attn_Wv"].T))
    L["l1a"].append(("wo", chunked(w["L1_attn_Wo"].T)))
    L["lora"] = []
    for nm, tw in (("q", False), ("k", True)):
        L["lora"].append((f"{nm}A", w[f"L1_attn_{nm}A"]))
        for tag, order in (("", fwd), ("s", bwd)):
            L["lora"].append((f"{nm}B{tag}", by_head(w[f"L1_attn_{nm}B"], order, tw)))
    L["lora"] += [("vA", w["L1_attn_vA"]), ("vB", w["L1_attn_vB"].T), ("oA", w["L1_attn_oA"]), ("oB", w["L1_attn_oB"].T)]
    L["eb2"] = [("eb2", w["L1_ffn_eb2"])]
    L["be2"] = [("be2", w["L3_ffn_be2"])]
    L["l1f"] = [("gamma", w["L1_ffn_ln_gamma"].reshape(P, 1)), ("beta", w["L1_ffn_ln_beta"].reshape(P, 1)),
                ("abel_w", w["L1_ffn_abel_w"]), ("abel_b", on_all_partitions(w["L1_ffn_abel_b"])),
                ("gate_w", w["L1_ffn_moe_gate_w"]), ("gate_b", on_all_partitions(w["L1_ffn_moe_gate_b"])),
                ("eb1", w["L1_ffn_eb1"].reshape(8, 2, P).transpose(2, 0, 1).reshape(P, -1)),
                ("gc_w", on_all_partitions(w["L1_ffn_gc_w"])), ("gc_b", on_all_partitions(w["L1_ffn_gc_b"])),
                ("ew1", w["L1_ffn_ew1"].transpose(1, 0, 2).reshape(P, -1)),
                ("ew2", w["L1_ffn_ew2"].reshape(8, 2, P, P).transpose(2, 0, 1, 3).reshape(P, -1))]
    L["l2a"] = [("n1", w["L2_attn_norm1_w"].reshape(P, 1)), ("n2", w["L2_attn_norm2_w"].reshape(P, 1)),
                ("g_wq", w["L2_attn_g_wq"]), ("g_down", w["L2_attn_g_kv_down"]), ("g_wo", w["L2_attn_g_wo"]),
                ("l_wq", w["L2_attn_l_wq"]), ("l_wkv", np.concatenate([w["L2_attn_l_wk"], w["L2_attn_l_wv"]], 1)),
                ("l_wo", w["L2_attn_l_wo"])]
    L["l2up"] = [("up", np.concatenate([w["L2_attn_g_k_up"], w["L2_attn_g_v_up"]], 1))]
    L["l2f"] = [("rw", w["L2_ffn_router_w"].T), ("eb", on_all_partitions(w["L2_ffn_expert_bias"])),
                ("s1", w["L2_ffn_shared_w1"].T), ("s2", w["L2_ffn_shared_w2"].T), ("s3", chunked(w["L2_ffn_shared_w3"].T)),
                ("w12", w["L2_ffn_w12"].transpose(2, 0, 1).reshape(P, -1)),
                ("w3", w["L2_ffn_w3"].transpose(2, 0, 1).reshape(P, -1))]
    kv = w["L3_attn_w_kv"]
    L["l3a"] = [("wq", w["L3_attn_w_q"]), ("wk", kv[:, :NH * HD]), ("wv", kv[:, NH * HD:]),
                ("wo", chunked(w["L3_attn_w_out"])), ("bo", on_all_partitions(w["L3_attn_b_out"])),
                ("scale", on_all_partitions(w["L3_attn_scale"]))]
    L["l3f"] = [("gw", w["L3_ffn_gate_W"]), ("gb", on_all_partitions(w["L3_ffn_gate_b"])),
                ("w1", w["L3_ffn_W1"].transpose(1, 0, 2).reshape(P, -1)),
                ("b1", on_all_partitions(w["L3_ffn_b1"])),
                ("g1", w["L3_ffn_g1"].T), ("be1", w["L3_ffn_be1"].T),
                ("w2", w["L3_ffn_W2"].transpose(1, 0, 2).reshape(P, -1)),
                ("b2", on_all_partitions(w["L3_ffn_b2"])),
                ("g2", on_all_partitions(w["L3_ffn_g2"]))]
    L["const"] = list(constants().items())
    return L


def program(nc, x_dram, packs, where, out, dram):
    ctx = ExitStack()
    with ctx:
        def sb(name, shape, dt=F32):
            return ctx.enter_context(nc.sbuf_tensor(name, shape, dt))

        def sem(name):
            return ctx.enter_context(nc.semaphore(name))

        body_sems = []

        loop_scope = [ExitStack()]

        def bsem(name):
            body_sems.append(loop_scope[0].enter_context(nc.semaphore(name)))
            return body_sems[-1]

        def end_of_body():
            with nc.Block() as block:
                @block.gpsimd
                def _(pool):
                    for s_ in body_sems:
                        pool.sem_clear(s_)
            body_sems.clear()

        def end_of_loop():
            loop_scope[0].close()
            loop_scope[0] = ExitStack()

        x_all = sb("x_all", [P, GROUPS * NT, P])
        x_tok = sb("x_tok", [P, NT, P])
        xT = sb("xT", [P, T])
        r_tok = sb("r_tok", [P, NT, P])
        bigA = sb("bigA", [P, NCH, T])
        bigB = sb("bigB", [P, NCH, T])
        bigC = sb("bigC", [P, NT, NH * HD])
        bigD = sb("bigD", [P, NT, NH * HD])
        bias_t = sb("bias_t", [P, NH, S])
        prob = sb("prob", [P, 4, SC, S])
        probT = sb("probT", [P, 3, 4, P])
        raw = prob
        nmax = sb("nmax", [P, B * NH, SC])
        sums = sb("sums", [P, 8, SC, 4])
        rsum = sb("rsum", [P, 8, SC, 4])
        rot = sb("rot", [P, P])
        stats = sb("stats", [P, 16, 6])
        mv = sb("mv", [P, 16, 2])
        var_e = sb("var_e", [P, 16])
        rstd = sb("rstd", [P, 16])
        newton = sb("newton", [P, 128])
        tiny = sb("tiny", [P, 24, NT * NE])
        ix8 = sb("ix8", [P, NT, 8], U32)
        taken = sb("taken", [P, NE])
        slot_f = sb("slot_f", [P, NT])
        slot_w = sb("slot_w", [P, GROUPS * NT], U32)
        slot_r = sb("slot_r", [P, GROUPS * NT], U32)
        gate0 = sb("gate0", [P, GROUPS * NT])
        bank = [ctx.enter_context(nc.psum_tensor(f"bank{i}", [P, 512], F32)) for i in range(8)]

        def flat(t):
            return t[:, :, :].rearrange("p a b -> p (a b)")

        held = {}
        lora_cols = packs["lora"].shape[1]
        home_l0a = sb("home_l0a", [P, max(packs["l0a"].shape[1], packs["l3a"].shape[1])])
        held["l0a"] = home_l0a[:, 0:packs["l0a"].shape[1]]
        held["l3a"] = home_l0a[:, 0:packs["l3a"].shape[1]]
        early, late = ("l1a", "l1f"), ("l2a", "l2up", "l2f", "l3f")
        width = {pk: ap.shape[1] for pk, ap in packs.items()}
        home_l1 = sb("home_l1", [P, max(sum(width[pk] for pk in early), sum(width[pk] for pk in late))])
        for some in (early, late):
            at = 0
            for pk in some:
                held[pk] = home_l1[0:packs[pk].shape[0], at:at + width[pk]]
                at += width[pk]
        held["gens"] = flat(bigB)[:, 0:width["gens"]]
        for pk in ("first", "const", "eb2", "be2"):
            held[pk] = sb(f"w_{pk}", list(packs[pk].shape))[:, :]
        loaded = {pk: sem(f"loaded_{pk}") for pk in packs}
        loaded_x = sem("loaded_x")

        def W(pk, part):
            a, b = where[pk][part]
            return held[pk][:, a:b]

        def v3(ap, n):
            return ap.rearrange("p (a b) -> p a b", a=n)

        ident = W("const", "ident")
        neghalf = W("const", "neghalf")

        class Chain:
            def __init__(self, eng, s_):
                self.eng, self.sem, self.n = eng, s_, 0

            def __call__(self, ins):
                self.n += 1
                ins.then_inc(self.sem, 1)
                self.eng.wait_ge(self.sem, self.n)

        def rsqrt(dve, step, v, y, t):
            step(dve.tensor_scalar(y.bitcast(I32), v.bitcast(I32), -0.5, 1597463007.0, ALU.mult, ALU.add))
            for _ in range(3):
                step(dve.scalar_tensor_tensor(out=t, in0=v, scalar=-0.5, in1=y, op0=ALU.mult, op1=ALU.mult))
                step(dve.tensor_tensor(t, t, y, ALU.mult))
                step(dve.scalar_tensor_tensor(out=y, in0=t, scalar=1.5, in1=y, op0=ALU.add, op1=ALU.mult))

        def first_loads():
            with nc.Block() as block:
                @block.sync
                def _(sp):
                    x_view = x_dram.rearrange("b (c p) d -> p (b c) d", p=P)
                    for pk in ("const", "first", "gens", "l0a"):
                        sp.dma_start(held[pk], packs[pk]).then_inc(loaded[pk], 16)
                    sp.dma_start(x_all[:, :, :], x_view).then_inc(loaded_x, 16)
                    for pk in ("l1a", "l1f", "eb2", "be2"):
                        sp.dma_start(held[pk], packs[pk]).then_inc(loaded[pk], 16)

        def post_norm(tag, last=False, group=None):
            stat_done, mean_done, step_s = bsem(f"{tag}_stat"), bsem(f"{tag}_mean"), bsem(f"{tag}_step")
            x_done, xt_done, stored = bsem(f"{tag}_x"), bsem(f"{tag}_xt"), bsem(f"{tag}_stored")
            with nc.Block() as block:
                @block.vector
                def _(dve):
                    for t in range(NT):
                        dve.bn_stats(stats[:, t, :], r_tok[:, t, :]).then_inc(stat_done, 1)
                    for t in range(NT):
                        dve.wait_ge(stat_done, t + 1)
                        dve.bn_aggr(mv[:, t, :], stats[:, t, :]).then_inc(mean_done, 1)
                    dve.wait_ge(mean_done, NT)
                    step = Chain(dve, step_s)
                    step(dve.tensor_scalar(var_e[:, 0:NT], mv[:, 0:NT, 1], LN_EPS, None, ALU.add))
                    rsqrt(dve, step, var_e[:, 0:NT], rstd[:, 0:NT], newton[:, 0:NT])
                    for t in range(NT):
                        dve.tensor_scalar(x_tok[:, t, :], r_tok[:, t, :], mv[:, t, 0:1], rstd[:, t:t + 1],
                                          ALU.subtract, ALU.mult).then_inc(x_done, 1)

                if last:
                    @block.sync
                    def _(sp):
                        sp.wait_ge(x_done, NT)
                        sp.dma_start(out.rearrange("(g b) (c p) d -> p g (b c) d", p=P, b=B)[:, group_slice(group), :, :],
                                     x_tok[:, :, :].unsqueeze(1)).then_inc(stored, 16)
                        sp.wait_ge(stored, 16)
                    return

                @block.tensor
                def _(pe):
                    for t in range(NT):
                        pe.wait_ge(x_done, t + 1)
                        nc.tensor.transpose(bank[0][:, t * P:(t + 1) * P], x_tok[:, t, :], ident).then_inc(xt_done, 1)

                @block.scalar
                def _(act):
                    act.wait_ge(xt_done, NT)
                    act.activation(xT[:, :], bank[0][:, :], ACT.Copy)

        def group_slice(i):
            return bass.ds(i, 1) if not isinstance(i, int) else slice(i, i + 1)

        def keep_x(group):
            with nc.Block() as block:
                @block.vector
                def _(dve):
                    dve.tensor_copy(x_all[:, bass.ts(group, NT), :], x_tok[:, :, :])

        def load_late():
            with nc.Block() as block:
                @block.sync
                def _(sp):
                    for pk in late:
                        sp.dma_start(held[pk], packs[pk]).then_inc(loaded[pk], 16)
                    for pk in late:
                        sp.wait_ge(loaded[pk], 16)

        def take_x(tag, group):
            took, turned = bsem(f"{tag}_took"), bsem(f"{tag}_turned")
            with nc.Block() as block:
                @block.vector
                def _(dve):
                    dve.tensor_copy(x_tok[:, :, :], x_all[:, bass.ts(group, NT), :]).then_inc(took, 1)

                @block.tensor
                def _(pe):
                    pe.wait_ge(took, 1)
                    for t in range(NT):
                        last = nc.tensor.transpose(bank[0][:, t * P:(t + 1) * P], x_tok[:, t, :], ident)
                    last.then_inc(turned, 1)

                @block.scalar
                def _(act):
                    act.wait_ge(turned, 1)
                    act.activation(xT[:, :], bank[0][:, :], ACT.Copy)

        def project(tag, items, needs):
            made, act_out, dve_out = bsem(f"{tag}_made"), bsem(f"{tag}_act_out"), bsem(f"{tag}_dve_out")
            with nc.Block() as block:
                @block.tensor
                def _(pe):
                    for pk, cnt in needs:
                        pe.wait_ge(loaded[pk], cnt)
                    for i, (l, r, d, s) in enumerate(items):
                        if i >= 8:
                            pe.wait_ge(act_out if i % 2 == 0 else dve_out, (i - 8) // 2 + 1)
                        nc.tensor.matmul(bank[i % 8][:, :], l, r, start=True, stop=True).then_inc(made, 1)

                @block.scalar
                def _(act):
                    for i, (l, r, d, s) in enumerate(items):
                        if i % 2 == 0:
                            act.wait_ge(made, i + 1)
                            act.activation(d, bank[i % 8][:, :], ACT.Copy, scale=s).then_inc(act_out, 1)

                @block.vector
                def _(dve):
                    for i, (l, r, d, s) in enumerate(items):
                        if i % 2 == 1:
                            dve.wait_ge(made, i + 1)
                            dve.tensor_scalar(d, bank[i % 8][:, :], s, None, ALU.mult).then_inc(dve_out, 1)

        def heads(tag, k_chunk, v_col, causal, whole=False):
            n_it = B * NH
            scores_done, max_done, exp_done = bsem(f"{tag}_scores"), bsem(f"{tag}_max"), bsem(f"{tag}_exp")
            trans_done, act_copy, dve_copy = bsem(f"{tag}_trans"), bsem(f"{tag}_act_copy"), bsem(f"{tag}_dve_copy")
            pv_done, norm_done, dve_step = bsem(f"{tag}_pv"), bsem(f"{tag}_norm"), bsem(f"{tag}_dve")
            keys = [P, S] if causal else [S, S]
            blocks = [(kc, qc) for kc in range(SC) for qc in range(SC) if kc * P < keys[qc]]

            def bh(i):
                return i // NH, i % NH

            def by_act(i):
                return i % 2 == 1

            with nc.Block() as block:
                @block.tensor
                def _(pe):
                    def scores(i):
                        b, h = bh(i)
                        if i >= 3:
                            pe.wait_ge(exp_done, 2 * (i - 2))
                        r0, rn_ = (0, P) if whole else (HD * (h % 2), HD)
                        for qc in range(SC):
                            q = bigA[r0:r0 + rn_, h // 2, b * S + qc * P:b * S + qc * P + P]
                            k = bigB[r0:r0 + rn_, k_chunk(h), b * S:b * S + keys[qc]]
                            last = nc.tensor.matmul(bank[i % 3][:, qc * S:qc * S + keys[qc]], q, k, start=True, stop=True)
                        last.then_inc(scores_done, 1)

                    def transposes(i):
                        pe.wait_ge(exp_done, 2 * i + 2)
                        if i >= 3:
                            j = i - 3
                            pe.wait_ge(act_copy if by_act(j) else dve_copy, j // 2 + 1)
                        for m, (kc, qc) in enumerate(blocks):
                            last = nc.tensor.transpose(bank[3 + i % 3][:, m * P:(m + 1) * P],
                                                       prob[:, i % 4, qc, kc * P:(kc + 1) * P], ident)
                        last.then_inc(trans_done, 1)

                    def values(i):
                        b, h = bh(i)
                        pe.wait_ge(act_copy if by_act(i) else dve_copy, i // 2 + 1)
                        g = i // 4
                        if i % 4 == 0 and g >= 2:
                            pe.wait_ge(norm_done, g - 1)
                        for qc in range(SC):
                            mine = [(m, kc) for m, (kc, q2) in enumerate(blocks) if q2 == qc]
                            for n_, (m, kc) in enumerate(mine):
                                last = nc.tensor.matmul(bank[6 + g % 2][:, qc * S + (h % 4) * HD:qc * S + (h % 4) * HD + HD],
                                                        probT[:, i % 3, m, :], bigC[:, b * SC + kc, v_col(h):v_col(h) + HD],
                                                        start=n_ == 0, stop=n_ == len(mine) - 1)
                        last.then_inc(pv_done, 1)

                    for i in range(n_it + 3):
                        if i < n_it:
                            scores(i)
                        if 0 <= i - 2 < n_it:
                            transposes(i - 2)
                        if 0 <= i - 3 < n_it:
                            values(i - 3)

                @block.vector
                def _(dve):
                    def copy_out(i):
                        dve.wait_ge(trans_done, i + 1)
                        if i >= 3:
                            dve.wait_ge(pv_done, i - 2)
                        m = len(blocks)
                        dve.tensor_copy(probT[:, i % 3, 0:m, :], bank[3 + i % 3][:, 0:m * P].rearrange("p (m c) -> p m c", m=m))\
                           .then_inc(dve_copy, 1)

                    def row_max(i):
                        b, h = bh(i)
                        dve.wait_ge(scores_done, i + 1)
                        if causal:
                            if i >= 4:
                                dve.wait_ge(trans_done, i - 3)
                            for qc in range(SC):
                                dve.tensor_tensor(raw[:, i % 4, qc, 0:keys[qc]], bank[i % 3][:, qc * S:qc * S + keys[qc]],
                                                  bias_t[:, h, S - keys[qc]:S], ALU.add).then_inc(dve_step, 1)
                            for qc in range(SC):
                                dve.wait_ge(dve_step, 2 * i + qc + 1)
                                dve.tensor_reduce(nmax[:, i, qc:qc + 1], raw[:, i % 4, qc, 0:keys[qc]], op=ALU.max,
                                                  axis=AX, negate=True).then_inc(max_done, 1)
                        else:
                            dve.tensor_reduce(nmax[:, i, :], bank[i % 3][:, :].rearrange("p (c t) -> p c t", c=SC), op=ALU.max,
                                              axis=AX, negate=True).then_inc(max_done, 2)

                    def normalise(g):
                        b, h = bh(4 * g)
                        dve.wait_ge(exp_done, 8 * g + 8)
                        dve.reciprocal(rsum[:, g, :, :], sums[:, g, :, :]).then_inc(norm_step, 1)
                        dve.wait_ge(norm_step, g + 1)
                        dve.wait_ge(pv_done, 4 * g + 4)
                        dve.tensor_tensor(bigD[:, b * SC:(b + 1) * SC, h * HD:(h + 4) * HD].rearrange("p c (h d) -> p c h d", d=HD),
                                          bank[6 + g % 2][:, :].rearrange("p (c h d) -> p c h d", c=SC, h=4),
                                          rsum[:, g, :, :].unsqueeze(3).broadcast_to([P, SC, 4, HD]), ALU.mult).then_inc(norm_done, 1)

                    norm_step = bsem(f"{tag}_rsum")
                    for i in range(n_it + 5):
                        if i < n_it:
                            row_max(i)
                        if 0 <= i - 2 < n_it and not by_act(i - 2):
                            copy_out(i - 2)
                        if 0 <= i - 4 < n_it and (i - 4) % 4 == 3:
                            normalise((i - 4) // 4)

                @block.scalar
                def _(act):
                    for i in range(n_it + 2):
                        if i < n_it:
                            act.wait_ge(max_done, 2 * i + 2)
                            if i >= 4:
                                act.wait_ge(trans_done, i - 3)
                            for qc in range(SC):
                                src = raw[:, i % 4, qc, 0:keys[qc]] if causal else bank[i % 3][:, qc * S:qc * S + keys[qc]]
                                act.activation(prob[:, i % 4, qc, 0:keys[qc]], src, ACT.Exp, bias=nmax[:, i, qc:qc + 1],
                                               accum_out=sums[:, i // 4, qc, i % 4:i % 4 + 1]).then_inc(exp_done, 1)
                        j = i - 2
                        if 0 <= j < n_it and by_act(j):
                            act.wait_ge(trans_done, j + 1)
                            if j >= 3:
                                act.wait_ge(pv_done, j - 2)
                            m = len(blocks)
                            act.activation(probT[:, j % 3, 0:m, :], bank[3 + j % 3][:, 0:m * P].rearrange("p (m c) -> p m c", m=m),
                                           ACT.Copy).then_inc(act_copy, 1)

        def out_proj(tag, wo, bias=None):
            turned, act_out, dve_out, made, biased = (bsem(f"{tag}_turned"), bsem(f"{tag}_act_out"), bsem(f"{tag}_dve_out"),
                                                      bsem(f"{tag}_made"), bsem(f"{tag}_biased"))
            wo3 = v3(wo, NCH)
            with nc.Block() as block:
                @block.tensor
                def _(pe):
                    for c in range(NCH):
                        if c >= 4:
                            pe.wait_ge(act_out if c % 2 == 0 else dve_out, (c - 4) // 2 + 1)
                        for t in range(NT):
                            last = nc.tensor.transpose(bank[c % 4][:, t * P:(t + 1) * P], bigD[:, t, c * P:(c + 1) * P], ident)
                        last.then_inc(turned, 1)
                    pe.wait_ge(act_out, NCH // 2)
                    pe.wait_ge(dve_out, NCH // 2)
                    for t in range(NT):
                        for c in range(NCH):
                            last = nc.tensor.matmul(bank[4][:, t * P:(t + 1) * P], bigA[:, c, t * P:(t + 1) * P], wo3[:, c, :],
                                                    start=c == 0, stop=c == NCH - 1)
                    last.then_inc(made, 1)

                @block.scalar
                def _(act):
                    for c in range(0, NCH, 2):
                        act.wait_ge(turned, c + 1)
                        act.activation(bigA[:, c, :], bank[c % 4][:, :], ACT.Copy).then_inc(act_out, 1)

                @block.vector
                def _(dve):
                    for c in range(1, NCH, 2):
                        dve.wait_ge(turned, c + 1)
                        dve.tensor_copy(bigA[:, c, :], bank[c % 4][:, :]).then_inc(dve_out, 1)
                    base = x_tok
                    if bias is not None:
                        dve.tensor_tensor(bigB[:, 0, :].rearrange("p (t d) -> p t d", t=NT), x_tok[:, :, :],
                                          bias.unsqueeze(1).broadcast_to([P, NT, P]), ALU.add).then_inc(biased, 1)
                        dve.wait_ge(biased, 1)
                        base = bigB[:, 0, :].rearrange("p (t d) -> p t d", t=NT)
                    else:
                        base = x_tok[:, :, :]
                    dve.wait_ge(made, 1)
                    dve.tensor_tensor(r_tok[:, :, :], bank[4][:, :].rearrange("p (t d) -> p t d", t=NT), base, ALU.add)

        def l0_bias():
            summed, padded, copied, stored, skewed = (sem("l0b_summed"), sem("l0b_padded"), sem("l0b_copied"),
                                                      sem("l0b_stored"), sem("l0b_skewed"))
            flipped, mirrored = sem("l0b_flipped"), flat(bigC)
            rpe = v3(W("first", "rpe"), SC)
            tri = v3(W("const", "revtri"), SC)
            small = flat(bigA)
            ext = small[0:NH, 0:S + P]
            with nc.Block() as block:
                @block.tensor
                def _(pe):
                    pe.wait_ge(loaded["first"], 16)
                    pe.wait_ge(loaded["const"], 16)
                    for c in range(SC):
                        last = nc.tensor.matmul(bank[0][0:NH, 0:S], rpe[:, c, :], tri[:, c, :], start=c == 0, stop=c == SC - 1)
                    last.then_inc(summed, 1)
                    pe.wait_ge(skewed, 16)
                    pe.wait_ge(copied, 1)
                    for c in range(8):
                        nc.tensor.matmul(bank[c][:, :], W("const", "flip"), mirrored[:, c * 512:(c + 1) * 512], start=True, stop=True)\
                          .then_inc(flipped, 1)

                @block.vector
                def _(dve):
                    dve.memset(small[0:NH, S:S + P], PAD).then_inc(padded, 1)
                    dve.wait_ge(summed, 1)
                    dve.tensor_copy(small[0:NH, 0:S], bank[0][0:NH, 0:S]).then_inc(copied, 1)
                    for c in range(8):
                        dve.wait_ge(flipped, c + 1)
                        dve.tensor_copy(bias_t[:, :, :].rearrange("p h s -> p (h s)")[:, c * 512:(c + 1) * 512], bank[c][:, :])

                @block.sync
                def _(sp):
                    sp.wait_ge(padded, 1)
                    sp.wait_ge(copied, 1)
                    sp.dma_start(dram["rpe"][:, :], ext).then_inc(stored, 16)
                    sp.wait_ge(stored, 16)
                    src = bass.AP(tensor=dram["rpe"].tensor, offset=0, ap=[[1, P], [S + P, NH], [1, S]])
                    sp.dma_start(mirrored.rearrange("p (h s) -> p h s", h=NH), src).then_inc(skewed, 16)

        def expms():
            SQ = 6
            a_in, aT_in = W("gens", "a"), W("gens", "aT")
            nsl = 6 * P
            slot = [bigD[:, :, :].rearrange("p a b -> p (a b)")[:, k * nsl:(k + 1) * nsl].rearrange("p (s n) -> p s n", s=2)
                    for k in range(5)]
            A1, A2, A3, Q, E = slot
            A4 = flat(bigC)[:, 0:nsl].rearrange("p (s n) -> p s n", s=2)
            made = sem("exp_made")
            exp_half = sem("exp_half")
            used = sem("exp_used")
            pb = [bank[0], bank[1]]

            def view(s, m):
                return s[:, 0, m * P:(m + 1) * P], s[:, 1, m * P:(m + 1) * P]

            with nc.Block() as block:
                rounds = [("A2", A1, A1), ("A3", A2, A1), ("A4", A2, A2), ("P", None, None)] + [("sq", E, E)] * SQ

                @block.tensor
                def _(pe):
                    n = 0
                    pe.wait_ge(used, 1)
                    for kind, X, Y in rounds:
                        if kind == "P":
                            X, Y = A4, Q
                        for m in range(3):
                            x, xt = view(X, m)
                            y, yt = view(Y, m)
                            nc.tensor.matmul(pb[0][:, m * P:(m + 1) * P], xt, y, start=True, stop=True)
                            last = nc.tensor.matmul(pb[1][:, m * P:(m + 1) * P], x, yt, start=True, stop=True)
                        last.then_inc(made, 1)
                        n += 1
                        pe.wait_ge(used, n + 1)
                    nc.tensor.matmul(bank[2][:, 0:P], view(E, 1)[1], view(E, 2)[0], start=True, stop=True).then_inc(made, 1)
                    pe.wait_ge(used, n + 2)
                    nc.tensor.matmul(bank[3][:, 0:P], view(E, 0)[1], A1[:, 0, 0:P], start=True, stop=True).then_inc(made, 1)

                @block.vector
                def _(dve):
                    step = Chain(dve, sem("exp_dve"))
                    idb = ident.unsqueeze(1).broadcast_to([P, 3, P])
                    t3 = lambda ap: ap.rearrange("p (m n) -> p m n", m=3)

                    dve.wait_ge(loaded["gens"], 16)
                    dve.wait_ge(loaded["const"], 16)
                    dve.tensor_scalar(A1[:, 0, :], a_in, 1.0 / 2 ** SQ, None, ALU.mult).then_inc(exp_half, 1)
                    dve.wait_ge(exp_half, 1)
                    dve.tensor_scalar(A1[:, 1, :], aT_in, 1.0 / 2 ** SQ, None, ALU.mult).then_inc(used, 1)
                    f = [1.0]
                    for k in range(1, 9):
                        f.append(f[-1] * k)
                    for n, (kind, _, _) in enumerate(rounds):
                        dve.wait_ge(made, n + 1)
                        if kind in ("A2", "A3", "A4"):
                            D = {"A2": A2, "A3": A3, "A4": A4}[kind]
                            step(dve.tensor_copy(D[:, 0, :], pb[0][:, 0:3 * P]))
                            if kind != "A4":
                                ins = dve.tensor_copy(D[:, 1, :], pb[1][:, 0:3 * P])
                                ins.then_inc(used, 1)
                                dve.wait_ge(used, n + 2)
                                continue
                            step(dve.tensor_copy(D[:, 1, :], pb[1][:, 0:3 * P]))
                            for s in range(2):
                                step(dve.tensor_scalar(t3(Q[:, s, :]), idb, 1.0 / f[4], None, ALU.mult))
                                for X, c in ((A1, 5), (A2, 6), (A3, 7), (A4, 8)):
                                    step(dve.scalar_tensor_tensor(out=Q[:, s, :], in0=X[:, s, :], scalar=1.0 / f[c], in1=Q[:, s, :],
                                                                  op0=ALU.mult, op1=ALU.add))
                                step(dve.tensor_tensor(t3(E[:, s, :]), t3(A1[:, s, :]), idb, ALU.add))
                                for X, c in ((A2, 2), (A3, 3)):
                                    step(dve.scalar_tensor_tensor(out=E[:, s, :], in0=X[:, s, :], scalar=1.0 / f[c], in1=E[:, s, :],
                                                                  op0=ALU.mult, op1=ALU.add))
                            dve.sem_inc(used, 1)
                        elif kind == "P":
                            step(dve.tensor_tensor(E[:, 0, :], pb[0][:, 0:3 * P], E[:, 0, :], ALU.add))
                            dve.tensor_tensor(E[:, 1, :], pb[1][:, 0:3 * P], E[:, 1, :], ALU.add).then_inc(used, 1)
                            dve.wait_ge(used, n + 2)
                        else:
                            step(dve.tensor_copy(E[:, 0, :], pb[0][:, 0:3 * P]))
                            dve.tensor_copy(E[:, 1, :], pb[1][:, 0:3 * P]).then_inc(used, 1)
                            dve.wait_ge(used, n + 2)
                    n = len(rounds)
                    dve.wait_ge(made, n + 1)
                    dve.tensor_copy(A1[:, 0, 0:P], bank[2][:, 0:P]).then_inc(used, 1)
                    dve.wait_ge(made, n + 2)
                    dve.tensor_copy(rot[:, :], bank[3][:, 0:P])


        def zero_slots():
            cleared, zeroed, none_taken = sem("z_cleared"), sem("z_zeroed"), sem("z_none_taken")
            rows = dram["slots"].rearrange("(p n) d -> p n d", p=P)
            with nc.Block() as block:
                @block.vector
                def _(dve):
                    dve.memset(taken[:, :], 0.0).then_inc(none_taken, 1)
                    dve.memset(bigD[:, :, :], 0.0).then_inc(cleared, 1)

                @block.sync
                def _(sp):
                    sp.wait_ge(cleared, 1)
                    sp.dma_start(rows, flat(bigD).rearrange("p (n d) -> p n d", d=P)).then_inc(zeroed, 16)
                    sp.wait_ge(zeroed, 16)

        put, fetched = sem("slots_put"), sem("results_fetched")

        def route0(group):
            n = NT * NE
            (lg, mx, ex, sm, eq, rk, best, hot, use, loc, pos, base, over, g_, wr) = [tiny[:, k, :] for k in range(15)]
            t3 = lambda ap: v3(ap, NT)
            col = lambda ap: t3(ap)[:, :, 0]

            def spread(ap):
                return col(ap).unsqueeze(2).broadcast_to([P, NT, NE])
            logits, shifted, exped, picked, counted = (bsem("r0_logits"), bsem("r0_shifted"), bsem("r0_exped"),
                                                       bsem("r0_picked"), bsem("r0_counted"))
            placed, kept, step_s = bsem("r0_placed"), bsem("r0_kept"), bsem("r0_step")
            upto, ones = W("const", "upto"), W("const", "ones")
            with nc.Block() as block:
                @block.tensor
                def _(pe):
                    for t in range(NT):
                        last = nc.tensor.matmul(bank[0][:, t * NE:(t + 1) * NE], xT[:, t * P:(t + 1) * P], W("first", "wg"),
                                                start=True, stop=True)
                    last.then_inc(logits, 1)
                    pe.wait_ge(picked, 1)
                    for t in range(NT):
                        for u in range(t + 1):
                            nc.tensor.matmul(bank[1][:, t * NE:(t + 1) * NE], upto if u == t else ones,
                                             hot[:, u * NE:(u + 1) * NE], start=u == 0, stop=u == t)
                    for u in range(NT):
                        last = nc.tensor.matmul(bank[2][:, 0:NE], ones, hot[:, u * NE:(u + 1) * NE], start=u == 0, stop=u == NT - 1)
                    last.then_inc(counted, 1)

                @block.scalar
                def _(act):
                    act.wait_ge(shifted, 1)
                    act.activation(ex, lg, ACT.Exp).then_inc(exped, 1)

                @block.vector
                def _(dve):
                    step = Chain(dve, step_s)
                    dve.wait_ge(logits, 1)
                    step(dve.tensor_reduce(col(mx), t3(bank[0][:, 0:n]), op=ALU.max, axis=AX))
                    dve.tensor_tensor(t3(lg), t3(bank[0][:, 0:n]), spread(mx), ALU.subtract).then_inc(shifted, 1)
                    dve.wait_ge(exped, 1)
                    step(dve.tensor_reduce(col(sm), t3(ex), op=ALU.add, axis=AX))
                    step(dve.tensor_reduce(col(best), t3(ex), op=ALU.max, axis=AX))
                    step(dve.reciprocal(col(g_), col(sm)))
                    step(dve.tensor_tensor(gate0[:, bass.ts(group, NT)], col(g_), col(best), ALU.mult))
                    step(dve.tensor_tensor(t3(eq), t3(ex), spread(best), ALU.is_equal))
                    step(dve.tensor_tensor(t3(rk), t3(eq), W("const", "desc8").unsqueeze(1).broadcast_to([P, NT, NE]), ALU.mult))
                    step(dve.tensor_reduce(col(use), t3(rk), op=ALU.max, axis=AX))
                    dve.tensor_tensor(t3(hot), t3(rk), spread(use), ALU.is_equal).then_inc(picked, 1)
                    dve.wait_ge(counted, 1)
                    step(dve.tensor_tensor(t3(loc), t3(bank[1][:, 0:n]), taken[:, :].unsqueeze(1).broadcast_to([P, NT, NE]), ALU.add))
                    step(dve.tensor_tensor(taken[:, :], taken[:, :], bank[2][:, 0:NE], ALU.add))
                    step(dve.tensor_tensor(loc, loc, hot, ALU.mult))
                    step(dve.tensor_reduce(col(pos), t3(loc), op=ALU.add, axis=AX))
                    step(dve.tensor_tensor(t3(base), t3(hot), W("const", "slot0").unsqueeze(1).broadcast_to([P, NT, NE]), ALU.mult))
                    step(dve.tensor_reduce(col(use), t3(base), op=ALU.add, axis=AX))
                    step(dve.tensor_scalar(col(over), col(pos), float(CAP), None, ALU.is_gt))
                    step(dve.tensor_scalar(col(wr), col(pos), float(CAP), None, ALU.min))
                    step(dve.scalar_tensor_tensor(out=slot_f[:, :], in0=col(wr), scalar=-1.0, in1=col(use), op0=ALU.add, op1=ALU.add))
                    step(dve.tensor_copy(slot_r[:, bass.ts(group, NT)], slot_f[:, :]))
                    step(dve.scalar_tensor_tensor(out=col(wr), in0=col(over), scalar=float(ALL_T), in1=slot_f[:, :],
                                                  op0=ALU.mult, op1=ALU.add))
                    step(dve.tensor_scalar(col(over), col(over), -1.0, 1.0, ALU.mult, ALU.add))
                    dve.tensor_tensor(gate0[:, bass.ts(group, NT)], gate0[:, bass.ts(group, NT)], col(over), ALU.mult).then_inc(kept, 1)
                    dve.tensor_copy(slot_now[:, :], col(wr)).then_inc(placed, 1)
                    dve.tensor_copy(x_all[:, bass.ts(group, NT), :], x_tok[:, :, :])

                @block.gpsimd
                def _(pool):
                    pool.wait_ge(placed, 1)
                    for t in range(NT):
                        pool.indirect_dma_start(dram["slots"], bass.IndirectOffsetOnAxis(ap=slot_now[:, t:t + 1], axis=0),
                                                x_tok[:, t, :], None, bounds_check=ALL_T - 1, oob_is_err=False).then_inc(put, 16)
                    pool.wait_ge(put, 16 * NT * (group + 1))

        slot_now = sb("slot_now", [P, NT], U32)

        def experts0(e, par):
            tg = f"e{par}"
            cols = packs["l0f"].shape[1]
            wbuf = [flat(bigA), flat(bigB)][par][:, 0:cols]
            hb = [bigC, bigD][par]
            d_tok = hb[:, 0, 0:512].rearrange("p (t d) -> p t d", t=NT)
            dT = hb[:, 0, 512:1024]
            h = [hb[:, 1, 0:512], hb[:, 1, 512:1024], hb[:, 2, 0:512], hb[:, 2, 512:1024]]
            eo = hb[:, 3, 0:512].rearrange("p (t d) -> p t d", t=NT)
            w1 = wbuf[:, 0:512]
            w2 = v3(wbuf[:, 512:1024], 4)
            b1 = wbuf[:, 1024:1028]
            b2 = wbuf[:, 1028:1028 + P]
            bk = bank[4 * par:4 * par + 4]
            return dict(w=wbuf, d_tok=d_tok, dT=dT, h=h, eo=eo, w1=w1, w2=w2, b1=b1, b2=b2, bk=bk, e=e,
                        got=bsem(f"{tg}_got"), gotw=bsem(f"{tg}_gotw"), turned=bsem(f"{tg}_turned"), dT_done=bsem(f"{tg}_dT"),
                        up=bsem(f"{tg}_up"), relu=bsem(f"{tg}_relu"), down=bsem(f"{tg}_down"), eo_done=bsem(f"{tg}_eo"),
                        stored=bsem(f"{tg}_stored"))

        def expert_pair(first):
            two = [experts0(first, 0), experts0(first + 1, 1)]
            pack_e = packs["l0f"].rearrange("(e p) n -> p e n", p=P)
            slots_e = dram["slots"].rearrange("(e t p) d -> p e t d", p=P, t=CAP // P)
            res_e = dram["results"].rearrange("(e t p) d -> p e t d", p=P, t=CAP // P)
            with nc.Block() as block:
                @block.sync
                def _(sp):
                    for q in two:
                        sp.dma_start(q["w"].unsqueeze(1), pack_e[:, group_slice(q["e"]), :]).then_inc(q["gotw"], 16)
                        sp.dma_start(q["d_tok"].unsqueeze(1), slots_e[:, group_slice(q["e"]), :, :]).then_inc(q["got"], 16)
                    for q in two:
                        sp.wait_ge(q["eo_done"], 1)
                        sp.dma_start(res_e[:, group_slice(q["e"]), :, :], q["eo"].unsqueeze(1)).then_inc(q["stored"], 16)
                    for q in two:
                        sp.wait_ge(q["stored"], 16)

                @block.tensor
                def _(pe):
                    for q in two:
                        pe.wait_ge(q["got"], 16)
                        for t in range(NT):
                            last = nc.tensor.transpose(q["bk"][0][:, t * P:(t + 1) * P], q["d_tok"][:, t, :], ident)
                        last.then_inc(q["turned"], 1)
                    for q in two:
                        pe.wait_ge(q["gotw"], 16)
                        pe.wait_ge(q["dT_done"], 1)
                        for c in range(4):
                            nc.tensor.matmul(q["bk"][c][:, :], q["w1"][:, c * P:(c + 1) * P], q["dT"], start=True, stop=True)\
                              .then_inc(q["up"], 1)
                    for q in two:
                        pe.wait_ge(q["relu"], 4)
                        for t in range(NT):
                            for c in range(4):
                                last = nc.tensor.matmul(q["bk"][0][:, t * P:(t + 1) * P], q["h"][c][:, t * P:(t + 1) * P],
                                                        q["w2"][:, c, :], start=c == 0, stop=c == 3)
                        last.then_inc(q["down"], 1)

                @block.scalar
                def _(act):
                    for q in two:
                        for c in range(4):
                            act.wait_ge(q["up"], c + 1)
                            act.activation(q["h"][c], q["bk"][c][:, :], ACT.Relu, bias=q["b1"][:, c:c + 1]).then_inc(q["relu"], 1)

                @block.vector
                def _(dve):
                    for q in two:
                        dve.wait_ge(q["turned"], 1)
                        dve.tensor_copy(q["dT"], q["bk"][0][:, :]).then_inc(q["dT_done"], 1)
                    for q in two:
                        dve.wait_ge(q["down"], 1)
                        dve.tensor_tensor(q["eo"], v3(q["bk"][0][:, :], NT), q["b2"].unsqueeze(1).broadcast_to([P, NT, P]),
                                          ALU.add).then_inc(q["eo_done"], 1)

        def combine0(group):
            scaled, ready = bsem("c0_scaled"), bsem("c0_ready")
            res = bigD[:, 0, 0:512].rearrange("p (t d) -> p t d", t=NT)
            with nc.Block() as block:
                @block.vector
                def _(dve):
                    dve.tensor_copy(slot_now[:, :], slot_r[:, bass.ts(group, NT)]).then_inc(ready, 1)
                    dve.wait_ge(fetched, 16 * NT * (group + 1))
                    dve.tensor_tensor(res, res, gate0[:, bass.ts(group, NT)].unsqueeze(2).broadcast_to([P, NT, P]), ALU.mult)\
                       .then_inc(scaled, 1)
                    dve.wait_ge(scaled, 1)
                    dve.tensor_tensor(r_tok[:, :, :], res, x_all[:, bass.ts(group, NT), :], ALU.add)

                @block.gpsimd
                def _(pool):
                    pool.wait_ge(ready, 1)
                    for t in range(NT):
                        pool.indirect_dma_start(res[:, t, :], None, dram["results"],
                                                bass.IndirectOffsetOnAxis(ap=slot_now[:, t:t + 1], axis=0),
                                                bounds_check=ALL_T - 1, oob_is_err=False).then_inc(fetched, 16)

        def l0_attention():
            q3, k3, wv = W("l0a", "wq"), W("l0a", "wk"), W("l0a", "wv")
            items = []
            for c in range(NCH):
                items.append((q3[:, c * P:(c + 1) * P], xT[:, :], bigA[:, c, :], HD ** -0.5))
                items.append((k3[:, c * P:(c + 1) * P], xT[:, :], bigB[:, c, :], 1.0))
            for t in range(NT):
                for h in range(2):
                    items.append((xT[:, t * P:(t + 1) * P], wv[:, h * 512:(h + 1) * 512], bigC[:, t, h * 512:(h + 1) * 512], 1.0))
            project("l0p", items, [])
            heads("l0h", lambda h: h // 2, lambda h: h * HD, True)
            out_proj("l0o", W("l0a", "wo"))

        def fold_lora():
            lw = where["lora"]
            n1 = lw["kA"][0]
            a0, b0 = flat(bigC)[0:8, :], flat(bigD)[0:8, :]
            got, made, added = sem("lora_got"), sem("lora_made"), sem("lora_added")

            def F(part):
                a, b = lw[part]
                return a0[:, a:b] if b <= n1 else b0[:, a - n1:b - n1]
            jobs = []
            for nm, cols in (("q", NH * HD), ("k", 512)):
                for tg in ("", "s"):
                    for c in range(0, cols, 512):
                        jobs.append([(F(f"{nm}A"), F(f"{nm}B{tg}")[:, c:c + 512], 0, 512, W("l1a", f"w{nm}{tg}")[:, c:c + 512])])
            jobs.append([(F("vA"), F("vB"), 0, 256, W("l1a", "wv"))])
            for half_ in range(2):
                jobs.append([(F("oA")[:, (4 * half_ + c) * P:(4 * half_ + c + 1) * P], F("oB"), c * P, P,
                              W("l1a", "wo")[:, (4 * half_) * P:(4 * half_ + 4) * P]) for c in range(4)])
            with nc.Block() as block:
                @block.sync
                def _(sp):
                    sp.dma_start(a0[:, 0:n1], packs["lora"][:, 0:n1]).then_inc(got, 16)
                    sp.dma_start(b0[:, 0:lora_cols - n1], packs["lora"][:, n1:lora_cols]).then_inc(got, 16)
                    sp.dma_start(held["l3a"], packs["l3a"]).then_inc(loaded["l3a"], 16)

                @block.tensor
                def _(pe):
                    pe.wait_ge(got, 32)
                    for i, job in enumerate(jobs):
                        if i >= 8:
                            pe.wait_ge(added, i - 7)
                        for (l, r, at, nn, d) in job:
                            last = nc.tensor.matmul(bank[i % 8][:, at:at + nn], l, r, start=True, stop=True)
                        last.then_inc(made, 1)

                @block.vector
                def _(dve):
                    dve.wait_ge(loaded["l1a"], 16)
                    for i, job in enumerate(jobs):
                        dve.wait_ge(made, i + 1)
                        d = job[0][4]
                        nn = d.shape[1]
                        dve.scalar_tensor_tensor(out=d, in0=bank[i % 8][:, 0:nn], scalar=2.0, in1=d, op0=ALU.mult, op1=ALU.add)\
                           .then_inc(added, 1)
                    for pk in ("l1f", "l3a", "eb2", "be2"):
                        dve.wait_ge(loaded[pk], 16)

        def l1_project():
            jobs = [("q", c) for c in range(NCH)] + [("k", c) for c in range(4)]
            made, mixed, out_done = bsem("l1p_made"), bsem("l1p_mixed"), bsem("l1p_out")
            v_made, half_done = bsem("l1p_v"), bsem("l1p_half")
            cos, sin = W("const", "rope_cos"), W("const", "rope_sin")
            t1 = [bigD[:, 0, 0:512], bigD[:, 1, 0:512]]
            t2 = [bigD[:, 0, 512:1024], bigD[:, 1, 512:1024]]
            with nc.Block() as block:
                @block.tensor
                def _(pe):
                    for i, (nm, c) in enumerate(jobs):
                        if i >= 3:
                            pe.wait_ge(mixed, 2 * (i - 2))
                        for s_, tg in enumerate(("", "s")):
                            last = nc.tensor.matmul(bank[2 * (i % 3) + s_][:, :], W("l1a", f"w{nm}{tg}")[:, c * P:(c + 1) * P], xT[:, :],
                                                    start=True, stop=True)
                        last.then_inc(made, 1)
                    for t in range(NT):
                        last = nc.tensor.matmul(bank[6 + t // 2][:, (t % 2) * 256:(t % 2) * 256 + 256], xT[:, t * P:(t + 1) * P],
                                                W("l1a", "wv"), start=True, stop=True)
                    last.then_inc(v_made, 1)

                @block.vector
                def _(dve):
                    keys2 = bigB[:, :, :].rearrange("p (c two) t -> p c two t", two=2)
                    dve.memset(keys2[HD:P, :, 0, :], 0.0)
                    dve.memset(keys2[0:HD, :, 1, :], 0.0)
                    for i, (nm, c) in enumerate(jobs):
                        s_ = HD ** -0.5 if nm == "q" else 1.0
                        dve.wait_ge(made, i + 1)
                        if i >= 2:
                            dve.wait_ge(out_done, i - 1)
                        b0, b1 = bank[2 * (i % 3)], bank[2 * (i % 3) + 1]
                        dve.scalar_tensor_tensor(out=t1[i % 2], in0=b0[:, :], scalar=s_, in1=cos, op0=ALU.mult, op1=ALU.mult)\
                           .then_inc(mixed, 1)
                        dve.scalar_tensor_tensor(out=t2[i % 2], in0=b1[:, :], scalar=s_, in1=sin, op0=ALU.mult, op1=ALU.mult)\
                           .then_inc(mixed, 1)

                @block.gpsimd
                def _(pool):
                    step = Chain(pool, half_done)
                    for i, (nm, c) in enumerate(jobs):
                        pool.wait_ge(mixed, 2 * i + 2)
                        if nm == "q":
                            pool.tensor_tensor(bigA[:, c, :], t1[i % 2], t2[i % 2], ALU.add).then_inc(out_done, 1)
                            pool.wait_ge(out_done, i + 1)
                        else:
                            step(pool.tensor_tensor(bigB[0:HD, 2 * c, :], t1[i % 2][0:HD, :], t2[i % 2][0:HD, :], ALU.add))
                            pool.tensor_tensor(bigB[HD:P, 2 * c + 1, :], t1[i % 2][HD:P, :], t2[i % 2][HD:P, :], ALU.add)\
                                .then_inc(out_done, 1)
                            pool.wait_ge(out_done, i + 1)

                @block.scalar
                def _(act):
                    act.wait_ge(v_made, 1)
                    for k in range(2):
                        act.activation(bigC[:, 2 * k:2 * k + 2, 0:256], v3(bank[6 + k][:, :], 2), ACT.Copy)

        def pre_norm(tag, gamma, beta, centred):
            st, mean, var, rs, xn, tr, half_done = (bsem(f"{tag}_st"), bsem(f"{tag}_mean"), bsem(f"{tag}_var"), bsem(f"{tag}_rs"),
                                                    bsem(f"{tag}_xn"), bsem(f"{tag}_tr"), bsem(f"{tag}_half"))
            y = bigB[:, 1, :].rearrange("p (t d) -> p t d", t=NT)
            with nc.Block() as block:
                @block.vector
                def _(dve):
                    step = Chain(dve, rs)
                    if centred:
                        for t in range(NT):
                            dve.bn_stats(stats[:, t, :], x_tok[:, t, :]).then_inc(st, 1)
                        for t in range(NT):
                            dve.wait_ge(st, t + 1)
                            dve.bn_aggr(mv[:, t, :], stats[:, t, :]).then_inc(mean, 1)
                        dve.wait_ge(mean, NT)
                        step(dve.tensor_scalar(var_e[:, 0:NT], mv[:, 0:NT, 1], LN_EPS, None, ALU.add))
                    else:
                        dve.tensor_tensor(y, x_tok[:, :, :], x_tok[:, :, :], ALU.mult).then_inc(st, 1)
                        dve.wait_ge(st, 1)
                        dve.tensor_reduce(var_e[:, 0:NT], y, op=ALU.add, axis=AX).then_inc(mean, 1)
                        dve.wait_ge(mean, 1)
                        dve.tensor_scalar(var_e[:, 0:NT], var_e[:, 0:NT], 1.0 / P, RMS_EPS, ALU.mult, ALU.add).then_inc(var, 1)
                        dve.wait_ge(var, 1)
                    rsqrt(dve, step, var_e[:, 0:NT], rstd[:, 0:NT], newton[:, 0:NT])
                    for t in range(NT):
                        if centred:
                            dve.tensor_scalar(y[:, t, :], x_tok[:, t, :], mv[:, t, 0:1], rstd[:, t:t + 1],
                                              ALU.subtract, ALU.mult).then_inc(xn, 1)
                        else:
                            dve.tensor_scalar(y[:, t, :], x_tok[:, t, :], rstd[:, t:t + 1], None, ALU.mult).then_inc(xn, 1)
                    dve.wait_ge(tr, NT)
                    if beta is None:
                        dve.tensor_scalar(bigB[:, 0, :], bank[0][:, :], gamma, None, ALU.mult)
                    else:
                        dve.tensor_scalar(bigB[:, 0, :], bank[0][:, :], gamma, beta, ALU.mult, ALU.add)

                @block.tensor
                def _(pe):
                    for t in range(NT):
                        pe.wait_ge(xn, t + 1)
                        nc.tensor.transpose(bank[0][:, t * P:(t + 1) * P], y[:, t, :], ident).then_inc(tr, 1)

        def top2(dve, step, lg, n_exp):
            mxs, ixf, h1, h2 = [v3(tiny[:, k, :], NT) for k in (20, 21, 22, 23)]
            for t in range(NT):
                step(dve.max(mxs[:, t, :], lg[:, t, :]))
                step(dve.max_index(ix8[:, t, :], mxs[:, t, :], lg[:, t, :]))
            step(dve.tensor_copy(ixf, ix8[:, :, :]))
            iota = W("const", "iota8").unsqueeze(1).broadcast_to([P, NT, 8])
            for k, h in ((0, h1), (1, h2)):
                step(dve.tensor_tensor(h, iota, ixf[:, :, k].unsqueeze(2).broadcast_to([P, NT, 8]), ALU.is_equal))
            return mxs, h1, h2

        def token_value(k):
            return tiny[:, k, 0:NT]

        def over8(ap):
            return ap.unsqueeze(2).broadcast_to([P, NT, 8])

        def softmax_of_two(dve, act_sems, step, mxs, h1, h2, wd, e_t, r_t, d_t):
            shifted, exped = act_sems
            dve.tensor_tensor(d_t, mxs[:, :, 1], mxs[:, :, 0], ALU.subtract).then_inc(shifted, 1)
            dve.wait_ge(exped, 1)
            step(dve.tensor_scalar(r_t, e_t, 1.0, None, ALU.add))
            step(dve.reciprocal(r_t, r_t))
            step(dve.tensor_tensor(e_t, e_t, r_t, ALU.mult))
            step(dve.tensor_tensor(h1, h1, over8(r_t), ALU.mult))
            step(dve.tensor_tensor(h2, h2, over8(e_t), ALU.mult))
            step(dve.tensor_tensor(wd, h1, h2, ALU.add))

        weights_of = v3(tiny[:, 19, :], NT)
        weightsT = sb("weightsT", [8, T])
        acc = sb("acc", [P, NT, P])
        other = sb("other", [P, NT, P])

        def l1_route():
            xnT = bigB[:, 0, :]
            made, shifted, exped, weighed, wt, abel_made, step_s = (bsem("l1r_made"), bsem("l1r_shifted"), bsem("l1r_exped"),
                                                                    bsem("l1r_weighed"), bsem("l1r_wt"), bsem("l1r_abel"), bsem("l1r_step"))
            biased = bsem("l1r_biased")
            lg = v3(tiny[:, 0, :], NT)
            e_t, r_t, d_t = token_value(1), token_value(2), token_value(3)
            with nc.Block() as block:
                @block.tensor
                def _(pe):
                    for t in range(NT):
                        last = nc.tensor.matmul(bank[0][:, t * NE:(t + 1) * NE], xnT[:, t * P:(t + 1) * P], W("l1f", "gate_w"),
                                                start=True, stop=True)
                    last.then_inc(made, 1)
                    for t in range(NT):
                        last = nc.tensor.matmul(bank[1][:, t * P:(t + 1) * P], xnT[:, t * P:(t + 1) * P], W("l1f", "abel_w"),
                                                start=True, stop=True)
                    last.then_inc(abel_made, 1)
                    pe.wait_ge(weighed, 1)
                    for t in range(NT):
                        last = nc.tensor.transpose(bank[2][0:8, t * P:(t + 1) * P], weights_of[:, t, :], ident)
                    last.then_inc(wt, 1)

                @block.scalar
                def _(act):
                    act.wait_ge(shifted, 1)
                    act.activation(e_t, d_t, ACT.Exp).then_inc(exped, 1)
                    act.wait_ge(biased, 1)
                    act.activation(other[:, :, :], r_tok[:, :, :], ACT.Gelu)
                    act.wait_ge(wt, 1)
                    act.activation(weightsT[:, :], bank[2][0:8, :], ACT.Copy)

                @block.vector
                def _(dve):
                    step = Chain(dve, step_s)
                    dve.wait_ge(made, 1)
                    step(dve.tensor_tensor(lg, v3(bank[0][:, 0:NT * NE], NT), W("l1f", "gate_b").unsqueeze(1).broadcast_to([P, NT, NE]), ALU.add))
                    mxs, h1, h2 = top2(dve, step, lg, NE)
                    softmax_of_two(dve, (shifted, exped), step, mxs, h1, h2, weights_of, e_t, r_t, d_t)
                    dve.sem_inc(weighed, 1)
                    dve.wait_ge(abel_made, 1)
                    dve.tensor_tensor(r_tok[:, :, :], v3(bank[1][:, :], NT), W("l1f", "abel_b").unsqueeze(1).broadcast_to([P, NT, P]), ALU.add)\
                       .then_inc(biased, 1)

        def l1_experts():
            xnT = bigB[:, 0, :]
            up, act_done, down, added, step_s, b_made = (bsem("l1e_up"), bsem("l1e_act"), bsem("l1e_down"), bsem("l1e_added"),
                                                         bsem("l1e_step"), bsem("l1e_bias"))
            ew1 = W("l1f", "ew1")
            ew2 = W("l1f", "ew2").rearrange("p (e c d) -> p e c d", e=NE, c=2)
            hb = [bigA[:, k, :] for k in range(4)]
            with nc.Block() as block:
                @block.tensor
                def _(pe):
                    for t in range(NT):
                        last = nc.tensor.matmul(bank[6][:, t * P:(t + 1) * P], weightsT[:, t * P:(t + 1) * P], held["eb2"],
                                                start=True, stop=True)
                    last.then_inc(b_made, 1)
                    for e in range(NE + 1):
                        if e < NE:
                            for c in range(2):
                                n = 2 * e + c
                                if n >= 4:
                                    pe.wait_ge(act_done, n - 3)
                                nc.tensor.matmul(bank[n % 4][:, :], ew1[:, n * P:(n + 1) * P], xnT, start=True, stop=True).then_inc(up, 1)
                        if e >= 1:
                            f = e - 1
                            pe.wait_ge(act_done, 2 * f + 2)
                            if f >= 2:
                                pe.wait_ge(added, f - 1)
                            for t in range(NT):
                                for c in range(2):
                                    last = nc.tensor.matmul(bank[4 + f % 2][:, t * P:(t + 1) * P], hb[(2 * f + c) % 4][:, t * P:(t + 1) * P],
                                                            ew2[:, f, c, :], start=c == 0, stop=c == 1)
                            last.then_inc(down, 1)

                @block.scalar
                def _(act):
                    for n in range(2 * NE):
                        act.wait_ge(up, n + 1)
                        if n >= 4:
                            act.wait_ge(down, (n - 4) // 2 + 1)
                        act.activation(hb[n % 4], bank[n % 4][:, :], ACT.Gelu, bias=W("l1f", "eb1")[:, n:n + 1]).then_inc(act_done, 1)

                @block.vector
                def _(dve):
                    step = Chain(dve, step_s)
                    dve.wait_ge(b_made, 1)
                    step(dve.tensor_copy(acc[:, :, :], v3(bank[6][:, :], NT)))
                    for e in range(NE):
                        dve.wait_ge(down, e + 1)
                        for t in range(NT):
                            last = dve.scalar_tensor_tensor(out=acc[:, t, :], in0=bank[4 + e % 2][:, t * P:(t + 1) * P],
                                                            scalar=weights_of[:, t, e:e + 1], in1=acc[:, t, :], op0=ALU.mult, op1=ALU.add)
                            last.then_inc(step_s, 1)
                        dve.wait_ge(step_s, 1 + NT * (e + 1))
                        dve.sem_inc(added, 1)

        def l1_mix():
            turned, copied, made, summed, exped, step_s = (bsem("l1m_turned"), bsem("l1m_copied"), bsem("l1m_made"),
                                                           bsem("l1m_summed"), bsem("l1m_exped"), bsem("l1m_step"))
            accT = bigA[:, 0, :]
            p1 = bigA[:, 1, :].rearrange("p (t d) -> p t d", t=NT)
            p2 = bigA[:, 2, :].rearrange("p (t d) -> p t d", t=NT)
            z1, z2, g_ = token_value(1), token_value(2), token_value(3)
            gc = W("l1f", "gc_w")
            moe = v3(bank[1][:, :], NT)
            with nc.Block() as block:
                @block.tensor
                def _(pe):
                    for t in range(NT):
                        last = nc.tensor.transpose(bank[0][:, t * P:(t + 1) * P], acc[:, t, :], ident)
                    last.then_inc(turned, 1)
                    pe.wait_ge(copied, 1)
                    for t in range(NT):
                        last = nc.tensor.matmul(bank[1][:, t * P:(t + 1) * P], accT[:, t * P:(t + 1) * P], rot[:, :], start=True, stop=True)
                    last.then_inc(made, 1)

                @block.scalar
                def _(act):
                    act.wait_ge(turned, 1)
                    act.activation(accT, bank[0][:, :], ACT.Copy).then_inc(copied, 1)
                    act.wait_ge(summed, 1)
                    act.activation(g_, z1, ACT.Exp, scale=-1.0).then_inc(exped, 1)

                @block.vector
                def _(dve):
                    step = Chain(dve, step_s)
                    step(dve.tensor_tensor(p1, other[:, :, :], gc[:, 0:P].unsqueeze(1).broadcast_to([P, NT, P]), ALU.mult))
                    step(dve.tensor_reduce(z1, p1, op=ALU.add, axis=AX))
                    dve.wait_ge(made, 1)
                    step(dve.tensor_tensor(p2, moe, gc[:, P:2 * P].unsqueeze(1).broadcast_to([P, NT, P]), ALU.mult))
                    step(dve.tensor_reduce(z2, p2, op=ALU.add, axis=AX))
                    step(dve.scalar_tensor_tensor(out=z1, in0=z1, scalar=W("l1f", "gc_b"), in1=z2, op0=ALU.add, op1=ALU.add))
                    dve.sem_inc(summed, 1)
                    step(dve.scalar_tensor_tensor(out=r_tok[:, :, :], in0=x_tok[:, :, :], scalar=2.0, in1=other[:, :, :],
                                                  op0=ALU.mult, op1=ALU.add))
                    step(dve.tensor_tensor(p1, moe, other[:, :, :], ALU.subtract))
                    dve.wait_ge(exped, 1)
                    step(dve.tensor_scalar(g_, g_, 1.0, None, ALU.add))
                    step(dve.reciprocal(g_, g_))
                    for t in range(NT):
                        dve.scalar_tensor_tensor(out=r_tok[:, t, :], in0=p1[:, t, :], scalar=g_[:, t:t + 1], in1=r_tok[:, t, :],
                                                 op0=ALU.mult, op1=ALU.add)

        def narrow(tag, wq, wkv, wo, latent, window):
            KV, D8, G4 = 4, 8, 4
            xnT = bigB[:, 0, :]
            cosq, sinq = v3(W("const", f"{tag[0]}_cos"), NT), v3(W("const", f"{tag[0]}_sin"), NT)
            qr = bigB[:, 2, :].rearrange("p (t h d) -> p t h d", t=NT, h=16)
            sq = bigB[:, 3, :].rearrange("p (a d) -> p a d", d=8)
            ta, tb = bigB[:, 4, 0:256], bigB[:, 4, 256:512]
            kr = bigB[:, 5, 0:128].rearrange("p (t h d) -> p t h d", t=NT, h=KV)
            sk = bigB[:, 5, 128:256].rearrange("p (a d) -> p a d", d=8)
            latT = bigB[0:32, 6, :]
            aoT = bigB[:, 7, :]
            qpad = flat(bigA)[:, 0:2048].rearrange("p (t a g d) -> p t a g d", t=NT, a=G4, g=KV)
            kpad = flat(bigA)[:, 2048:2560].rearrange("p (t g d) -> p t g d", t=NT, g=KV)
            vx = flat(bigA)[:, 2560:2560 + NT * KV * 32].rearrange("p (t g d) -> p t g d", t=NT, g=KV)
            ao = bigB[:, 2, :].rearrange("p (t h d) -> p t h d", t=NT, h=16)
            qT = flat(bigC)[:, 0:2048].rearrange("p (t a q) -> p t a q", t=NT, a=G4)
            kz = flat(bigC)[:, 2048:4096].rearrange("p (g t k) -> p g t k", g=KV, t=NT)
            pr = [bigD[:, k, 0:512] for k in range(4)]
            few = flat(bigA)[:, 3072:4096]
            ss2, r2 = few[:, 0:80], few[:, 80:160]
            rq, rk_ = r2[:, 0:64], r2[:, 64:80]
            rec = few[:, 256:320].rearrange("p (t h) -> p t h", t=NT)
            pads, q_made, kv_made, lat_made, lat_done = [bsem(f"{tag}_{n}") for n in ("pads", "q", "kv", "lat", "latd")]
            padded, tq, tk = [bsem(f"{tag}_{n}") for n in ("padded", "tq", "tk")]
            step_s = bsem(f"{tag}_step")
            with nc.Block() as block:
                @block.gpsimd
                def _(pool):
                    pool.memset(flat(bigA)[:, 0:2560], 0.0).then_inc(pads, 1)
                    pool.memset(vx, 1.0).then_inc(pads, 1)

                @block.tensor
                def _(pe):
                    for t in range(NT):
                        last = nc.tensor.matmul(bank[0][:, t * P:(t + 1) * P], xnT[:, t * P:(t + 1) * P], wq, start=True, stop=True)
                    last.then_inc(q_made, 1)
                    if latent is not None:
                        nc.tensor.matmul(bank[1][0:32, :], latent, xnT, start=True, stop=True).then_inc(lat_made, 1)
                        pe.wait_ge(lat_done, 1)
                    for t in range(NT):
                        l = latT[:, t * P:(t + 1) * P] if latent is not None else xnT[:, t * P:(t + 1) * P]
                        last = nc.tensor.matmul(bank[2][:, t * 64:(t + 1) * 64], l, wkv, start=True, stop=True)
                    last.then_inc(kv_made, 1)
                    pe.wait_ge(padded, 1)
                    for t in range(NT):
                        for a in range(G4):
                            last = nc.tensor.transpose(bank[4 + t][:, a * P:(a + 1) * P], qpad[:, t, a, :, :].rearrange("p g d -> p (g d)"), ident)
                        last.then_inc(tq, 1)
                    for t in range(NT):
                        last = nc.tensor.transpose(bank[3][:, t * P:(t + 1) * P], kpad[:, t, :, :].rearrange("p g d -> p (g d)"), ident)
                    last.then_inc(tk, 1)

                @block.scalar
                def _(act):
                    if latent is not None:
                        act.wait_ge(lat_made, 1)
                        act.activation(latT, bank[1][0:32, :], ACT.Copy).then_inc(lat_done, 1)
                    for t in range(NT):
                        act.wait_ge(tq, t + 1)
                        act.activation(qT[:, t, :, :], v3(bank[4 + t][:, :], G4), ACT.Copy)
                    act.wait_ge(tk, 1)
                    for g in range(KV):
                        act.activation(kz[:, g, :, :], v3(bank[3][:, :], NT), ACT.Copy, scale=W("const", "rows32")[:, g:g + 1])

                @block.vector
                def _(dve):
                    step = Chain(dve, step_s)

                    def rotate(src, dst, nh):
                        e, o = [src.rearrange("p t (h i e) -> p t h i e", i=4, e=2)[:, :, :, :, k] for k in (0, 1)]
                        c = cosq.unsqueeze(2).broadcast_to([P, NT, nh, 4])
                        s_ = sinq.unsqueeze(2).broadcast_to([P, NT, nh, 4])
                        A = ta[:, 0:NT * nh * 4].rearrange("p (t h i) -> p t h i", t=NT, h=nh)
                        Bv = tb[:, 0:NT * nh * 4].rearrange("p (t h i) -> p t h i", t=NT, h=nh)
                        step(dve.tensor_tensor(A, e, c, ALU.mult))
                        step(dve.tensor_tensor(Bv, o, s_, ALU.mult))
                        step(dve.tensor_tensor(dst[:, :, :, 0:4], A, Bv, ALU.subtract))
                        step(dve.tensor_tensor(A, e, s_, ALU.mult))
                        step(dve.tensor_tensor(Bv, o, c, ALU.mult))
                        step(dve.tensor_tensor(dst[:, :, :, 4:8], A, Bv, ALU.add))
                    dve.wait_ge(q_made, 1)
                    rotate(v3(bank[0][:, :], NT), qr, 16)
                    qf = qr.rearrange("p t h d -> p (t h) d")
                    step(dve.tensor_tensor(sq, qf, qf, ALU.mult))
                    step(dve.tensor_reduce(ss2[:, 0:64], sq, op=ALU.add, axis=AX))
                    dve.wait_ge(kv_made, 1)
                    rotate(v3(bank[2][:, 0:256], NT)[:, :, 0:32], kr, KV)
                    kf = kr.rearrange("p t h d -> p (t h) d")
                    step(dve.tensor_tensor(sk, kf, kf, ALU.mult))
                    step(dve.tensor_reduce(ss2[:, 64:80], sk, op=ALU.add, axis=AX))
                    step(dve.tensor_scalar(ss2, ss2, 1.0 / D8, RMS_EPS, ALU.mult, ALU.add))
                    rsqrt(dve, step, ss2, r2, newton[:, 0:80])
                    dve.wait_ge(pads, 2)
                    r4 = rq.rearrange("p (t g a) -> p t g a", t=NT, g=KV)
                    for t in range(NT):
                        step(dve.tensor_tensor(qpad[:, t, :, :, 0:8].rearrange("p a g d -> p g a d"),
                                               qr[:, t, :, :].rearrange("p (g a) d -> p g a d", g=KV),
                                               r4[:, t, :, :].unsqueeze(3).broadcast_to([P, KV, G4, D8]), ALU.mult))
                    dve.tensor_tensor(kpad[:, :, :, 0:8], kr, rk_.rearrange("p (t g) -> p t g", t=NT).unsqueeze(3).broadcast_to([P, NT, KV, D8]),
                                      ALU.mult).then_inc(padded, 1)
                    dve.tensor_copy(vx[:, :, :, 0:8], v3(bank[2][:, 0:256], NT)[:, :, 32:64].rearrange("p t (g d) -> p t g d", d=8))

            jobs = [(b, qc, g) for b in range(B) for qc in range(SC) for g in range(KV)]
            units = [(b, qc, g, kc) for (b, qc, g) in jobs for kc in range(qc, -1, -1)]
            masked = [kc == qc or window for (b, qc, g, kc) in units]
            first_unit = [units.index((b, qc, g, qc)) for (b, qc, g) in jobs] + [len(units)]
            REACH = 32

            def queries(u):
                b, qc, g, kc = units[u]
                return P if kc == qc or not window else REACH

            def cut(ap, u):
                return ap.rearrange("p (a q) -> p a q", a=G4)[:, :, 0:queries(u)]
            sc_done, ex_done, mask_done, pv_done, o_done, o_turned, normed, turned, aot, y_made = [bsem(f"{tag}_{n}") for n in
                                ("sc", "ex", "mask", "pv", "o", "ot", "normed", "turned", "aot", "y")]
            recip_s = bsem(f"{tag}_recip")
            oT = [bigB[:, 3 + t, :] for t in range(NT)]
            with nc.Block() as block:
                @block.tensor
                def _(pe):
                    def scores(j):
                        for u in range(first_unit[j], first_unit[j + 1]):
                            b, qc, g, kc = units[u]
                            if u >= 4:
                                pe.wait_ge(ex_done, u - 3)
                            nc.tensor.matmul(cut(bank[u % 4][:, :], u), kz[:, g, b * SC + kc, :],
                                             qT[:, b * SC + qc, :, 0:queries(u)], start=True, stop=True).then_inc(sc_done, 1)

                    def values(j):
                        b, qc, g = jobs[j]
                        t = b * SC + qc
                        if g == 0 and t >= 2:
                            pe.wait_ge(o_done, t - 1)
                        for u in range(first_unit[j], first_unit[j + 1]):
                            kc = units[u][3]
                            pe.wait_ge(ex_done, u + 1)
                            if masked[u]:
                                pe.wait_ge(mask_done, sum(masked[:u + 1]))
                            last = nc.tensor.matmul(cut(bank[4 + t % 2][32 * g:32 * g + 32, :], u), vx[:, b * SC + kc, g, :],
                                                    cut(pr[u % 4], u), start=kc == qc, stop=kc == 0)
                        last.then_inc(pv_done, 1)

                    def to_tokens(t):
                        pe.wait_ge(o_done, t + 1)
                        if t >= 2:
                            pe.wait_ge(normed, t - 1)
                        for a in range(G4):
                            last = nc.tensor.transpose(bank[6 + t % 2][:, a * P:(a + 1) * P], oT[t][:, a * P:(a + 1) * P], ident)
                        last.then_inc(o_turned, 1)
                    scores(0)
                    for j in range(len(jobs) + 2):
                        if j + 1 < len(jobs):
                            scores(j + 1)
                        if j < len(jobs):
                            values(j)
                        if j >= 5 and (j - 5) % KV == 0:
                            to_tokens((j - 5) // KV)
                    pe.wait_ge(normed, NT)
                    for t in range(NT):
                        last = nc.tensor.transpose(bank[0][:, t * P:(t + 1) * P], ao[:, t, :, :].rearrange("p h d -> p (h d)"), ident)
                    last.then_inc(turned, 1)
                    pe.wait_ge(aot, 1)
                    for t in range(NT):
                        last = nc.tensor.matmul(bank[1][:, t * P:(t + 1) * P], aoT[:, t * P:(t + 1) * P], wo, start=True, stop=True)
                    last.then_inc(y_made, 1)

                @block.scalar
                def _(act):
                    for j in range(len(jobs) + 2):
                        for u in range(first_unit[j], first_unit[j + 1]) if j < len(jobs) else ():
                            act.wait_ge(sc_done, u + 1)
                            if u >= 4:
                                act.wait_ge(pv_done, jobs.index(units[u - 4][0:3]) + 1)
                            act.activation(cut(pr[u % 4], u), cut(bank[u % 4][:, :], u), ACT.Exp, scale=float(1.0 / np.sqrt(8.0)))\
                               .then_inc(ex_done, 1)
                        if j >= 5 and (j - 5) % KV == 0:
                            t = (j - 5) // KV
                            act.wait_ge(pv_done, KV * (t + 1))
                            act.activation(oT[t], bank[4 + t % 2][:, :], ACT.Copy).then_inc(o_done, 1)
                    act.wait_ge(turned, 1)
                    act.activation(aoT, bank[0][:, :], ACT.Copy).then_inc(aot, 1)

                @block.vector
                def _(dve):
                    for j in range(len(jobs) + 3):
                        for u in range(first_unit[j], first_unit[j + 1]) if j < len(jobs) else ():
                            if masked[u]:
                                b, qc, g, kc = units[u]
                                m = W("const", ("near" if window else "causal") if kc == qc else "near_prev")[:, 0:queries(u)]
                                dve.wait_ge(ex_done, u + 1)
                                v = cut(pr[u % 4], u)
                                dve.tensor_tensor(v, v, m.unsqueeze(1).broadcast_to([P, G4, queries(u)]), ALU.mult).then_inc(mask_done, 1)
                        if j >= 6 and (j - 6) % KV == 0:
                            t = (j - 6) // KV
                            o = bank[6 + t % 2][:, :].rearrange("p (a g d) -> p g a d", a=G4, g=KV)
                            dve.wait_ge(o_turned, t + 1)
                            dve.reciprocal(rec[:, t, :].rearrange("p (g a) -> p g a", g=KV), o[:, :, :, 8]).then_inc(recip_s, 1)
                            dve.wait_ge(recip_s, t + 1)
                            dve.tensor_tensor(ao[:, t, :, :].rearrange("p (g a) d -> p g a d", g=KV), o[:, :, :, 0:8],
                                              rec[:, t, :].rearrange("p (g a) -> p g a", g=KV).unsqueeze(3).broadcast_to([P, KV, G4, 8]),
                                              ALU.mult).then_inc(normed, 1)
                    dve.wait_ge(y_made, 1)
                    dve.tensor_tensor(x_tok[:, :, :], v3(bank[1][:, :], NT), x_tok[:, :, :], ALU.add)

        def add_saved():
            with nc.Block() as block:
                @block.vector
                def _(dve):
                    dve.tensor_tensor(r_tok[:, :, :], acc[:, :, :], x_tok[:, :, :], ALU.add)

        def save_x():
            with nc.Block() as block:
                @block.vector
                def _(dve):
                    dve.tensor_copy(acc[:, :, :], x_tok[:, :, :])

        def l2_experts():
            made, negexp, step_s, gated = bsem("l2e_made"), bsem("l2e_exp"), bsem("l2e_step"), bsem("l2e_gated")
            up, silu, hid, down = bsem("l2e_up"), bsem("l2e_silu"), bsem("l2e_hid"), bsem("l2e_down")
            lg = v3(tiny[:, 0, :], NT)
            sc_ = v3(tiny[:, 1, :], NT)
            s1, s2, s3 = W("l2f", "s1"), W("l2f", "s2"), v3(W("l2f", "s3"), 4)
            w12, w3 = W("l2f", "w12"), v3(W("l2f", "w3"), NE)
            jobs = [(s1[:, c * P:(c + 1) * P], s2[:, c * P:(c + 1) * P]) for c in range(4)]
            jobs += [(w12[:, 2 * e * P:(2 * e + 1) * P], w12[:, (2 * e + 1) * P:(2 * e + 2) * P]) for e in range(NE)]
            sl = [bigB[:, k, :] for k in range(2)]
            hb = [bigA[:, k, :] for k in range(8)]
            with nc.Block() as block:
                @block.tensor
                def _(pe):
                    for t in range(NT):
                        last = nc.tensor.matmul(bank[7][:, t * NE:(t + 1) * NE], xT[:, t * P:(t + 1) * P], W("l2f", "rw"), start=True, stop=True)
                    last.then_inc(made, 1)

                    def downs(k):
                        pe.wait_ge(hid, 4 + k)
                        if k >= 2:
                            pe.wait_ge(gated, k - 1)
                        for t in range(NT):
                            for c in range(4 if k == 0 else 1):
                                h = hb[c] if k == 0 else hb[4 + (k - 1) % 4]
                                last = nc.tensor.matmul(bank[4 + k % 2][:, t * P:(t + 1) * P], h[:, t * P:(t + 1) * P],
                                                        s3[:, c, :] if k == 0 else w3[:, k - 1, :], start=c == 0, stop=c == (3 if k == 0 else 0))
                        last.then_inc(down, 1)
                    for j, (a, b_) in enumerate(jobs):
                        if j >= 2:
                            pe.wait_ge(hid, j - 1)
                        nc.tensor.matmul(bank[2 * (j % 2)][:, :], a, xT[:, :], start=True, stop=True).then_inc(up, 1)
                        nc.tensor.matmul(bank[2 * (j % 2) + 1][:, :], b_, xT[:, :], start=True, stop=True).then_inc(up, 1)
                        if j >= 4:
                            downs(j - 4)
                    downs(NE)

                @block.scalar
                def _(act):
                    act.wait_ge(made, 1)
                    act.activation(tiny[:, 0, :], bank[7][:, 0:NT * NE], ACT.Sigmoid).then_inc(negexp, 1)
                    for j in range(len(jobs)):
                        act.wait_ge(up, 2 * j + 1)
                        if j >= 2:
                            act.wait_ge(hid, j - 1)
                        act.activation(sl[j % 2], bank[2 * (j % 2)][:, :], ACT.Silu).then_inc(silu, 1)

                @block.vector
                def _(dve):
                    step = Chain(dve, step_s)

                    def hidden(j):
                        dve.wait_ge(silu, j + 1)
                        dve.wait_ge(up, 2 * j + 2)
                        if j >= 8:
                            dve.wait_ge(down, j - 6)
                        dve.tensor_tensor(hb[j if j < 4 else 4 + j % 4], sl[j % 2], bank[2 * (j % 2) + 1][:, :], ALU.mult).then_inc(hid, 1)

                    def gate(k):
                        dve.wait_ge(down, k + 1)
                        if k == 0:
                            step(dve.tensor_tensor(r_tok[:, :, :], v3(bank[4][:, :], NT), x_tok[:, :, :], ALU.add))
                            dve.sem_inc(gated, 1)
                            return
                        for t in range(NT):
                            dve.scalar_tensor_tensor(out=r_tok[:, t, :], in0=bank[4 + k % 2][:, t * P:(t + 1) * P],
                                                     scalar=weights_of[:, t, k - 1:k], in1=r_tok[:, t, :], op0=ALU.mult, op1=ALU.add)\
                               .then_inc(step_s, 1)
                            step.n += 1
                        dve.wait_ge(step_s, step.n)
                        dve.sem_inc(gated, 1)
                    dve.wait_ge(negexp, 1)
                    step(dve.tensor_tensor(sc_, lg, W("l2f", "eb").unsqueeze(1).broadcast_to([P, NT, NE]), ALU.add))
                    mxs, h1, h2 = top2(dve, step, sc_, NE)
                    step(dve.tensor_tensor(h1, h1, h2, ALU.add))
                    step(dve.tensor_tensor(weights_of, h1, lg, ALU.mult))
                    for j in range(len(jobs)):
                        hidden(j)
                        if j >= 5:
                            gate(j - 5)
                    gate(NE - 1)
                    gate(NE)

        ktok = flat3 = None

        def l3_attention():
            qtok, ktok = bigD, bias_t[:, :, :].rearrange("p h s -> p (h s)").rearrange("p (t n) -> p t n", t=NT)
            jobs = [(w, t, h) for w in ("wq", "wk", "wv") for t in range(NT) for h in range(2)]
            tok = {"wq": qtok, "wk": ktok, "wv": bigC}
            n2 = bigB[:, 0, 0:128]
            sqs = [bigA[:, k, :] for k in range(2)]
            made, copied, squared, summed, lens, esd, nq = [bsem(f"l3p_{n}") for n in
                                                            ("made", "copied", "squared", "summed", "lens", "es", "nq")]
            es = bigB[:, 1, 0:NH]
            rn = tiny[:, 8:12, :].rearrange("p a b -> p (a b)")
            with nc.Block() as block:
                @block.tensor
                def _(pe):
                    for i, (w, t, h) in enumerate(jobs):
                        if i >= 8:
                            pe.wait_ge(copied, i - 7)
                            if i - 8 < 16:
                                pe.wait_ge(squared, i - 7)
                        nc.tensor.matmul(bank[i % 8][:, :], xT[:, t * P:(t + 1) * P], W("l3a", w)[:, h * 512:(h + 1) * 512],
                                         start=True, stop=True).then_inc(made, 1)

                @block.scalar
                def _(act):
                    act.activation(es, W("l3a", "scale"), ACT.Exp).then_inc(esd, 1)
                    for i, (w, t, h) in enumerate(jobs):
                        act.wait_ge(made, i + 1)
                        act.activation(tok[w][:, t, h * 512:(h + 1) * 512], bank[i % 8][:, :], ACT.Copy).then_inc(copied, 1)
                        if w != "wv":
                            if i >= 2:
                                act.wait_ge(summed, i - 1)
                            act.activation(sqs[i % 2], bank[i % 8][:, :], ACT.Square).then_inc(squared, 1)

                @block.vector
                def _(dve):
                    for i, (w, t, h) in enumerate(jobs):
                        if w != "wv":
                            dve.wait_ge(squared, i + 1)
                            dve.tensor_reduce(n2[:, i * 8:(i + 1) * 8], v3(sqs[i % 2], 8), op=ALU.add, axis=AX).then_inc(summed, 1)
                    dve.wait_ge(summed, 16)
                    step = Chain(dve, lens)
                    step(dve.tensor_scalar(n2, n2, 1e-24, None, ALU.max))
                    rsqrt(dve, step, n2, rn, newton[:, :])
                    dve.wait_ge(esd, 1)
                    dve.tensor_tensor(v3(rn[:, 0:64], NT), v3(rn[:, 0:64], NT), es.unsqueeze(1).broadcast_to([P, NT, NH]), ALU.mult).then_inc(nq, 1)

            scaled, turned, act_out = [bsem(f"l3t_{n}") for n in ("scaled", "turned", "act_out")]
            items = [(0, c) for c in range(NCH)] + [(1, c) for c in range(NCH)]
            with nc.Block() as block:
                @block.vector
                def _(dve):
                    def scale_tile(k):
                        w, t = k // NT, k % NT
                        v = (qtok if w == 0 else ktok)[:, t, :].rearrange("p (h d) -> p h d", d=HD)
                        dve.tensor_tensor(v, v, rn[:, w * 64 + t * NH:w * 64 + (t + 1) * NH].unsqueeze(2).broadcast_to([P, NH, HD]), ALU.mult)\
                           .then_inc(scaled, 1)
                    for k in range(2 * NT):
                        scale_tile(k)

                @block.tensor
                def _(pe):
                    for i, (w, c) in enumerate(items):
                        pe.wait_ge(scaled, NT * (w + 1))
                        if i >= 8:
                            pe.wait_ge(act_out, i - 7)
                        for t in range(NT):
                            last = nc.tensor.transpose(bank[i % 8][:, t * P:(t + 1) * P], (qtok if w == 0 else ktok)[:, t, c * P:(c + 1) * P], ident)
                        last.then_inc(turned, 1)

                @block.scalar
                def _(act):
                    for i, (w, c) in enumerate(items):
                        act.wait_ge(turned, i + 1)
                        act.activation((bigA if w == 0 else bigB)[:, c, :], bank[i % 8][:, :], ACT.Copy).then_inc(act_out, 1)
            heads("l3h", lambda h: h // 2, lambda h: h * HD, False)
            out_proj("l3o", W("l3a", "wo"), bias=W("l3a", "bo"))

        def l3_experts():
            E4 = 4
            lg = v3(tiny[:, 0, :], NT)
            e_t, r_t, d_t = token_value(1), token_value(2), token_value(3)
            made, shifted, exped, weighed, wt, step_s = [bsem(f"l3f_{n}") for n in ("made", "shifted", "exped", "weighed", "wt", "step")]
            up, ubias, ustat, umean, un, ut, h_done, down = [bsem(f"l3f_{n}") for n in
                ("up", "ubias", "ustat", "umean", "un", "ut", "h", "down")]
            dbias, dstat, dmean, dn = [bsem(f"l3f_{n}") for n in ("dbias", "dstat", "dmean", "dn")]
            be_made = bsem("l3f_be")
            wtd = bsem("l3f_wtd")
            u = flat(bigA)[:, 0:2048].rearrange("p (e t d) -> p e t d", e=E4, t=NT)
            un_ = flat(bigA)[:, 2048:4096].rearrange("p (e t d) -> p e t d", e=E4, t=NT)
            hT = [bigC[:, k, 0:512] for k in range(4)]
            d_ = flat(bigD)[:, 0:2048].rearrange("p (e t d) -> p e t d", e=E4, t=NT)
            w1, w2 = W("l3f", "w1"), W("l3f", "w2")
            b1, b2, g2 = W("l3f", "b1"), W("l3f", "b2"), W("l3f", "g2")
            with nc.Block() as block:
                @block.tensor
                def _(pe):
                    for t in range(NT):
                        last = nc.tensor.matmul(bank[7][:, t * 8:t * 8 + E4], xT[:, t * P:(t + 1) * P], W("l3f", "gw"), start=True, stop=True)
                    last.then_inc(made, 1)
                    for e in range(E4):
                        for t in range(NT):
                            last = nc.tensor.matmul(bank[e][:, t * P:(t + 1) * P], xT[:, t * P:(t + 1) * P], w1[:, e * P:(e + 1) * P],
                                                    start=True, stop=True)
                        last.then_inc(up, 1)
                    pe.wait_ge(weighed, 1)
                    for t in range(NT):
                        last = nc.tensor.transpose(bank[4][0:8, t * P:(t + 1) * P], weights_of[:, t, :], ident)
                    last.then_inc(wt, 1)
                    for e in range(E4):
                        pe.wait_ge(un, NT * (e + 1))
                        for t in range(NT):
                            last = nc.tensor.transpose(bank[e][:, t * P:(t + 1) * P], un_[:, e, t, :], ident)
                        last.then_inc(ut, 1)
                    for e in range(E4):
                        pe.wait_ge(h_done, e + 1)
                        for t in range(NT):
                            last = nc.tensor.matmul(bank[e][:, t * P:(t + 1) * P], hT[e][:, t * P:(t + 1) * P], w2[:, e * P:(e + 1) * P],
                                                    start=True, stop=True)
                        last.then_inc(down, 1)
                    pe.wait_ge(wtd, 1)
                    for t in range(NT):
                        last = nc.tensor.matmul(bank[5][:, t * P:(t + 1) * P], weightsT[0:E4, t * P:(t + 1) * P], held["be2"], start=True, stop=True)
                    last.then_inc(be_made, 1)

                @block.scalar
                def _(act):
                    act.wait_ge(shifted, 1)
                    act.activation(e_t, d_t, ACT.Exp).then_inc(exped, 1)
                    act.wait_ge(wt, 1)
                    act.activation(weightsT[:, :], bank[4][0:8, :], ACT.Copy).then_inc(wtd, 1)
                    for e in range(E4):
                        act.wait_ge(ut, e + 1)
                        act.activation(hT[e], bank[e][:, :], ACT.Relu, bias=W("l3f", "be1")[:, e:e + 1], scale=W("l3f", "g1")[:, e:e + 1])\
                           .then_inc(h_done, 1)

                @block.vector
                def _(dve):
                    step = Chain(dve, step_s)
                    step(dve.memset(tiny[:, 0, :], -3.0e38))
                    dve.wait_ge(made, 1)
                    step(dve.tensor_tensor(lg[:, :, 0:E4], v3(bank[7][:, 0:NT * 8], NT)[:, :, 0:E4],
                                           W("l3f", "gb").unsqueeze(1).broadcast_to([P, NT, E4]), ALU.add))
                    mxs, h1, h2 = top2(dve, step, lg, E4)
                    softmax_of_two(dve, (shifted, exped), step, mxs, h1, h2, weights_of, e_t, r_t, d_t)
                    dve.sem_inc(weighed, 1)

                    def normed(src_done, bias, dst, sb_, ss, sm_):
                        for e in range(E4):
                            dve.wait_ge(src_done, e + 1)
                            dve.tensor_tensor(dst[:, e, :, :], v3(bank[e][:, :], NT), bias[:, e * P:(e + 1) * P].unsqueeze(1).broadcast_to([P, NT, P]),
                                              ALU.add).then_inc(sb_, 1)
                        for k in range(16):
                            dve.wait_ge(sb_, k // NT + 1)
                            dve.bn_stats(stats[:, k, :], dst[:, k // NT, k % NT, :]).then_inc(ss, 1)
                        for k in range(16):
                            dve.wait_ge(ss, k + 1)
                            dve.bn_aggr(mv[:, k, :], stats[:, k, :]).then_inc(sm_, 1)
                        dve.wait_ge(sm_, 16)
                        step(dve.tensor_scalar(var_e[:, :], mv[:, :, 1], LN_EPS, None, ALU.add))
                        rsqrt(dve, step, var_e[:, :], rstd[:, :], newton[:, 0:16])
                    normed(up, b1, u, ubias, ustat, umean)
                    for k in range(16):
                        dve.tensor_scalar(un_[:, k // NT, k % NT, :], u[:, k // NT, k % NT, :], mv[:, k, 0:1], rstd[:, k:k + 1],
                                          ALU.subtract, ALU.mult).then_inc(un, 1)
                    dve.wait_ge(un, 16)
                    normed(down, b2, d_, dbias, dstat, dmean)
                    step(dve.tensor_tensor(v3(rstd[:, :], E4), v3(rstd[:, :], E4), weights_of[:, :, 0:E4].rearrange("p t e -> p e t"), ALU.mult))
                    for k in range(16):
                        dve.tensor_scalar(u[:, k // NT, k % NT, :], d_[:, k // NT, k % NT, :], mv[:, k, 0:1], rstd[:, k:k + 1],
                                          ALU.subtract, ALU.mult).then_inc(dn, 1)
                    dve.wait_ge(be_made, 1)
                    step(dve.scalar_tensor_tensor(out=r_tok[:, :, :], in0=x_tok[:, :, :], scalar=2.0, in1=v3(bank[5][:, :], NT),
                                                  op0=ALU.mult, op1=ALU.add))
                    for e in range(E4):
                        dve.wait_ge(dn, NT * (e + 1))
                        step(dve.tensor_tensor(u[:, e, :, :], u[:, e, :, :], g2[:, e * P:(e + 1) * P].unsqueeze(1).broadcast_to([P, NT, P]), ALU.mult))
                        step(dve.tensor_tensor(r_tok[:, :, :], r_tok[:, :, :], u[:, e, :, :], ALU.add))

        def wait_for(eng, pks):
            for pk in pks:
                eng.wait_ge(loaded[pk], 16)

        first_loads()
        l0_bias()
        expms()
        zero_slots()
        with nc.Block() as block:
            @block.vector
            def _(dve):
                wait_for(dve, ("first", "const", "l0a"))
                dve.wait_ge(loaded_x, 16)
        with nc.Fori(0, GROUPS) as g:
            take_x("l0x", g)
            l0_attention()
            post_norm("l0n")
            route0(g)
            end_of_body()
        end_of_loop()
        with nc.Fori(0, NE // 2) as pair:
            expert_pair(pair * 2)
            end_of_body()
        end_of_loop()
        fold_lora()
        with nc.Fori(0, GROUPS) as g:
            combine0(g)
            post_norm("l0m")
            l1_project()
            heads("l1h", lambda h: 2 * (h // 4) + h % 2, lambda h: h // 4 * HD, False, whole=True)
            out_proj("l1o", W("l1a", "wo"))
            post_norm("l1n")
            pre_norm("l1q", W("l1f", "gamma"), W("l1f", "beta"), True)
            l1_route()
            l1_experts()
            l1_mix()
            post_norm("l1y")
            keep_x(g)
            end_of_body()
        end_of_loop()
        load_late()
        with nc.Fori(0, GROUPS) as g:
            take_x("l2x", g)
            save_x()
            pre_norm("gn", W("l2a", "n1"), None, False)
            narrow("g", W("l2a", "g_wq"), held["l2up"], W("l2a", "g_wo"), W("l2a", "g_down"), False)
            pre_norm("ln", W("l2a", "n2"), None, False)
            narrow("l", W("l2a", "l_wq"), W("l2a", "l_wkv"), W("l2a", "l_wo"), None, True)
            add_saved()
            post_norm("l2n")
            l2_experts()
            post_norm("l2m")
            keep_x(g)
            end_of_body()
        end_of_loop()
        with nc.Fori(0, GROUPS) as g:
            take_x("l3x", g)
            l3_attention()
            post_norm("l3n")
            l3_experts()
            post_norm("l3m", True, g)
            end_of_body()
        end_of_loop()


def kernel(**inputs):
    import numpy as _np
    import concourse.bacc as _bacc
    from concourse import mybir as _mybir
    from concourse.bass_utils import run_bass_kernel_spmd as _run

    w = {n: _np.asarray(a) for n, a in inputs.items()}
    nc = _bacc.Bacc("TRN2", target_bir_lowering=False, num_devices=1)
    f32 = _mybir.dt.float32
    x = _np.ascontiguousarray(w["L0_attn_x"])
    arrays, packs, where = {"in_x": x}, {}, {}
    x_dram = nc.dram_tensor("in_x", x.shape, f32, kind="ExternalInput").ap()
    for pk, parts in layout(w).items():
        at, where[pk] = 0, {}
        for name, a in parts:
            where[pk][name] = (at, at + a.shape[1])
            at += a.shape[1]
        a = _np.ascontiguousarray(_np.concatenate([a for _, a in parts], axis=1))
        arrays[f"in_{pk}"] = a
        packs[pk] = nc.dram_tensor(f"in_{pk}", a.shape, f32, kind="ExternalInput").ap()
    out = nc.dram_tensor("out", (ALL_B, S, P), f32, kind="ExternalOutput").ap()
    dram = {"rpe": nc.dram_tensor("rpe_rows", (NH, S + P), f32, kind="Internal").ap(),
            "slots": nc.dram_tensor("slots", (ALL_T, P), f32, kind="Internal").ap(),
            "results": nc.dram_tensor("results", (ALL_T, P), f32, kind="Internal").ap()}
    program(nc, x_dram, packs, where, out, dram)
    r = _run(nc, [arrays], core_ids=[0])
    return r.results[0]["out"]
```

```python
from contextlib import ExitStack

import numpy as np

import concourse.bass as bass
from concourse import mybir

F32 = mybir.dt.float32
U32 = mybir.dt.uint32
I32 = mybir.dt.int32
ALU = mybir.AluOpType
ACT = mybir.ActivationFunctionType
AX = mybir.AxisListType.X

P = 128
ALL_B, S = 16, 256
B = 2
T = B * S
GROUPS = ALL_B // B
ALL_T = ALL_B * S
NT = T // P
NE = 8
CAP = ALL_T // NE
SC = S // P
NH, HD = 16, 64
NCH = NH * HD // P
PAD = -30000.0
LN_EPS = 1e-5
RMS_EPS = 1e-6


def chunked(a):
    c = a.shape[0] // P
    return np.ascontiguousarray(a.reshape(c, P, -1).transpose(1, 0, 2).reshape(P, -1))


def on_all_partitions(v):
    return np.broadcast_to(v.reshape(1, -1), (P, v.size))


def constants():
    i = np.arange(P)
    c = {}
    c["ident"] = np.eye(P)
    c["flip"] = np.eye(P)[::-1]
    j, u = np.arange(S)[:, None], np.arange(S)[None, :]
    c["revtri"] = chunked((j <= S - 1 - u).astype(np.float32))
    c["upto"] = (i[:, None] <= i[None, :])
    c["ones"] = np.ones((P, P))
    c["slot0"] = np.broadcast_to(CAP * np.arange(8.0), (P, 8))
    c["rows32"] = (i[:, None] // 32 == np.arange(4)[None, :])
    c["iota8"] = np.broadcast_to(np.arange(8.0), (P, 8))
    c["desc8"] = np.broadcast_to(8 - np.arange(8.0), (P, 8))
    c["neghalf"] = np.full((P, P), -0.5)
    inv = 1.0 / 10000.0 ** (np.arange(0, HD, 2, dtype=np.float32) / np.float32(HD))
    ang = np.arange(S, dtype=np.float32)[None, :] * inv.astype(np.float32)[:, None]
    cos, sin = np.cos(ang), np.sin(ang)
    ch = np.tile(np.concatenate([cos, cos]), (2, B))
    sh = np.tile(np.concatenate([-sin, sin]), (2, B))
    c["rope_cos"], c["rope_sin"] = ch, sh
    for tag, base in (("g", 1000000.0), ("l", 10000.0)):
        inv = (1.0 / np.float32(base) ** (np.arange(0, 8, 2, dtype=np.float32) / np.float32(8))).astype(np.float32)
        ang = np.arange(S, dtype=np.float32)[:, None] * inv[None, :]
        for nm, f in (("cos", np.cos), ("sin", np.sin)):
            t = np.tile(f(ang), (B, 1)).reshape(NT, P, 4).transpose(1, 0, 2)
            c[f"{tag}_{nm}"] = t.reshape(P, -1)
    d = i[None, :] - i[:, None]
    c["causal"] = (d >= 0)
    c["near"] = (d >= 0) & (d < 32)
    c["near_prev"] = (d + P < 32)
    return {k: np.ascontiguousarray(v, dtype=np.float32) for k, v in c.items()}


def layout(w):
    rows = lambda a: a
    L = {}
    qkv = w["L0_attn_qkv"].reshape(P, 3, NH * HD)
    L["first"] = [("rpe", chunked(w["L0_attn_rpe_bias"].T)), ("wg", w["L0_ffn_wg"])]
    L["l0a"] = [("wq", qkv[:, 0]), ("wk", qkv[:, 1]), ("wv", qkv[:, 2]),
                ("wo", chunked(w["L0_attn_out_w"].reshape(NH * HD, P)))]
    w1 = w["L0_ffn_w1"]
    w2 = w["L0_ffn_w2"].reshape(NE, 4, P, P).transpose(0, 2, 1, 3).reshape(NE, P, 4 * P)
    b1 = w["L0_ffn_b1"].reshape(NE, 4, P).transpose(0, 2, 1)
    b2 = np.broadcast_to(w["L0_ffn_b2"][:, None, :], (NE, P, P))
    L["l0f"] = [("all", np.concatenate([w1, w2, b1, b2], axis=2).reshape(NE * P, -1))]
    L["gens"] = [("a", w["L1_ffn_gens"].transpose(1, 0, 2).reshape(P, -1)),
                 ("aT", w["L1_ffn_gens"].transpose(2, 0, 1).reshape(P, -1))]
    half = np.arange(0, HD, 2)
    fwd = np.concatenate([half, half + 1])
    bwd = np.concatenate([half + 1, half])

    def by_head(a, order, twice=False):
        h = a.reshape(-1, HD, a.shape[1])[:, order]
        if twice:
            h = np.repeat(h, 2, axis=0)
        return h.reshape(-1, a.shape[1]).T

    L["l1a"] = []
    for nm, tw in (("q", False), ("k", True)):
        for tag, order in (("", fwd), ("s", bwd)):
            L["l1a"].append((f"w{nm}{tag}", by_head(w[f"L1_attn_W{nm}"], order, tw)))
    L["l1a"].append(("wv", w["L1_attn_Wv"].T))
    L["l1a"].append(("wo", chunked(w["L1_attn_Wo"].T)))
    L["lora"] = []
    for nm, tw in (("q", False), ("k", True)):
        L["lora"].append((f"{nm}A", w[f"L1_attn_{nm}A"]))
        for tag, order in (("", fwd), ("s", bwd)):
            L["lora"].append((f"{nm}B{tag}", by_head(w[f"L1_attn_{nm}B"], order, tw)))
    L["lora"] += [("vA", w["L1_attn_vA"]), ("vB", w["L1_attn_vB"].T), ("oA", w["L1_attn_oA"]), ("oB", w["L1_attn_oB"].T)]
    L["eb2"] = [("eb2", w["L1_ffn_eb2"])]
    L["be2"] = [("be2", w["L3_ffn_be2"])]
    L["l1f"] = [("gamma", w["L1_ffn_ln_gamma"].reshape(P, 1)), ("beta", w["L1_ffn_ln_beta"].reshape(P, 1)),
                ("abel_w", w["L1_ffn_abel_w"]), ("abel_b", on_all_partitions(w["L1_ffn_abel_b"])),
                ("gate_w", w["L1_ffn_moe_gate_w"]), ("gate_b", on_all_partitions(w["L1_ffn_moe_gate_b"])),
                ("eb1", w["L1_ffn_eb1"].reshape(8, 2, P).transpose(2, 0, 1).reshape(P, -1)),
                ("gc_w", on_all_partitions(w["L1_ffn_gc_w"])), ("gc_b", on_all_partitions(w["L1_ffn_gc_b"])),
                ("ew1", w["L1_ffn_ew1"].transpose(1, 0, 2).reshape(P, -1)),
                ("ew2", w["L1_ffn_ew2"].reshape(8, 2, P, P).transpose(2, 0, 1, 3).reshape(P, -1))]
    L["l2a"] = [("n1", w["L2_attn_norm1_w"].reshape(P, 1)), ("n2", w["L2_attn_norm2_w"].reshape(P, 1)),
                ("g_wq", w["L2_attn_g_wq"]), ("g_down", w["L2_attn_g_kv_down"]), ("g_wo", w["L2_attn_g_wo"]),
                ("l_wq", w["L2_attn_l_wq"]), ("l_wkv", np.concatenate([w["L2_attn_l_wk"], w["L2_attn_l_wv"]], 1)),
                ("l_wo", w["L2_attn_l_wo"])]
    L["l2up"] = [("up", np.concatenate([w["L2_attn_g_k_up"], w["L2_attn_g_v_up"]], 1))]
    L["l2f"] = [("rw", w["L2_ffn_router_w"].T), ("eb", on_all_partitions(w["L2_ffn_expert_bias"])),
                ("s1", w["L2_ffn_shared_w1"].T), ("s2", w["L2_ffn_shared_w2"].T), ("s3", chunked(w["L2_ffn_shared_w3"].T)),
                ("w12", w["L2_ffn_w12"].transpose(2, 0, 1).reshape(P, -1)),
                ("w3", w["L2_ffn_w3"].transpose(2, 0, 1).reshape(P, -1))]
    kv = w["L3_attn_w_kv"]
    L["l3a"] = [("wq", w["L3_attn_w_q"]), ("wk", kv[:, :NH * HD]), ("wv", kv[:, NH * HD:]),
                ("wo", chunked(w["L3_attn_w_out"])), ("bo", on_all_partitions(w["L3_attn_b_out"])),
                ("scale", on_all_partitions(w["L3_attn_scale"]))]
    L["l3f"] = [("gw", w["L3_ffn_gate_W"]), ("gb", on_all_partitions(w["L3_ffn_gate_b"])),
                ("w1", w["L3_ffn_W1"].transpose(1, 0, 2).reshape(P, -1)),
                ("b1", on_all_partitions(w["L3_ffn_b1"])),
                ("g1", w["L3_ffn_g1"].T), ("be1", w["L3_ffn_be1"].T),
                ("w2", w["L3_ffn_W2"].transpose(1, 0, 2).reshape(P, -1)),
                ("b2", on_all_partitions(w["L3_ffn_b2"])),
                ("g2", on_all_partitions(w["L3_ffn_g2"]))]
    L["const"] = list(constants().items())
    return L


def program(nc, x_dram, packs, where, out, dram):
    ctx = ExitStack()
    with ctx:
        def sb(name, shape, dt=F32):
            return ctx.enter_context(nc.sbuf_tensor(name, shape, dt))

        def sem(name):
            return ctx.enter_context(nc.semaphore(name))

        body_sems = []

        loop_scope = [ExitStack()]

        def bsem(name):
            body_sems.append(loop_scope[0].enter_context(nc.semaphore(name)))
            return body_sems[-1]

        def end_of_body():
            with nc.Block(no_gpsimd_drain=True) as block:
                @block.gpsimd
                def _(pool):
                    nums = sorted(s_.num for s_ in body_sems)
                    while nums:
                        n = 1
                        while n < len(nums) and nums[n] == nums[0] + n:
                            n += 1
                        pool.sem_clear(range(nums[0], nums[0] + n))
                        nums = nums[n:]
            body_sems.clear()

        def end_of_loop():
            loop_scope[0].close()
            loop_scope[0] = ExitStack()

        x_all = sb("x_all", [P, GROUPS * NT, P])
        x_tok = sb("x_tok", [P, NT, P])
        xT = sb("xT", [P, T])
        r_tok = sb("r_tok", [P, NT, P])
        bigA = sb("bigA", [P, NCH, T])
        bigB = sb("bigB", [P, NCH, T])
        bigC = sb("bigC", [P, NT, NH * HD])
        bigD = sb("bigD", [P, NT, NH * HD])
        bias_t = sb("bias_t", [P, NH, S])
        prob = sb("prob", [P, 4, SC, S])
        probT = sb("probT", [P, 3, 4, P])
        raw = prob
        nmax = sb("nmax", [P, B * NH, SC])
        sums = sb("sums", [P, 8, SC, 4])
        rsum = sb("rsum", [P, 8, SC, 4])
        rot = sb("rot", [P, P])
        stats = sb("stats", [P, 16, 6])
        mv = sb("mv", [P, 16, 2])
        var_e = sb("var_e", [P, 16])
        rstd = sb("rstd", [P, 16])
        newton = sb("newton", [P, 128])
        tiny = sb("tiny", [P, 24, NT * NE])
        ix8 = sb("ix8", [P, NT, 8], U32)
        taken = sb("taken", [P, NE])
        slot_f = sb("slot_f", [P, NT])
        slot_w = sb("slot_w", [P, GROUPS * NT], U32)
        slot_r = sb("slot_r", [P, (GROUPS + 1) * NT], U32)
        gate0 = sb("gate0", [P, GROUPS * NT])
        bank = [ctx.enter_context(nc.psum_tensor(f"bank{i}", [P, 512], F32)) for i in range(8)]

        def flat(t):
            return t[:, :, :].rearrange("p a b -> p (a b)")

        held = {}
        lora_cols = packs["lora"].shape[1]
        home_l0a = sb("home_l0a", [P, max(packs["l0a"].shape[1], packs["l3a"].shape[1])])
        held["l0a"] = home_l0a[:, 0:packs["l0a"].shape[1]]
        held["l3a"] = home_l0a[:, 0:packs["l3a"].shape[1]]
        early, late = ("l1a", "l1f"), ("l2a", "l2up", "l2f", "l3f")
        width = {pk: ap.shape[1] for pk, ap in packs.items()}
        home_l1 = sb("home_l1", [P, max(sum(width[pk] for pk in early), sum(width[pk] for pk in late))])
        for some in (early, late):
            at = 0
            for pk in some:
                held[pk] = home_l1[0:packs[pk].shape[0], at:at + width[pk]]
                at += width[pk]
        held["gens"] = flat(bigB)[:, 0:width["gens"]]
        for pk in ("first", "const", "eb2", "be2"):
            held[pk] = sb(f"w_{pk}", list(packs[pk].shape))[:, :]
        loaded = {pk: sem(f"loaded_{pk}") for pk in packs}
        loaded_x = sem("loaded_x")

        def W(pk, part):
            a, b = where[pk][part]
            return held[pk][:, a:b]

        def v3(ap, n):
            return ap.rearrange("p (a b) -> p a b", a=n)

        ident = W("const", "ident")
        neghalf = W("const", "neghalf")

        class Chain:
            def __init__(self, eng, s_):
                self.eng, self.sem, self.n = eng, s_, 0

            def __call__(self, ins):
                self.n += 1
                ins.then_inc(self.sem, 1)
                self.eng.wait_ge(self.sem, self.n)

        def rsqrt(dve, step, v, y, t):
            step(dve.tensor_scalar(y.bitcast(I32), v.bitcast(I32), -0.5, 1597463007.0, ALU.mult, ALU.add))
            for _ in range(3):
                step(dve.scalar_tensor_tensor(out=t, in0=v, scalar=-0.5, in1=y, op0=ALU.mult, op1=ALU.mult))
                step(dve.tensor_tensor(t, t, y, ALU.mult))
                step(dve.scalar_tensor_tensor(out=y, in0=t, scalar=1.5, in1=y, op0=ALU.add, op1=ALU.mult))

        put, fetched, stored = sem("slots_put"), sem("results_fetched"), sem("stored")
        cleared, zeroed = sem("z_cleared"), sem("z_zeroed")
        zeros = prob[:, :, :, :].rearrange("p a c s -> p (a c s)")

        def first_loads():
            with nc.Block(no_gpsimd_drain=True) as block:
                @block.vector
                def _(dve):
                    dve.sem_inc(stored, 1)
                    dve.memset(taken[:, :], 0.0)
                    dve.memset(zeros, 0.0).then_inc(cleared, 1)

                @block.sync
                def _(sp):
                    x_view = x_dram.rearrange("b (c p) d -> p (b c) d", p=P)
                    for pk in ("const", "first", "gens", "l0a"):
                        sp.dma_start(held[pk], packs[pk]).then_inc(loaded[pk], 16)
                    sp.dma_start(x_all[:, :, :], x_view).then_inc(loaded_x, 16)
                    for pk in ("eb2", "be2"):
                        sp.dma_start(held[pk], packs[pk]).then_inc(loaded[pk], 16)
                    sp.wait_ge(cleared, 1)
                    rows = dram["slots"].rearrange("(h p n) d -> h p (n d)", h=2, p=P)
                    for h in range(2):
                        sp.dma_start(rows[h], zeros).then_inc(zeroed, 16)

        def all_stored():
            with nc.Block(no_gpsimd_drain=True) as block:
                @block.sync
                def _(sp):
                    sp.wait_ge(stored, 16 * GROUPS + 1)

        def post_norm(tag, last=False, group=None):
            stat_done, mean_done, step_s = bsem(f"{tag}_stat"), bsem(f"{tag}_mean"), bsem(f"{tag}_step")
            x_done, xt_done = bsem(f"{tag}_x"), bsem(f"{tag}_xt")
            y = to_put if last else x_tok
            with nc.Block(no_gpsimd_drain=True) as block:
                @block.vector
                def _(dve):
                    for t in range(NT):
                        dve.bn_stats(stats[:, t, :], r_tok[:, t, :]).then_inc(stat_done, 1)
                    for t in range(NT):
                        dve.wait_ge(stat_done, t + 1)
                        dve.bn_aggr(mv[:, t, :], stats[:, t, :]).then_inc(mean_done, 1)
                    dve.wait_ge(mean_done, NT)
                    step = Chain(dve, step_s)
                    step(dve.tensor_scalar(var_e[:, 0:NT], mv[:, 0:NT, 1], LN_EPS, None, ALU.add))
                    rsqrt(dve, step, var_e[:, 0:NT], rstd[:, 0:NT], newton[:, 0:NT])
                    if last:
                        dve.wait_ge(stored, 16 * group + 1)
                    for t in range(NT):
                        dve.tensor_scalar(y[:, t, :], r_tok[:, t, :], mv[:, t, 0:1], rstd[:, t:t + 1],
                                          ALU.subtract, ALU.mult).then_inc(x_done, 1)

                if last:
                    @block.sync
                    def _(sp):
                        sp.wait_ge(x_done, NT)
                        sp.dma_start(out.rearrange("(g b) (c p) d -> p g (b c) d", p=P, b=B)[:, group_slice(group), :, :],
                                     y[:, :, :].unsqueeze(1)).then_inc(stored, 16)
                    return

                @block.tensor
                def _(pe):
                    for t in range(NT):
                        pe.wait_ge(x_done, t + 1)
                        nc.tensor.transpose(bank[0][:, t * P:(t + 1) * P], x_tok[:, t, :], ident).then_inc(xt_done, 1)

                @block.scalar
                def _(act):
                    act.wait_ge(xt_done, NT)
                    act.activation(xT[:, :], bank[0][:, :], ACT.Copy)

        def group_slice(i):
            return bass.ds(i, 1) if not isinstance(i, int) else slice(i, i + 1)

        def keep_x(group):
            with nc.Block(no_gpsimd_drain=True) as block:
                @block.vector
                def _(dve):
                    dve.tensor_copy(x_all[:, bass.ts(group, NT), :], x_tok[:, :, :])

        def load_late():
            with nc.Block(no_gpsimd_drain=True) as block:
                @block.sync
                def _(sp):
                    for pk in late:
                        sp.dma_start(held[pk], packs[pk]).then_inc(loaded[pk], 16)
                    for pk in late:
                        sp.wait_ge(loaded[pk], 16)
                    sp.wait_ge(fetched, 16 * NT * (GROUPS + 1))

        def take_x(tag, group):
            took, turned = bsem(f"{tag}_took"), bsem(f"{tag}_turned")
            with nc.Block(no_gpsimd_drain=True) as block:
                @block.vector
                def _(dve):
                    dve.tensor_copy(x_tok[:, :, :], x_all[:, bass.ts(group, NT), :]).then_inc(took, 1)

                @block.tensor
                def _(pe):
                    pe.wait_ge(took, 1)
                    for t in range(NT):
                        last = nc.tensor.transpose(bank[0][:, t * P:(t + 1) * P], x_tok[:, t, :], ident)
                    last.then_inc(turned, 1)

                @block.scalar
                def _(act):
                    act.wait_ge(turned, 1)
                    act.activation(xT[:, :], bank[0][:, :], ACT.Copy)

        keys_even = bigB
        keys_odd = home_l1[:, 0:NCH * T].rearrange("p (c t) -> p c t", c=NCH)

        def zero_beside_keys():
            with nc.Block(no_gpsimd_drain=True) as block:
                @block.vector
                def _(dve):
                    dve.memset(keys_even[HD:P, :, :], 0.0)
                    dve.memset(keys_odd[0:HD, :, :], 0.0)

        def project(tag, items, needs):
            made, act_out, dve_out = bsem(f"{tag}_made"), bsem(f"{tag}_act_out"), bsem(f"{tag}_dve_out")
            with nc.Block(no_gpsimd_drain=True) as block:
                @block.tensor
                def _(pe):
                    for pk, cnt in needs:
                        pe.wait_ge(loaded[pk], cnt)
                    for i, (l, r, d, s) in enumerate(items):
                        if i >= 8:
                            pe.wait_ge(act_out if i % 2 == 0 else dve_out, (i - 8) // 2 + 1)
                        nc.tensor.matmul(bank[i % 8][:, :], l, r, start=True, stop=True).then_inc(made, 1)

                @block.scalar
                def _(act):
                    for i, (l, r, d, s) in enumerate(items):
                        if i % 2 == 0:
                            act.wait_ge(made, i + 1)
                            if isinstance(d, tuple):
                                act.activation(d[0], bank[i % 8][0:HD, :], ACT.Copy, scale=s)
                                act.activation(d[1], bank[i % 8][HD:P, :], ACT.Copy, scale=s).then_inc(act_out, 1)
                            else:
                                act.activation(d, bank[i % 8][:, :], ACT.Copy, scale=s).then_inc(act_out, 1)

                @block.vector
                def _(dve):
                    for i, (l, r, d, s) in enumerate(items):
                        if i % 2 == 1:
                            dve.wait_ge(made, i + 1)
                            if isinstance(d, tuple):
                                dve.tensor_scalar(d[0], bank[i % 8][0:HD, :], s, None, ALU.mult)
                                dve.tensor_scalar(d[1], bank[i % 8][HD:P, :], s, None, ALU.mult).then_inc(dve_out, 1)
                            else:
                                dve.tensor_scalar(d, bank[i % 8][:, :], s, None, ALU.mult).then_inc(dve_out, 1)

        def heads(tag, keys_of, v_col, causal):
            n_it = B * NH
            scores_done, max_done, exp_done = bsem(f"{tag}_scores"), bsem(f"{tag}_max"), bsem(f"{tag}_exp")
            trans_done, act_copy, dve_copy = bsem(f"{tag}_trans"), bsem(f"{tag}_act_copy"), bsem(f"{tag}_dve_copy")
            pv_done, norm_done, dve_step = bsem(f"{tag}_pv"), bsem(f"{tag}_norm"), bsem(f"{tag}_dve")
            keys = [P, S] if causal else [S, S]
            blocks = [(kc, qc) for kc in range(SC) for qc in range(SC) if kc * P < keys[qc]]

            def bh(i):
                return i // NH, i % NH

            def by_act(i):
                return causal or i % 2 == 1

            def copies(i):
                return i + 1 if causal else i // 2 + 1

            with nc.Block(no_gpsimd_drain=True) as block:
                @block.tensor
                def _(pe):
                    def scores(i):
                        b, h = bh(i)
                        if i >= 3:
                            pe.wait_ge(exp_done, 2 * (i - 2))
                        for qc in range(SC):
                            q = bigA[:, h // 2, b * S + qc * P:b * S + qc * P + P]
                            k = keys_of(h)[:, b * S:b * S + keys[qc]]
                            last = nc.tensor.matmul(bank[i % 3][:, qc * S:qc * S + keys[qc]], q, k, start=True, stop=True)
                        last.then_inc(scores_done, 1)

                    def transposes(i):
                        pe.wait_ge(exp_done, 2 * i + 2)
                        if i >= 3:
                            j = i - 3
                            pe.wait_ge(act_copy if by_act(j) else dve_copy, copies(j))
                        for m, (kc, qc) in enumerate(blocks):
                            last = nc.tensor.transpose(bank[3 + i % 3][:, m * P:(m + 1) * P],
                                                       prob[:, i % 4, qc, kc * P:(kc + 1) * P], ident)
                        last.then_inc(trans_done, 1)

                    def values(i):
                        b, h = bh(i)
                        pe.wait_ge(act_copy if by_act(i) else dve_copy, copies(i))
                        g = i // 4
                        if i % 4 == 0 and g >= 2:
                            pe.wait_ge(norm_done, g - 1)
                        for qc in range(SC):
                            mine = [(m, kc) for m, (kc, q2) in enumerate(blocks) if q2 == qc]
                            for n_, (m, kc) in enumerate(mine):
                                last = nc.tensor.matmul(bank[6 + g % 2][:, qc * S + (h % 4) * HD:qc * S + (h % 4) * HD + HD],
                                                        probT[:, i % 3, m, :], bigC[:, b * SC + kc, v_col(h):v_col(h) + HD],
                                                        start=n_ == 0, stop=n_ == len(mine) - 1)
                        last.then_inc(pv_done, 1)

                    for i in range(n_it + 3):
                        if i < n_it:
                            scores(i)
                        if 0 <= i - 2 < n_it:
                            transposes(i - 2)
                        if 0 <= i - 3 < n_it:
                            values(i - 3)

                @block.vector
                def _(dve):
                    def copy_out(i):
                        dve.wait_ge(trans_done, i + 1)
                        if i >= 3:
                            dve.wait_ge(pv_done, i - 2)
                        m = len(blocks)
                        dve.tensor_copy(probT[:, i % 3, 0:m, :], bank[3 + i % 3][:, 0:m * P].rearrange("p (m c) -> p m c", m=m))\
                           .then_inc(dve_copy, 1)

                    def row_max(i):
                        b, h = bh(i)
                        dve.wait_ge(scores_done, i + 1)
                        if causal:
                            if i >= 4:
                                dve.wait_ge(trans_done, i - 3)
                            for qc in range(SC):
                                dve.tensor_tensor(raw[:, i % 4, qc, 0:keys[qc]], bank[i % 3][:, qc * S:qc * S + keys[qc]],
                                                  bias_t[:, h, S - keys[qc]:S], ALU.add).then_inc(dve_step, 1)
                            for qc in range(SC):
                                dve.wait_ge(dve_step, 2 * i + qc + 1)
                                dve.tensor_reduce(nmax[:, i, qc:qc + 1], raw[:, i % 4, qc, 0:keys[qc]], op=ALU.max,
                                                  axis=AX, negate=True).then_inc(max_done, 1)
                        else:
                            dve.tensor_reduce(nmax[:, i, :], bank[i % 3][:, :].rearrange("p (c t) -> p c t", c=SC), op=ALU.max,
                                              axis=AX, negate=True).then_inc(max_done, 2)

                    def normalise(g):
                        b, h = bh(4 * g)
                        dve.wait_ge(exp_done, 8 * g + 8)
                        dve.reciprocal(rsum[:, g, :, :], sums[:, g, :, :]).then_inc(norm_step, 1)
                        dve.wait_ge(norm_step, g + 1)
                        dve.wait_ge(pv_done, 4 * g + 4)
                        dve.tensor_tensor(bigD[:, b * SC:(b + 1) * SC, h * HD:(h + 4) * HD].rearrange("p c (h d) -> p c h d", d=HD),
                                          bank[6 + g % 2][:, :].rearrange("p (c h d) -> p c h d", c=SC, h=4),
                                          rsum[:, g, :, :].unsqueeze(3).broadcast_to([P, SC, 4, HD]), ALU.mult).then_inc(norm_done, 1)

                    norm_step = bsem(f"{tag}_rsum")
                    for i in range(n_it + 5):
                        if i < n_it:
                            row_max(i)
                        if 0 <= i - 2 < n_it and not by_act(i - 2):
                            copy_out(i - 2)
                        if 0 <= i - 4 < n_it and (i - 4) % 4 == 3:
                            normalise((i - 4) // 4)

                @block.scalar
                def _(act):
                    for i in range(n_it + 2):
                        j = i - 2
                        if 0 <= j < n_it and by_act(j):
                            act.wait_ge(trans_done, j + 1)
                            if j >= 3:
                                act.wait_ge(pv_done, j - 2)
                            m = len(blocks)
                            act.activation(probT[:, j % 3, 0:m, :], bank[3 + j % 3][:, 0:m * P].rearrange("p (m c) -> p m c", m=m),
                                           ACT.Copy).then_inc(act_copy, 1)
                        if i < n_it:
                            act.wait_ge(max_done, 2 * i + 2)
                            if i >= 4:
                                act.wait_ge(trans_done, i - 3)
                            for qc in range(SC):
                                src = raw[:, i % 4, qc, 0:keys[qc]] if causal else bank[i % 3][:, qc * S:qc * S + keys[qc]]
                                act.activation(prob[:, i % 4, qc, 0:keys[qc]], src, ACT.Exp, bias=nmax[:, i, qc:qc + 1],
                                               accum_out=sums[:, i // 4, qc, i % 4:i % 4 + 1]).then_inc(exp_done, 1)

        def out_proj(tag, wo, bias=None):
            turned, act_out, dve_out, made, biased = (bsem(f"{tag}_turned"), bsem(f"{tag}_act_out"), bsem(f"{tag}_dve_out"),
                                                      bsem(f"{tag}_made"), bsem(f"{tag}_biased"))
            wo3 = v3(wo, NCH)
            with nc.Block(no_gpsimd_drain=True) as block:
                @block.tensor
                def _(pe):
                    for c in range(NCH + 1):
                        if c < NCH:
                            if c >= 4:
                                pe.wait_ge(act_out if c % 2 == 0 else dve_out, (c - 4) // 2 + 1)
                            for t in range(NT):
                                last = nc.tensor.transpose(bank[c % 4][:, t * P:(t + 1) * P], bigD[:, t, c * P:(c + 1) * P], ident)
                            last.then_inc(turned, 1)
                        if c >= 1:
                            k = c - 1
                            pe.wait_ge(act_out if k % 2 == 0 else dve_out, k // 2 + 1)
                            for t in range(NT):
                                last = nc.tensor.matmul(bank[4 + t][:, 0:P], bigA[:, k, t * P:(t + 1) * P], wo3[:, k, :],
                                                        start=k == 0, stop=k == NCH - 1)
                    last.then_inc(made, 1)

                @block.scalar
                def _(act):
                    for c in range(0, NCH, 2):
                        act.wait_ge(turned, c + 1)
                        act.activation(bigA[:, c, :], bank[c % 4][:, :], ACT.Copy).then_inc(act_out, 1)

                @block.vector
                def _(dve):
                    for c in range(1, NCH, 2):
                        dve.wait_ge(turned, c + 1)
                        dve.tensor_copy(bigA[:, c, :], bank[c % 4][:, :]).then_inc(dve_out, 1)
                    base = x_tok
                    if bias is not None:
                        dve.tensor_tensor(acc[:, :, :], x_tok[:, :, :],
                                          bias.unsqueeze(1).broadcast_to([P, NT, P]), ALU.add).then_inc(biased, 1)
                        dve.wait_ge(biased, 1)
                        base = acc[:, :, :]
                    else:
                        base = x_tok[:, :, :]
                    dve.wait_ge(made, 1)
                    for t in range(NT):
                        dve.tensor_tensor(r_tok[:, t, :], bank[4 + t][:, 0:P], base[:, t, :], ALU.add)

        skewed, flipped, mirrored = sem("l0b_skewed"), sem("l0b_flipped"), flat(bigC)

        def l0_bias():
            summed, padded, copied, stored_rpe = (sem("l0b_summed"), sem("l0b_padded"), sem("l0b_copied"), sem("l0b_stored"))
            rpe = v3(W("first", "rpe"), SC)
            tri = v3(W("const", "revtri"), SC)
            small = flat(bigA)
            ext = small[0:NH, 0:S + P]
            with nc.Block(no_gpsimd_drain=True) as block:
                @block.tensor
                def _(pe):
                    pe.wait_ge(loaded["first"], 16)
                    pe.wait_ge(loaded["const"], 16)
                    for c in range(SC):
                        last = nc.tensor.matmul(bank[0][0:NH, 0:S], rpe[:, c, :], tri[:, c, :], start=c == 0, stop=c == SC - 1)
                    last.then_inc(summed, 1)

                @block.vector
                def _(dve):
                    dve.memset(small[0:NH, S:S + P], PAD).then_inc(padded, 1)
                    dve.wait_ge(summed, 1)
                    dve.tensor_copy(small[0:NH, 0:S], bank[0][0:NH, 0:S]).then_inc(copied, 1)

                @block.sync
                def _(sp):
                    sp.wait_ge(padded, 1)
                    sp.wait_ge(copied, 1)
                    sp.dma_start(dram["rpe"][:, :], ext).then_inc(stored_rpe, 16)
                    sp.wait_ge(stored_rpe, 16)
                    src = bass.AP(tensor=dram["rpe"].tensor, offset=0, ap=[[1, P], [S + P, NH], [1, S]])
                    sp.dma_start(mirrored.rearrange("p (h s) -> p h s", h=NH), src).then_inc(skewed, 16)

        def l0_bias_table():
            with nc.Block(no_gpsimd_drain=True) as block:
                @block.tensor
                def _(pe):
                    pe.wait_ge(skewed, 16)
                    for c in range(8):
                        nc.tensor.matmul(bank[c][:, :], W("const", "flip"), mirrored[:, c * 512:(c + 1) * 512], start=True, stop=True)\
                          .then_inc(flipped, 1)

                @block.vector
                def _(dve):
                    for c in range(8):
                        dve.wait_ge(flipped, c + 1)
                        dve.tensor_copy(bias_t[:, :, :].rearrange("p h s -> p (h s)")[:, c * 512:(c + 1) * 512], bank[c][:, :])

        def expms():
            SQ = 6
            a_in, aT_in = W("gens", "a"), W("gens", "aT")
            nsl = 6 * P
            slot = [bigD[:, :, :].rearrange("p a b -> p (a b)")[:, k * nsl:(k + 1) * nsl].rearrange("p (s n) -> p s n", s=2)
                    for k in range(5)]
            A1, A2, A3, Q, E = slot
            A4 = probT[:, :, :, :].rearrange("p a m c -> p (a m c)")[:, 0:nsl].rearrange("p (s n) -> p s n", s=2)
            made = sem("exp_made")
            exp_half = sem("exp_half")
            used = sem("exp_used")
            pb = [bank[0], bank[1]]

            def view(s, m):
                return s[:, 0, m * P:(m + 1) * P], s[:, 1, m * P:(m + 1) * P]

            with nc.Block(no_gpsimd_drain=True) as block:
                rounds = [("A2", A1, A1), ("A3", A2, A1), ("A4", A2, A2), ("P", None, None)] + [("sq", E, E)] * SQ

                @block.tensor
                def _(pe):
                    n = 0
                    pe.wait_ge(used, 1)
                    for kind, X, Y in rounds:
                        if kind == "P":
                            X, Y = A4, Q
                        for m in range(3):
                            x, xt = view(X, m)
                            y, yt = view(Y, m)
                            nc.tensor.matmul(pb[0][:, m * P:(m + 1) * P], xt, y, start=True, stop=True)
                            last = nc.tensor.matmul(pb[1][:, m * P:(m + 1) * P], x, yt, start=True, stop=True)
                        last.then_inc(made, 1)
                        n += 1
                        pe.wait_ge(used, n + 1)
                    nc.tensor.matmul(bank[2][:, 0:P], view(E, 1)[1], view(E, 2)[0], start=True, stop=True).then_inc(made, 1)
                    pe.wait_ge(used, n + 2)
                    nc.tensor.matmul(bank[3][:, 0:P], view(E, 0)[1], A1[:, 0, 0:P], start=True, stop=True).then_inc(made, 1)

                @block.vector
                def _(dve):
                    step = Chain(dve, sem("exp_dve"))
                    idb = ident.unsqueeze(1).broadcast_to([P, 3, P])
                    t3 = lambda ap: ap.rearrange("p (m n) -> p m n", m=3)

                    dve.wait_ge(loaded["gens"], 16)
                    dve.wait_ge(loaded["const"], 16)
                    dve.tensor_scalar(A1[:, 0, :], a_in, 1.0 / 2 ** SQ, None, ALU.mult).then_inc(exp_half, 1)
                    dve.wait_ge(exp_half, 1)
                    dve.tensor_scalar(A1[:, 1, :], aT_in, 1.0 / 2 ** SQ, None, ALU.mult).then_inc(used, 1)
                    f = [1.0]
                    for k in range(1, 9):
                        f.append(f[-1] * k)
                    for n, (kind, _, _) in enumerate(rounds):
                        dve.wait_ge(made, n + 1)
                        if kind in ("A2", "A3", "A4"):
                            D = {"A2": A2, "A3": A3, "A4": A4}[kind]
                            step(dve.tensor_copy(D[:, 0, :], pb[0][:, 0:3 * P]))
                            if kind != "A4":
                                ins = dve.tensor_copy(D[:, 1, :], pb[1][:, 0:3 * P])
                                ins.then_inc(used, 1)
                                dve.wait_ge(used, n + 2)
                                continue
                            step(dve.tensor_copy(D[:, 1, :], pb[1][:, 0:3 * P]))
                            for s in range(2):
                                step(dve.tensor_scalar(t3(Q[:, s, :]), idb, 1.0 / f[4], None, ALU.mult))
                                for X, c in ((A1, 5), (A2, 6), (A3, 7), (A4, 8)):
                                    step(dve.scalar_tensor_tensor(out=Q[:, s, :], in0=X[:, s, :], scalar=1.0 / f[c], in1=Q[:, s, :],
                                                                  op0=ALU.mult, op1=ALU.add))
                                step(dve.tensor_tensor(t3(E[:, s, :]), t3(A1[:, s, :]), idb, ALU.add))
                                for X, c in ((A2, 2), (A3, 3)):
                                    step(dve.scalar_tensor_tensor(out=E[:, s, :], in0=X[:, s, :], scalar=1.0 / f[c], in1=E[:, s, :],
                                                                  op0=ALU.mult, op1=ALU.add))
                            dve.sem_inc(used, 1)
                        elif kind == "P":
                            step(dve.tensor_tensor(E[:, 0, :], pb[0][:, 0:3 * P], E[:, 0, :], ALU.add))
                            dve.tensor_tensor(E[:, 1, :], pb[1][:, 0:3 * P], E[:, 1, :], ALU.add).then_inc(used, 1)
                            dve.wait_ge(used, n + 2)
                        else:
                            step(dve.tensor_copy(E[:, 0, :], pb[0][:, 0:3 * P]))
                            dve.tensor_copy(E[:, 1, :], pb[1][:, 0:3 * P]).then_inc(used, 1)
                            dve.wait_ge(used, n + 2)
                    n = len(rounds)
                    dve.wait_ge(made, n + 1)
                    dve.tensor_copy(A1[:, 0, 0:P], bank[2][:, 0:P]).then_inc(used, 1)
                    dve.wait_ge(made, n + 2)
                    dve.tensor_copy(rot[:, :], bank[3][:, 0:P])


        def put_tokens(pool):
            for t in range(NT):
                pool.indirect_dma_start(dram["slots"], bass.IndirectOffsetOnAxis(ap=slot_now[:, t:t + 1], axis=0),
                                        to_put[:, t, :], None, bounds_check=ALL_T - 1, oob_is_err=False).then_inc(put, 16)

        def put_nothing():
            past, nowhere = sem("past"), sem("nowhere")
            with nc.Block(no_gpsimd_drain=True) as block:
                @block.vector
                def _(dve):
                    dve.memset(to_put[:, :, :], 0.0).then_inc(nowhere, 1)
                    dve.memset(slot_f[:, :], float(ALL_T)).then_inc(past, 1)
                    dve.wait_ge(past, 1)
                    dve.tensor_copy(slot_now[:, :], slot_f[:, :]).then_inc(nowhere, 1)

                @block.gpsimd
                def _(pool):
                    pool.wait_ge(nowhere, 2)
                    put_tokens(pool)

        def route0(group):
            n = NT * NE
            (lg, mx, ex, sm, eq, rk, best, hot, use, loc, pos, base, over, g_, wr) = [tiny[:, k, :] for k in range(15)]
            t3 = lambda ap: v3(ap, NT)
            col = lambda ap: t3(ap)[:, :, 0]

            def spread(ap):
                return col(ap).unsqueeze(2).broadcast_to([P, NT, NE])
            logits, shifted, exped, picked, counted = (bsem("r0_logits"), bsem("r0_shifted"), bsem("r0_exped"),
                                                       bsem("r0_picked"), bsem("r0_counted"))
            placed, kept, step_s = bsem("r0_placed"), bsem("r0_kept"), bsem("r0_step")
            upto, ones = W("const", "upto"), W("const", "ones")
            with nc.Block(no_gpsimd_drain=True) as block:
                @block.tensor
                def _(pe):
                    for t in range(NT):
                        last = nc.tensor.matmul(bank[0][:, t * NE:(t + 1) * NE], xT[:, t * P:(t + 1) * P], W("first", "wg"),
                                                start=True, stop=True)
                    last.then_inc(logits, 1)
                    pe.wait_ge(picked, 1)
                    nc.tensor.matmul(bank[1][:, 0:n], upto, hot, start=True, stop=False)
                    for u in range(1, NT):
                        nc.tensor.matmul(bank[1][:, u * NE:n], ones, hot[:, 0:n - u * NE], start=False, stop=u == NT - 1)
                    nc.tensor.matmul(bank[2][:, 0:n], ones, hot, start=True, stop=True).then_inc(counted, 1)

                @block.scalar
                def _(act):
                    act.wait_ge(shifted, 1)
                    act.activation(ex, lg, ACT.Exp).then_inc(exped, 1)

                @block.vector
                def _(dve):
                    step = Chain(dve, step_s)
                    dve.wait_ge(logits, 1)
                    step(dve.tensor_reduce(col(mx), t3(bank[0][:, 0:n]), op=ALU.max, axis=AX))
                    dve.tensor_tensor(t3(lg), t3(bank[0][:, 0:n]), spread(mx), ALU.subtract).then_inc(shifted, 1)
                    dve.wait_ge(exped, 1)
                    step(dve.tensor_reduce(col(sm), t3(ex), op=ALU.add, axis=AX))
                    step(dve.tensor_reduce(col(best), t3(ex), op=ALU.max, axis=AX))
                    step(dve.reciprocal(col(g_), col(sm)))
                    step(dve.tensor_tensor(gate0[:, bass.ts(group, NT)], col(g_), col(best), ALU.mult))
                    step(dve.tensor_tensor(t3(eq), t3(ex), spread(best), ALU.is_equal))
                    step(dve.tensor_tensor(t3(rk), t3(eq), W("const", "desc8").unsqueeze(1).broadcast_to([P, NT, NE]), ALU.mult))
                    step(dve.tensor_reduce(col(use), t3(rk), op=ALU.max, axis=AX))
                    dve.tensor_tensor(t3(hot), t3(rk), spread(use), ALU.is_equal).then_inc(picked, 1)
                    dve.wait_ge(counted, 1)
                    step(dve.tensor_tensor(t3(loc), t3(bank[1][:, 0:n]), taken[:, :].unsqueeze(1).broadcast_to([P, NT, NE]), ALU.add))
                    step(dve.tensor_reduce(eq[:, 0:NE], t3(bank[2][:, 0:n]).rearrange("p t e -> p e t"), op=ALU.add, axis=AX))
                    step(dve.tensor_tensor(taken[:, :], taken[:, :], eq[:, 0:NE], ALU.add))
                    step(dve.tensor_tensor(loc, loc, hot, ALU.mult))
                    step(dve.tensor_reduce(col(pos), t3(loc), op=ALU.add, axis=AX))
                    step(dve.tensor_tensor(t3(base), t3(hot), W("const", "slot0").unsqueeze(1).broadcast_to([P, NT, NE]), ALU.mult))
                    step(dve.tensor_reduce(col(use), t3(base), op=ALU.add, axis=AX))
                    step(dve.tensor_scalar(col(over), col(pos), float(CAP), None, ALU.is_gt))
                    step(dve.tensor_scalar(col(wr), col(pos), float(CAP), None, ALU.min))
                    step(dve.scalar_tensor_tensor(out=slot_f[:, :], in0=col(wr), scalar=-1.0, in1=col(use), op0=ALU.add, op1=ALU.add))
                    step(dve.tensor_copy(slot_r[:, bass.ts(group, NT)], slot_f[:, :]))
                    step(dve.scalar_tensor_tensor(out=col(wr), in0=col(over), scalar=float(ALL_T), in1=slot_f[:, :],
                                                  op0=ALU.mult, op1=ALU.add))
                    step(dve.tensor_scalar(col(over), col(over), -1.0, 1.0, ALU.mult, ALU.add))
                    dve.tensor_tensor(gate0[:, bass.ts(group, NT)], gate0[:, bass.ts(group, NT)], col(over), ALU.mult).then_inc(kept, 1)
                    dve.wait_ge(put, 16 * NT * (group + 1))
                    dve.tensor_copy(slot_now[:, :], col(wr)).then_inc(placed, 1)
                    dve.tensor_copy(to_put[:, :, :], x_tok[:, :, :]).then_inc(placed, 1)
                    dve.tensor_copy(x_all[:, bass.ts(group, NT), :], x_tok[:, :, :])

                @block.gpsimd
                def _(pool):
                    pool.wait_ge(placed, 2)
                    put_tokens(pool)

        def all_put():
            with nc.Block(no_gpsimd_drain=True) as block:
                @block.sync
                def _(sp):
                    sp.wait_ge(put, 16 * NT * (GROUPS + 1))

        slot_now = sb("slot_now", [P, NT], U32)
        to_put = sb("to_put", [P, NT, P])

        def experts0(e, par):
            tg = f"e{par}"
            cols = packs["l0f"].shape[1]
            wbuf = [flat(bigA), flat(bigB)][par][:, 0:cols]
            hb = [bigC, bigD][par]
            d_tok = hb[:, 0, 0:512].rearrange("p (t d) -> p t d", t=NT)
            dT = hb[:, 0, 512:1024]
            h = [hb[:, 1, 0:512], hb[:, 1, 512:1024], hb[:, 2, 0:512], hb[:, 2, 512:1024]]
            eo = hb[:, 3, 0:512].rearrange("p (t d) -> p t d", t=NT)
            w1 = wbuf[:, 0:512]
            w2 = v3(wbuf[:, 512:1024], 4)
            b1 = wbuf[:, 1024:1028]
            b2 = wbuf[:, 1028:1028 + P]
            bk = bank[4 * par:4 * par + 4]
            return dict(w=wbuf, d_tok=d_tok, dT=dT, h=h, eo=eo, w1=w1, w2=w2, b1=b1, b2=b2, bk=bk, e=e,
                        got=bsem(f"{tg}_got"), gotw=bsem(f"{tg}_gotw"), turned=bsem(f"{tg}_turned"), dT_done=bsem(f"{tg}_dT"),
                        up=bsem(f"{tg}_up"), relu=bsem(f"{tg}_relu"), down=bsem(f"{tg}_down"), eo_done=bsem(f"{tg}_eo"),
                        stored=bsem(f"{tg}_stored"))

        def load_early():
            with nc.Block(no_gpsimd_drain=True) as block:
                @block.sync
                def _(sp):
                    for pk in early:
                        sp.dma_start(held[pk], packs[pk]).then_inc(loaded[pk], 16)

        def expert_pair(first):
            two = [experts0(first, 0), experts0(first + 1, 1)]
            pack_e = packs["l0f"].rearrange("(e p) n -> p e n", p=P)
            slots_e = dram["slots"].rearrange("(e t p) d -> p e t d", p=P, t=CAP // P)
            res_e = dram["results"].rearrange("(e t p) d -> p e t d", p=P, t=CAP // P)
            with nc.Block(no_gpsimd_drain=True) as block:
                @block.sync
                def _(sp):
                    for q in two:
                        sp.dma_start(q["w"].unsqueeze(1), pack_e[:, group_slice(q["e"]), :]).then_inc(q["gotw"], 16)
                        sp.dma_start(q["d_tok"].unsqueeze(1), slots_e[:, group_slice(q["e"]), :, :]).then_inc(q["got"], 16)
                    for q in two:
                        sp.wait_ge(q["eo_done"], 1)
                        sp.dma_start(res_e[:, group_slice(q["e"]), :, :], q["eo"].unsqueeze(1)).then_inc(q["stored"], 16)
                    for q in two:
                        sp.wait_ge(q["stored"], 16)

                @block.tensor
                def _(pe):
                    for q in two:
                        pe.wait_ge(q["got"], 16)
                        for t in range(NT):
                            last = nc.tensor.transpose(q["bk"][0][:, t * P:(t + 1) * P], q["d_tok"][:, t, :], ident)
                        last.then_inc(q["turned"], 1)
                    for q in two:
                        pe.wait_ge(q["gotw"], 16)
                        pe.wait_ge(q["dT_done"], 1)
                        for c in range(4):
                            nc.tensor.matmul(q["bk"][c][:, :], q["w1"][:, c * P:(c + 1) * P], q["dT"], start=True, stop=True)\
                              .then_inc(q["up"], 1)
                    for q in two:
                        pe.wait_ge(q["relu"], 4)
                        for t in range(NT):
                            for c in range(4):
                                last = nc.tensor.matmul(q["bk"][0][:, t * P:(t + 1) * P], q["h"][c][:, t * P:(t + 1) * P],
                                                        q["w2"][:, c, :], start=c == 0, stop=c == 3)
                        last.then_inc(q["down"], 1)

                @block.scalar
                def _(act):
                    for q in two:
                        for c in range(4):
                            act.wait_ge(q["up"], c + 1)
                            act.activation(q["h"][c], q["bk"][c][:, :], ACT.Relu, bias=q["b1"][:, c:c + 1]).then_inc(q["relu"], 1)

                @block.vector
                def _(dve):
                    for q in two:
                        dve.wait_ge(q["turned"], 1)
                        dve.tensor_copy(q["dT"], q["bk"][0][:, :]).then_inc(q["dT_done"], 1)
                    for q in two:
                        dve.wait_ge(q["down"], 1)
                        dve.tensor_tensor(q["eo"], v3(q["bk"][0][:, :], NT), q["b2"].unsqueeze(1).broadcast_to([P, NT, P]),
                                          ALU.add).then_inc(q["eo_done"], 1)

        fetching = to_put

        def fetch(pool):
            for t in range(NT):
                pool.indirect_dma_start(fetching[:, t, :], None, dram["results"],
                                        bass.IndirectOffsetOnAxis(ap=slot_now[:, t:t + 1], axis=0),
                                        bounds_check=ALL_T - 1, oob_is_err=False).then_inc(fetched, 16)

        def fetch_first():
            ready0 = sem("ready0")
            with nc.Block(no_gpsimd_drain=True) as block:
                @block.vector
                def _(dve):
                    dve.memset(slot_r[:, GROUPS * NT:(GROUPS + 1) * NT], 0)
                    dve.tensor_copy(slot_now[:, :], slot_r[:, 0:NT]).then_inc(ready0, 1)

                @block.gpsimd
                def _(pool):
                    pool.wait_ge(ready0, 1)
                    fetch(pool)

        def combine0(group):
            scaled, ready = bsem("c0_scaled"), bsem("c0_ready")
            res = bigD[:, 0, 0:512].rearrange("p (t d) -> p t d", t=NT)
            with nc.Block(no_gpsimd_drain=True) as block:
                @block.vector
                def _(dve):
                    dve.wait_ge(fetched, 16 * NT * (group + 1))
                    dve.tensor_tensor(res, fetching[:, :, :], gate0[:, bass.ts(group, NT)].unsqueeze(2).broadcast_to([P, NT, P]), ALU.mult)\
                       .then_inc(scaled, 1)
                    dve.tensor_copy(slot_now[:, :], slot_r[:, bass.ts(group + 1, NT)]).then_inc(ready, 1)
                    dve.wait_ge(scaled, 1)
                    dve.tensor_tensor(r_tok[:, :, :], res, x_all[:, bass.ts(group, NT), :], ALU.add)

                @block.gpsimd
                def _(pool):
                    pool.wait_ge(scaled, 1)
                    pool.wait_ge(ready, 1)
                    fetch(pool)

        def l0_attention():
            q3, k3, wv = W("l0a", "wq"), W("l0a", "wk"), W("l0a", "wv")
            items = []
            for c in range(NCH):
                items.append((q3[:, c * P:(c + 1) * P], xT[:, :], bigA[:, c, :], HD ** -0.5))
                items.append((k3[:, c * P:(c + 1) * P], xT[:, :], (keys_even[0:HD, c, :], keys_odd[HD:P, c, :]), 1.0))
            for t in range(NT):
                for h in range(2):
                    items.append((xT[:, t * P:(t + 1) * P], wv[:, h * 512:(h + 1) * 512], bigC[:, t, h * 512:(h + 1) * 512], 1.0))
            project("l0p", items, [])
            heads("l0h", lambda h: (keys_even, keys_odd)[h % 2][:, h // 2, :], lambda h: h * HD, True)
            out_proj("l0o", W("l0a", "wo"))

        def fold_lora():
            lw = where["lora"]
            n1 = lw["kA"][0]
            a0, b0 = flat(bigC)[0:8, :], flat(bigD)[0:8, :]
            got, made, added = sem("lora_got"), sem("lora_made"), sem("lora_added")

            def F(part):
                a, b = lw[part]
                return a0[:, a:b] if b <= n1 else b0[:, a - n1:b - n1]
            jobs = []
            for nm, cols in (("q", NH * HD), ("k", 512)):
                for tg in ("", "s"):
                    for c in range(0, cols, 512):
                        jobs.append([(F(f"{nm}A"), F(f"{nm}B{tg}")[:, c:c + 512], 0, 512, W("l1a", f"w{nm}{tg}")[:, c:c + 512])])
            jobs.append([(F("vA"), F("vB"), 0, 256, W("l1a", "wv"))])
            for half_ in range(2):
                jobs.append([(F("oA")[:, (4 * half_ + c) * P:(4 * half_ + c + 1) * P], F("oB"), c * P, P,
                              W("l1a", "wo")[:, (4 * half_) * P:(4 * half_ + 4) * P]) for c in range(4)])
            with nc.Block(no_gpsimd_drain=True) as block:
                @block.sync
                def _(sp):
                    sp.dma_start(a0[:, 0:n1], packs["lora"][:, 0:n1]).then_inc(got, 16)
                    sp.dma_start(b0[:, 0:lora_cols - n1], packs["lora"][:, n1:lora_cols]).then_inc(got, 16)
                    sp.dma_start(held["l3a"], packs["l3a"]).then_inc(loaded["l3a"], 16)

                @block.tensor
                def _(pe):
                    pe.wait_ge(got, 32)
                    for i, job in enumerate(jobs):
                        if i >= 8:
                            pe.wait_ge(added, i - 7)
                        for (l, r, at, nn, d) in job:
                            last = nc.tensor.matmul(bank[i % 8][:, at:at + nn], l, r, start=True, stop=True)
                        last.then_inc(made, 1)

                @block.vector
                def _(dve):
                    dve.wait_ge(loaded["l1a"], 16)
                    for i, job in enumerate(jobs):
                        dve.wait_ge(made, i + 1)
                        d = job[0][4]
                        nn = d.shape[1]
                        dve.scalar_tensor_tensor(out=d, in0=bank[i % 8][:, 0:nn], scalar=2.0, in1=d, op0=ALU.mult, op1=ALU.add)\
                           .then_inc(added, 1)
                    for pk in ("l1f", "l3a", "eb2", "be2"):
                        dve.wait_ge(loaded[pk], 16)

        def zero_beside_keys1():
            keys2 = bigB[:, :, :].rearrange("p (c two) t -> p c two t", two=2)
            with nc.Block(no_gpsimd_drain=True) as block:
                @block.vector
                def _(dve):
                    dve.memset(keys2[HD:P, :, 0, :], 0.0)
                    dve.memset(keys2[0:HD, :, 1, :], 0.0)

        def l1_project(group):
            jobs = [("k", c) for c in range(4)] + [("q", c) for c in range(NCH)]
            made, mixed, out_done = bsem("l1p_made"), bsem("l1p_mixed"), bsem("l1p_out")
            v_made, half_done = bsem("l1p_v"), bsem("l1p_half")
            cos, sin = W("const", "rope_cos"), W("const", "rope_sin")
            t1 = [bigD[:, k, 0:512] for k in range(4)]
            t2 = [bigD[:, k, 512:1024] for k in range(4)]
            with nc.Block(no_gpsimd_drain=True) as block:
                @block.tensor
                def _(pe):
                    for i, (nm, c) in enumerate(jobs):
                        if i >= 3:
                            pe.wait_ge(mixed, 2 * (i - 2))
                        for s_, tg in enumerate(("", "s")):
                            last = nc.tensor.matmul(bank[2 * (i % 3) + s_][:, :], W("l1a", f"w{nm}{tg}")[:, c * P:(c + 1) * P], xT[:, :],
                                                    start=True, stop=True)
                        last.then_inc(made, 1)
                    for t in range(NT):
                        last = nc.tensor.matmul(bank[6 + t // 2][:, (t % 2) * 256:(t % 2) * 256 + 256], xT[:, t * P:(t + 1) * P],
                                                W("l1a", "wv"), start=True, stop=True)
                    last.then_inc(v_made, 1)

                @block.vector
                def _(dve):
                    for i, (nm, c) in enumerate(jobs):
                        s_ = HD ** -0.5 if nm == "q" else 1.0
                        dve.wait_ge(made, i + 1)
                        if i >= 4:
                            dve.wait_ge(out_done, i - 3)
                        b0, b1 = bank[2 * (i % 3)], bank[2 * (i % 3) + 1]
                        dve.scalar_tensor_tensor(out=t1[i % 4], in0=b0[:, :], scalar=s_, in1=cos, op0=ALU.mult, op1=ALU.mult)\
                           .then_inc(mixed, 1)
                        dve.scalar_tensor_tensor(out=t2[i % 4], in0=b1[:, :], scalar=s_, in1=sin, op0=ALU.mult, op1=ALU.mult)\
                           .then_inc(mixed, 1)

                @block.gpsimd
                def _(pool):
                    pool.wait_ge(fetched, 16 * NT * (group + 2))
                    step = Chain(pool, half_done)
                    for i, (nm, c) in enumerate(jobs):
                        pool.wait_ge(mixed, 2 * i + 2)
                        if nm == "q":
                            pool.tensor_tensor(bigA[:, c, :], t1[i % 4], t2[i % 4], ALU.add).then_inc(out_done, 1)
                            pool.wait_ge(out_done, i + 1)
                        else:
                            step(pool.tensor_tensor(bigB[0:HD, 2 * c, :], t1[i % 4][0:HD, :], t2[i % 4][0:HD, :], ALU.add))
                            pool.tensor_tensor(bigB[HD:P, 2 * c + 1, :], t1[i % 4][HD:P, :], t2[i % 4][HD:P, :], ALU.add)\
                                .then_inc(out_done, 1)
                            pool.wait_ge(out_done, i + 1)

                @block.scalar
                def _(act):
                    act.wait_ge(v_made, 1)
                    for k in range(2):
                        act.activation(bigC[:, 2 * k:2 * k + 2, 0:256], v3(bank[6 + k][:, :], 2), ACT.Copy)

        def pre_norm(tag, gamma, beta, centred, dst, y):
            st, mean, var, rs, xn, tr, half_done = (bsem(f"{tag}_st"), bsem(f"{tag}_mean"), bsem(f"{tag}_var"), bsem(f"{tag}_rs"),
                                                    bsem(f"{tag}_xn"), bsem(f"{tag}_tr"), bsem(f"{tag}_half"))
            y = v3(y, NT)
            with nc.Block(no_gpsimd_drain=True) as block:
                @block.vector
                def _(dve):
                    step = Chain(dve, rs)
                    if centred:
                        for t in range(NT):
                            dve.bn_stats(stats[:, t, :], x_tok[:, t, :]).then_inc(st, 1)
                        for t in range(NT):
                            dve.wait_ge(st, t + 1)
                            dve.bn_aggr(mv[:, t, :], stats[:, t, :]).then_inc(mean, 1)
                        dve.wait_ge(mean, NT)
                        step(dve.tensor_scalar(var_e[:, 0:NT], mv[:, 0:NT, 1], LN_EPS, None, ALU.add))
                    else:
                        dve.tensor_tensor(y, x_tok[:, :, :], x_tok[:, :, :], ALU.mult).then_inc(st, 1)
                        dve.wait_ge(st, 1)
                        dve.tensor_reduce(var_e[:, 0:NT], y, op=ALU.add, axis=AX).then_inc(mean, 1)
                        dve.wait_ge(mean, 1)
                        dve.tensor_scalar(var_e[:, 0:NT], var_e[:, 0:NT], 1.0 / P, RMS_EPS, ALU.mult, ALU.add).then_inc(var, 1)
                        dve.wait_ge(var, 1)
                    rsqrt(dve, step, var_e[:, 0:NT], rstd[:, 0:NT], newton[:, 0:NT])
                    for t in range(NT):
                        if centred:
                            dve.tensor_scalar(y[:, t, :], x_tok[:, t, :], mv[:, t, 0:1], rstd[:, t:t + 1],
                                              ALU.subtract, ALU.mult).then_inc(xn, 1)
                        else:
                            dve.tensor_scalar(y[:, t, :], x_tok[:, t, :], rstd[:, t:t + 1], None, ALU.mult).then_inc(xn, 1)
                    dve.wait_ge(tr, NT)
                    if beta is None:
                        dve.tensor_scalar(dst, bank[0][:, :], gamma, None, ALU.mult)
                    else:
                        dve.tensor_scalar(dst, bank[0][:, :], gamma, beta, ALU.mult, ALU.add)

                @block.tensor
                def _(pe):
                    for t in range(NT):
                        pe.wait_ge(xn, t + 1)
                        nc.tensor.transpose(bank[0][:, t * P:(t + 1) * P], y[:, t, :], ident).then_inc(tr, 1)

        def top2(dve, step, lg, n_exp):
            mxs, ixf, h1, h2 = [v3(tiny[:, k, :], NT) for k in (20, 21, 22, 23)]
            for t in range(NT):
                step(dve.max(mxs[:, t, :], lg[:, t, :]))
                step(dve.max_index(ix8[:, t, :], mxs[:, t, :], lg[:, t, :]))
            step(dve.tensor_copy(ixf, ix8[:, :, :]))
            iota = W("const", "iota8").unsqueeze(1).broadcast_to([P, NT, 8])
            for k, h in ((0, h1), (1, h2)):
                step(dve.tensor_tensor(h, iota, ixf[:, :, k].unsqueeze(2).broadcast_to([P, NT, 8]), ALU.is_equal))
            return mxs, h1, h2

        def token_value(k):
            return tiny[:, k, 0:NT]

        def over8(ap):
            return ap.unsqueeze(2).broadcast_to([P, NT, 8])

        def softmax_of_two(dve, act_sems, step, mxs, h1, h2, wd, e_t, r_t, d_t):
            shifted, exped = act_sems
            dve.tensor_tensor(d_t, mxs[:, :, 1], mxs[:, :, 0], ALU.subtract).then_inc(shifted, 1)
            dve.wait_ge(exped, 1)
            step(dve.tensor_scalar(r_t, e_t, 1.0, None, ALU.add))
            step(dve.reciprocal(r_t, r_t))
            step(dve.tensor_tensor(e_t, e_t, r_t, ALU.mult))
            step(dve.tensor_tensor(h1, h1, over8(r_t), ALU.mult))
            step(dve.tensor_tensor(h2, h2, over8(e_t), ALU.mult))
            step(dve.tensor_tensor(wd, h1, h2, ALU.add))

        weights_of = v3(tiny[:, 19, :], NT)
        weightsT = sb("weightsT", [8, T])
        acc = sb("acc", [P, NT, P])
        other = sb("other", [P, NT, P])

        def l1_route():
            xnT = bigC[:, 0, 0:512]
            made, shifted, exped, weighed, wt, abel_made, step_s = (bsem("l1r_made"), bsem("l1r_shifted"), bsem("l1r_exped"),
                                                                    bsem("l1r_weighed"), bsem("l1r_wt"), bsem("l1r_abel"), bsem("l1r_step"))
            biased = bsem("l1r_biased")
            lg = v3(tiny[:, 0, :], NT)
            e_t, r_t, d_t = token_value(1), token_value(2), token_value(3)
            with nc.Block(no_gpsimd_drain=True) as block:
                @block.tensor
                def _(pe):
                    for t in range(NT):
                        last = nc.tensor.matmul(bank[0][:, t * NE:(t + 1) * NE], xnT[:, t * P:(t + 1) * P], W("l1f", "gate_w"),
                                                start=True, stop=True)
                    last.then_inc(made, 1)
                    for t in range(NT):
                        last = nc.tensor.matmul(bank[1][:, t * P:(t + 1) * P], xnT[:, t * P:(t + 1) * P], W("l1f", "abel_w"),
                                                start=True, stop=True)
                    last.then_inc(abel_made, 1)
                    pe.wait_ge(weighed, 1)
                    for t in range(NT):
                        last = nc.tensor.transpose(bank[2][0:8, t * P:(t + 1) * P], weights_of[:, t, :], ident)
                    last.then_inc(wt, 1)

                @block.scalar
                def _(act):
                    act.wait_ge(shifted, 1)
                    act.activation(e_t, d_t, ACT.Exp).then_inc(exped, 1)
                    act.wait_ge(biased, 1)
                    act.activation(other[:, :, :], r_tok[:, :, :], ACT.Gelu)
                    act.wait_ge(wt, 1)
                    act.activation(weightsT[:, :], bank[2][0:8, :], ACT.Copy)

                @block.vector
                def _(dve):
                    step = Chain(dve, step_s)
                    dve.wait_ge(made, 1)
                    step(dve.tensor_tensor(lg, v3(bank[0][:, 0:NT * NE], NT), W("l1f", "gate_b").unsqueeze(1).broadcast_to([P, NT, NE]), ALU.add))
                    mxs, h1, h2 = top2(dve, step, lg, NE)
                    softmax_of_two(dve, (shifted, exped), step, mxs, h1, h2, weights_of, e_t, r_t, d_t)
                    dve.sem_inc(weighed, 1)
                    dve.wait_ge(abel_made, 1)
                    dve.tensor_tensor(r_tok[:, :, :], v3(bank[1][:, :], NT), W("l1f", "abel_b").unsqueeze(1).broadcast_to([P, NT, P]), ALU.add)\
                       .then_inc(biased, 1)

        def l1_experts():
            xnT = bigC[:, 0, 0:512]
            up, act_done, down, added, step_s, b_made = (bsem("l1e_up"), bsem("l1e_act"), bsem("l1e_down"), bsem("l1e_added"),
                                                         bsem("l1e_step"), bsem("l1e_bias"))
            ew1 = W("l1f", "ew1")
            ew2 = W("l1f", "ew2").rearrange("p (e c d) -> p e c d", e=NE, c=2)
            hb = [bigA[:, k, :] for k in range(4)]
            with nc.Block(no_gpsimd_drain=True) as block:
                @block.tensor
                def _(pe):
                    for t in range(NT):
                        last = nc.tensor.matmul(bank[6][:, t * P:(t + 1) * P], weightsT[:, t * P:(t + 1) * P], held["eb2"],
                                                start=True, stop=True)
                    last.then_inc(b_made, 1)
                    for e in range(NE + 1):
                        if e < NE:
                            for c in range(2):
                                n = 2 * e + c
                                if n >= 4:
                                    pe.wait_ge(act_done, n - 3)
                                nc.tensor.matmul(bank[n % 4][:, :], ew1[:, n * P:(n + 1) * P], xnT, start=True, stop=True).then_inc(up, 1)
                        if e >= 1:
                            f = e - 1
                            pe.wait_ge(act_done, 2 * f + 2)
                            if f >= 2:
                                pe.wait_ge(added, f - 1)
                            for t in range(NT):
                                for c in range(2):
                                    last = nc.tensor.matmul(bank[4 + f % 2][:, t * P:(t + 1) * P], hb[(2 * f + c) % 4][:, t * P:(t + 1) * P],
                                                            ew2[:, f, c, :], start=c == 0, stop=c == 1)
                            last.then_inc(down, 1)

                @block.scalar
                def _(act):
                    for n in range(2 * NE):
                        act.wait_ge(up, n + 1)
                        if n >= 4:
                            act.wait_ge(down, (n - 4) // 2 + 1)
                        act.activation(hb[n % 4], bank[n % 4][:, :], ACT.Gelu, bias=W("l1f", "eb1")[:, n:n + 1]).then_inc(act_done, 1)

                @block.vector
                def _(dve):
                    step = Chain(dve, step_s)
                    dve.wait_ge(b_made, 1)
                    step(dve.tensor_copy(acc[:, :, :], v3(bank[6][:, :], NT)))
                    for e in range(NE):
                        dve.wait_ge(down, e + 1)
                        for t in range(NT):
                            last = dve.scalar_tensor_tensor(out=acc[:, t, :], in0=bank[4 + e % 2][:, t * P:(t + 1) * P],
                                                            scalar=weights_of[:, t, e:e + 1], in1=acc[:, t, :], op0=ALU.mult, op1=ALU.add)
                            last.then_inc(step_s, 1)
                        dve.wait_ge(step_s, 1 + NT * (e + 1))
                        dve.sem_inc(added, 1)

        def l1_mix():
            turned, copied, made, summed, exped, step_s = (bsem("l1m_turned"), bsem("l1m_copied"), bsem("l1m_made"),
                                                           bsem("l1m_summed"), bsem("l1m_exped"), bsem("l1m_step"))
            accT = bigA[:, 0, :]
            p1 = bigA[:, 1, :].rearrange("p (t d) -> p t d", t=NT)
            p2 = bigA[:, 2, :].rearrange("p (t d) -> p t d", t=NT)
            z1, z2, g_ = token_value(1), token_value(2), token_value(3)
            gc = W("l1f", "gc_w")
            moe = v3(bank[1][:, :], NT)
            with nc.Block(no_gpsimd_drain=True) as block:
                @block.tensor
                def _(pe):
                    for t in range(NT):
                        last = nc.tensor.transpose(bank[0][:, t * P:(t + 1) * P], acc[:, t, :], ident)
                    last.then_inc(turned, 1)
                    pe.wait_ge(copied, 1)
                    for t in range(NT):
                        last = nc.tensor.matmul(bank[1][:, t * P:(t + 1) * P], accT[:, t * P:(t + 1) * P], rot[:, :], start=True, stop=True)
                    last.then_inc(made, 1)

                @block.scalar
                def _(act):
                    act.wait_ge(turned, 1)
                    act.activation(accT, bank[0][:, :], ACT.Copy).then_inc(copied, 1)
                    act.wait_ge(summed, 1)
                    act.activation(g_, z1, ACT.Exp, scale=-1.0).then_inc(exped, 1)

                @block.vector
                def _(dve):
                    step = Chain(dve, step_s)
                    step(dve.tensor_tensor(p1, other[:, :, :], gc[:, 0:P].unsqueeze(1).broadcast_to([P, NT, P]), ALU.mult))
                    step(dve.tensor_reduce(z1, p1, op=ALU.add, axis=AX))
                    dve.wait_ge(made, 1)
                    step(dve.tensor_tensor(p2, moe, gc[:, P:2 * P].unsqueeze(1).broadcast_to([P, NT, P]), ALU.mult))
                    step(dve.tensor_reduce(z2, p2, op=ALU.add, axis=AX))
                    step(dve.scalar_tensor_tensor(out=z1, in0=z1, scalar=W("l1f", "gc_b"), in1=z2, op0=ALU.add, op1=ALU.add))
                    dve.sem_inc(summed, 1)
                    step(dve.scalar_tensor_tensor(out=r_tok[:, :, :], in0=x_tok[:, :, :], scalar=2.0, in1=other[:, :, :],
                                                  op0=ALU.mult, op1=ALU.add))
                    step(dve.tensor_tensor(p1, moe, other[:, :, :], ALU.subtract))
                    dve.wait_ge(exped, 1)
                    step(dve.tensor_scalar(g_, g_, 1.0, None, ALU.add))
                    step(dve.reciprocal(g_, g_))
                    for t in range(NT):
                        dve.scalar_tensor_tensor(out=r_tok[:, t, :], in0=p1[:, t, :], scalar=g_[:, t:t + 1], in1=r_tok[:, t, :],
                                                 op0=ALU.mult, op1=ALU.add)

        def narrow(tag, wq, wkv, wo, latent, window):
            KV, D8, G4 = 4, 8, 4
            xnT = bigB[:, 0, :]
            cosq, sinq = v3(W("const", f"{tag[0]}_cos"), NT), v3(W("const", f"{tag[0]}_sin"), NT)
            qr = bigB[:, 2, :].rearrange("p (t h d) -> p t h d", t=NT, h=16)
            sq = bigB[:, 3, :].rearrange("p (a d) -> p a d", d=8)
            ta, tb = bigB[:, 4, 0:256], bigB[:, 4, 256:512]
            kr = bigB[:, 5, 0:128].rearrange("p (t h d) -> p t h d", t=NT, h=KV)
            sk = bigB[:, 5, 128:256].rearrange("p (a d) -> p a d", d=8)
            latT = bigB[0:32, 6, :]
            aoT = bigB[:, 7, :]
            qpad = flat(bigA)[:, 0:2048].rearrange("p (t a g d) -> p t a g d", t=NT, a=G4, g=KV)
            kpad = flat(bigA)[:, 2048:2560].rearrange("p (t g d) -> p t g d", t=NT, g=KV)
            vx = flat(bigA)[:, 2560:2560 + NT * KV * 32].rearrange("p (t g d) -> p t g d", t=NT, g=KV)
            ao = bigB[:, 2, :].rearrange("p (t h d) -> p t h d", t=NT, h=16)
            qT = flat(bigC)[:, 0:2048].rearrange("p (t a q) -> p t a q", t=NT, a=G4)
            kz = flat(bigC)[:, 2048:4096].rearrange("p (g t k) -> p g t k", g=KV, t=NT)
            pr = [bigD[:, k, 0:512] for k in range(4)]
            few = flat(bigA)[:, 3072:4096]
            ss2, r2 = few[:, 0:80], few[:, 80:160]
            rq, rk_ = r2[:, 0:64], r2[:, 64:80]
            rec = few[:, 256:320].rearrange("p (t h) -> p t h", t=NT)
            pads, q_made, kv_made, lat_made, lat_done = [bsem(f"{tag}_{n}") for n in ("pads", "q", "kv", "lat", "latd")]
            padded, tq, tk = [bsem(f"{tag}_{n}") for n in ("padded", "tq", "tk")]
            step_s = bsem(f"{tag}_step")
            with nc.Block(no_gpsimd_drain=True) as block:
                @block.gpsimd
                def _(pool):
                    pool.memset(flat(bigA)[:, 0:2560], 0.0).then_inc(pads, 1)
                    pool.memset(vx, 1.0).then_inc(pads, 1)

                @block.tensor
                def _(pe):
                    for t in range(NT):
                        last = nc.tensor.matmul(bank[0][:, t * P:(t + 1) * P], xnT[:, t * P:(t + 1) * P], wq, start=True, stop=True)
                    last.then_inc(q_made, 1)
                    if latent is not None:
                        nc.tensor.matmul(bank[1][0:32, :], latent, xnT, start=True, stop=True).then_inc(lat_made, 1)
                        pe.wait_ge(lat_done, 1)
                    for t in range(NT):
                        l = latT[:, t * P:(t + 1) * P] if latent is not None else xnT[:, t * P:(t + 1) * P]
                        last = nc.tensor.matmul(bank[2][:, t * 64:(t + 1) * 64], l, wkv, start=True, stop=True)
                    last.then_inc(kv_made, 1)
                    pe.wait_ge(padded, 1)
                    for t in range(NT):
                        for a in range(G4):
                            last = nc.tensor.transpose(bank[4 + t][:, a * P:(a + 1) * P], qpad[:, t, a, :, :].rearrange("p g d -> p (g d)"), ident)
                        last.then_inc(tq, 1)
                    for t in range(NT):
                        last = nc.tensor.transpose(bank[3][:, t * P:(t + 1) * P], kpad[:, t, :, :].rearrange("p g d -> p (g d)"), ident)
                    last.then_inc(tk, 1)

                @block.scalar
                def _(act):
                    if latent is not None:
                        act.wait_ge(lat_made, 1)
                        act.activation(latT, bank[1][0:32, :], ACT.Copy).then_inc(lat_done, 1)
                    for t in range(NT):
                        act.wait_ge(tq, t + 1)
                        act.activation(qT[:, t, :, :], v3(bank[4 + t][:, :], G4), ACT.Copy)
                    act.wait_ge(tk, 1)
                    for g in range(KV):
                        act.activation(kz[:, g, :, :], v3(bank[3][:, :], NT), ACT.Copy, scale=W("const", "rows32")[:, g:g + 1])

                @block.vector
                def _(dve):
                    step = Chain(dve, step_s)

                    def rotate(src, dst, nh):
                        e, o = [src.rearrange("p t (h i e) -> p t h i e", i=4, e=2)[:, :, :, :, k] for k in (0, 1)]
                        c = cosq.unsqueeze(2).broadcast_to([P, NT, nh, 4])
                        s_ = sinq.unsqueeze(2).broadcast_to([P, NT, nh, 4])
                        A = ta[:, 0:NT * nh * 4].rearrange("p (t h i) -> p t h i", t=NT, h=nh)
                        Bv = tb[:, 0:NT * nh * 4].rearrange("p (t h i) -> p t h i", t=NT, h=nh)
                        step(dve.tensor_tensor(A, e, c, ALU.mult))
                        step(dve.tensor_tensor(Bv, o, s_, ALU.mult))
                        step(dve.tensor_tensor(dst[:, :, :, 0:4], A, Bv, ALU.subtract))
                        step(dve.tensor_tensor(A, e, s_, ALU.mult))
                        step(dve.tensor_tensor(Bv, o, c, ALU.mult))
                        step(dve.tensor_tensor(dst[:, :, :, 4:8], A, Bv, ALU.add))
                    dve.wait_ge(q_made, 1)
                    rotate(v3(bank[0][:, :], NT), qr, 16)
                    qf = qr.rearrange("p t h d -> p (t h) d")
                    step(dve.tensor_tensor(sq, qf, qf, ALU.mult))
                    step(dve.tensor_reduce(ss2[:, 0:64], sq, op=ALU.add, axis=AX))
                    dve.wait_ge(kv_made, 1)
                    rotate(v3(bank[2][:, 0:256], NT)[:, :, 0:32], kr, KV)
                    kf = kr.rearrange("p t h d -> p (t h) d")
                    step(dve.tensor_tensor(sk, kf, kf, ALU.mult))
                    step(dve.tensor_reduce(ss2[:, 64:80], sk, op=ALU.add, axis=AX))
                    step(dve.tensor_scalar(ss2, ss2, 1.0 / D8, RMS_EPS, ALU.mult, ALU.add))
                    rsqrt(dve, step, ss2, r2, newton[:, 0:80])
                    dve.wait_ge(pads, 2)
                    r4 = rq.rearrange("p (t g a) -> p t g a", t=NT, g=KV)
                    for t in range(NT):
                        step(dve.tensor_tensor(qpad[:, t, :, :, 0:8].rearrange("p a g d -> p g a d"),
                                               qr[:, t, :, :].rearrange("p (g a) d -> p g a d", g=KV),
                                               r4[:, t, :, :].unsqueeze(3).broadcast_to([P, KV, G4, D8]), ALU.mult))
                    dve.tensor_tensor(kpad[:, :, :, 0:8], kr, rk_.rearrange("p (t g) -> p t g", t=NT).unsqueeze(3).broadcast_to([P, NT, KV, D8]),
                                      ALU.mult).then_inc(padded, 1)
                    dve.tensor_copy(vx[:, :, :, 0:8], v3(bank[2][:, 0:256], NT)[:, :, 32:64].rearrange("p t (g d) -> p t g d", d=8))

            jobs = [(b, qc, g) for b in range(B) for qc in range(SC) for g in range(KV)]
            units = [(b, qc, g, kc) for (b, qc, g) in jobs for kc in range(qc, -1, -1)]
            masked = [kc == qc or window for (b, qc, g, kc) in units]
            first_unit = [units.index((b, qc, g, qc)) for (b, qc, g) in jobs] + [len(units)]
            REACH = 32

            def queries(u):
                b, qc, g, kc = units[u]
                return P if kc == qc or not window else REACH

            def cut(ap, u):
                return ap.rearrange("p (a q) -> p a q", a=G4)[:, :, 0:queries(u)]
            sc_done, ex_done, mask_done, pv_done, o_done, o_turned, normed, turned, aot, y_made = [bsem(f"{tag}_{n}") for n in
                                ("sc", "ex", "mask", "pv", "o", "ot", "normed", "turned", "aot", "y")]
            recip_s = bsem(f"{tag}_recip")
            oT = [bigB[:, 3 + t, :] for t in range(NT)]
            with nc.Block(no_gpsimd_drain=True) as block:
                @block.tensor
                def _(pe):
                    def scores(j):
                        for u in range(first_unit[j], first_unit[j + 1]):
                            b, qc, g, kc = units[u]
                            if u >= 4:
                                pe.wait_ge(ex_done, u - 3)
                            nc.tensor.matmul(cut(bank[u % 4][:, :], u), kz[:, g, b * SC + kc, :],
                                             qT[:, b * SC + qc, :, 0:queries(u)], start=True, stop=True).then_inc(sc_done, 1)

                    def values(j):
                        b, qc, g = jobs[j]
                        t = b * SC + qc
                        if g == 0 and t >= 2:
                            pe.wait_ge(o_done, t - 1)
                        for u in range(first_unit[j], first_unit[j + 1]):
                            kc = units[u][3]
                            pe.wait_ge(ex_done, u + 1)
                            if masked[u]:
                                pe.wait_ge(mask_done, sum(masked[:u + 1]))
                            last = nc.tensor.matmul(cut(bank[4 + t % 2][32 * g:32 * g + 32, :], u), vx[:, b * SC + kc, g, :],
                                                    cut(pr[u % 4], u), start=kc == qc, stop=kc == 0)
                        last.then_inc(pv_done, 1)

                    def to_tokens(t):
                        pe.wait_ge(o_done, t + 1)
                        if t >= 2:
                            pe.wait_ge(normed, t - 1)
                        for a in range(G4):
                            last = nc.tensor.transpose(bank[6 + t % 2][:, a * P:(a + 1) * P], oT[t][:, a * P:(a + 1) * P], ident)
                        last.then_inc(o_turned, 1)
                    scores(0)
                    for j in range(len(jobs) + 2):
                        if j + 1 < len(jobs):
                            scores(j + 1)
                        if j < len(jobs):
                            values(j)
                        if j >= 5 and (j - 5) % KV == 0:
                            to_tokens((j - 5) // KV)
                    pe.wait_ge(normed, NT)
                    for t in range(NT):
                        last = nc.tensor.transpose(bank[0][:, t * P:(t + 1) * P], ao[:, t, :, :].rearrange("p h d -> p (h d)"), ident)
                    last.then_inc(turned, 1)
                    pe.wait_ge(aot, 1)
                    for t in range(NT):
                        last = nc.tensor.matmul(bank[1][:, t * P:(t + 1) * P], aoT[:, t * P:(t + 1) * P], wo, start=True, stop=True)
                    last.then_inc(y_made, 1)

                @block.scalar
                def _(act):
                    for j in range(len(jobs) + 2):
                        for u in range(first_unit[j], first_unit[j + 1]) if j < len(jobs) else ():
                            act.wait_ge(sc_done, u + 1)
                            if u >= 4:
                                act.wait_ge(pv_done, jobs.index(units[u - 4][0:3]) + 1)
                            act.activation(cut(pr[u % 4], u), cut(bank[u % 4][:, :], u), ACT.Exp, scale=float(1.0 / np.sqrt(8.0)))\
                               .then_inc(ex_done, 1)
                        if j >= 5 and (j - 5) % KV == 0:
                            t = (j - 5) // KV
                            act.wait_ge(pv_done, KV * (t + 1))
                            act.activation(oT[t], bank[4 + t % 2][:, :], ACT.Copy).then_inc(o_done, 1)
                    act.wait_ge(turned, 1)
                    act.activation(aoT, bank[0][:, :], ACT.Copy).then_inc(aot, 1)

                @block.vector
                def _(dve):
                    for j in range(len(jobs) + 3):
                        for u in range(first_unit[j], first_unit[j + 1]) if j < len(jobs) else ():
                            if masked[u]:
                                b, qc, g, kc = units[u]
                                m = W("const", ("near" if window else "causal") if kc == qc else "near_prev")[:, 0:queries(u)]
                                dve.wait_ge(ex_done, u + 1)
                                v = cut(pr[u % 4], u)
                                dve.tensor_tensor(v, v, m.unsqueeze(1).broadcast_to([P, G4, queries(u)]), ALU.mult).then_inc(mask_done, 1)
                        if j >= 6 and (j - 6) % KV == 0:
                            t = (j - 6) // KV
                            o = bank[6 + t % 2][:, :].rearrange("p (a g d) -> p g a d", a=G4, g=KV)
                            dve.wait_ge(o_turned, t + 1)
                            dve.reciprocal(rec[:, t, :].rearrange("p (g a) -> p g a", g=KV), o[:, :, :, 8]).then_inc(recip_s, 1)
                            dve.wait_ge(recip_s, t + 1)
                            dve.tensor_tensor(ao[:, t, :, :].rearrange("p (g a) d -> p g a d", g=KV), o[:, :, :, 0:8],
                                              rec[:, t, :].rearrange("p (g a) -> p g a", g=KV).unsqueeze(3).broadcast_to([P, KV, G4, 8]),
                                              ALU.mult).then_inc(normed, 1)
                    dve.wait_ge(y_made, 1)
                    dve.tensor_tensor(x_tok[:, :, :], v3(bank[1][:, :], NT), x_tok[:, :, :], ALU.add)

        def add_saved():
            with nc.Block(no_gpsimd_drain=True) as block:
                @block.vector
                def _(dve):
                    dve.tensor_tensor(r_tok[:, :, :], acc[:, :, :], x_tok[:, :, :], ALU.add)

        def save_x():
            with nc.Block(no_gpsimd_drain=True) as block:
                @block.vector
                def _(dve):
                    dve.tensor_copy(acc[:, :, :], x_tok[:, :, :])

        def l2_experts():
            made, negexp, step_s, gated = bsem("l2e_made"), bsem("l2e_exp"), bsem("l2e_step"), bsem("l2e_gated")
            up, silu, hid, down = bsem("l2e_up"), bsem("l2e_silu"), bsem("l2e_hid"), bsem("l2e_down")
            lg = v3(tiny[:, 0, :], NT)
            sc_ = v3(tiny[:, 1, :], NT)
            s1, s2, s3 = W("l2f", "s1"), W("l2f", "s2"), v3(W("l2f", "s3"), 4)
            w12, w3 = W("l2f", "w12"), v3(W("l2f", "w3"), NE)
            jobs = [(s1[:, c * P:(c + 1) * P], s2[:, c * P:(c + 1) * P]) for c in range(4)]
            jobs += [(w12[:, 2 * e * P:(2 * e + 1) * P], w12[:, (2 * e + 1) * P:(2 * e + 2) * P]) for e in range(NE)]
            sl = [bigB[:, k, :] for k in range(2)]
            hb = [bigA[:, k, :] for k in range(8)]
            with nc.Block(no_gpsimd_drain=True) as block:
                @block.tensor
                def _(pe):
                    for t in range(NT):
                        last = nc.tensor.matmul(bank[7][:, t * NE:(t + 1) * NE], xT[:, t * P:(t + 1) * P], W("l2f", "rw"), start=True, stop=True)
                    last.then_inc(made, 1)

                    def downs(k):
                        pe.wait_ge(hid, 4 + k)
                        if k >= 2:
                            pe.wait_ge(gated, k - 1)
                        for t in range(NT):
                            for c in range(4 if k == 0 else 1):
                                h = hb[c] if k == 0 else hb[4 + (k - 1) % 4]
                                last = nc.tensor.matmul(bank[4 + k % 2][:, t * P:(t + 1) * P], h[:, t * P:(t + 1) * P],
                                                        s3[:, c, :] if k == 0 else w3[:, k - 1, :], start=c == 0, stop=c == (3 if k == 0 else 0))
                        last.then_inc(down, 1)
                    for j, (a, b_) in enumerate(jobs):
                        if j >= 2:
                            pe.wait_ge(hid, j - 1)
                        nc.tensor.matmul(bank[2 * (j % 2)][:, :], a, xT[:, :], start=True, stop=True).then_inc(up, 1)
                        nc.tensor.matmul(bank[2 * (j % 2) + 1][:, :], b_, xT[:, :], start=True, stop=True).then_inc(up, 1)
                        if j >= 4:
                            downs(j - 4)
                    downs(NE)

                @block.scalar
                def _(act):
                    act.wait_ge(made, 1)
                    act.activation(tiny[:, 0, :], bank[7][:, 0:NT * NE], ACT.Sigmoid).then_inc(negexp, 1)
                    for j in range(len(jobs)):
                        act.wait_ge(up, 2 * j + 1)
                        if j >= 2:
                            act.wait_ge(hid, j - 1)
                        act.activation(sl[j % 2], bank[2 * (j % 2)][:, :], ACT.Silu).then_inc(silu, 1)

                @block.vector
                def _(dve):
                    step = Chain(dve, step_s)

                    def hidden(j):
                        dve.wait_ge(silu, j + 1)
                        dve.wait_ge(up, 2 * j + 2)
                        if j >= 8:
                            dve.wait_ge(down, j - 6)
                        dve.tensor_tensor(hb[j if j < 4 else 4 + j % 4], sl[j % 2], bank[2 * (j % 2) + 1][:, :], ALU.mult).then_inc(hid, 1)

                    def gate(k):
                        dve.wait_ge(down, k + 1)
                        if k == 0:
                            step(dve.tensor_tensor(r_tok[:, :, :], v3(bank[4][:, :], NT), x_tok[:, :, :], ALU.add))
                            dve.sem_inc(gated, 1)
                            return
                        for t in range(NT):
                            dve.scalar_tensor_tensor(out=r_tok[:, t, :], in0=bank[4 + k % 2][:, t * P:(t + 1) * P],
                                                     scalar=weights_of[:, t, k - 1:k], in1=r_tok[:, t, :], op0=ALU.mult, op1=ALU.add)\
                               .then_inc(step_s, 1)
                            step.n += 1
                        dve.wait_ge(step_s, step.n)
                        dve.sem_inc(gated, 1)
                    dve.wait_ge(negexp, 1)
                    step(dve.tensor_tensor(sc_, lg, W("l2f", "eb").unsqueeze(1).broadcast_to([P, NT, NE]), ALU.add))
                    mxs, h1, h2 = top2(dve, step, sc_, NE)
                    step(dve.tensor_tensor(h1, h1, h2, ALU.add))
                    step(dve.tensor_tensor(weights_of, h1, lg, ALU.mult))
                    for j in range(len(jobs)):
                        hidden(j)
                        if j >= 5:
                            gate(j - 5)
                    gate(NE - 1)
                    gate(NE)

        ktok = flat3 = None

        def l3_attention():
            qtok, ktok = bigD, bias_t[:, :, :].rearrange("p h s -> p (h s)").rearrange("p (t n) -> p t n", t=NT)
            jobs = [(w, t, h) for w in ("wq", "wk", "wv") for t in range(NT) for h in range(2)]
            tok = {"wq": qtok, "wk": ktok, "wv": bigC}
            n2 = acc[:, 0, :]
            sqs = [bigA[:, k, :] for k in range(2)]
            made, copied, squared, summed, lens, esd, nq = [bsem(f"l3p_{n}") for n in
                                                            ("made", "copied", "squared", "summed", "lens", "es", "nq")]
            es = acc[:, 1, 0:NH]
            rn = tiny[:, 8:12, :].rearrange("p a b -> p (a b)")
            with nc.Block(no_gpsimd_drain=True) as block:
                @block.tensor
                def _(pe):
                    for i, (w, t, h) in enumerate(jobs):
                        if i >= 8:
                            pe.wait_ge(copied, i - 7)
                            if i - 8 < 16:
                                pe.wait_ge(squared, i - 7)
                        nc.tensor.matmul(bank[i % 8][:, :], xT[:, t * P:(t + 1) * P], W("l3a", w)[:, h * 512:(h + 1) * 512],
                                         start=True, stop=True).then_inc(made, 1)

                @block.scalar
                def _(act):
                    act.activation(es, W("l3a", "scale"), ACT.Exp).then_inc(esd, 1)
                    for i, (w, t, h) in enumerate(jobs):
                        act.wait_ge(made, i + 1)
                        act.activation(tok[w][:, t, h * 512:(h + 1) * 512], bank[i % 8][:, :], ACT.Copy).then_inc(copied, 1)
                        if w != "wv":
                            if i >= 2:
                                act.wait_ge(summed, i - 1)
                            act.activation(sqs[i % 2], bank[i % 8][:, :], ACT.Square).then_inc(squared, 1)

                @block.vector
                def _(dve):
                    for i, (w, t, h) in enumerate(jobs):
                        if w != "wv":
                            dve.wait_ge(squared, i + 1)
                            dve.tensor_reduce(n2[:, i * 8:(i + 1) * 8], v3(sqs[i % 2], 8), op=ALU.add, axis=AX).then_inc(summed, 1)
                    dve.wait_ge(summed, 16)
                    step = Chain(dve, lens)
                    step(dve.tensor_scalar(n2, n2, 1e-24, None, ALU.max))
                    rsqrt(dve, step, n2, rn, newton[:, :])
                    dve.wait_ge(esd, 1)
                    dve.tensor_tensor(v3(rn[:, 0:64], NT), v3(rn[:, 0:64], NT), es.unsqueeze(1).broadcast_to([P, NT, NH]), ALU.mult).then_inc(nq, 1)

            scaled, turned, act_out = [bsem(f"l3t_{n}") for n in ("scaled", "turned", "act_out")]
            items = [(0, c) for c in range(NCH)] + [(1, c) for c in range(NCH)]
            with nc.Block(no_gpsimd_drain=True) as block:
                @block.vector
                def _(dve):
                    def scale_tile(k):
                        w, t = k // NT, k % NT
                        v = (qtok if w == 0 else ktok)[:, t, :].rearrange("p (h d) -> p h d", d=HD)
                        dve.tensor_tensor(v, v, rn[:, w * 64 + t * NH:w * 64 + (t + 1) * NH].unsqueeze(2).broadcast_to([P, NH, HD]), ALU.mult)\
                           .then_inc(scaled, 1)
                    for k in range(2 * NT):
                        scale_tile(k)

                @block.tensor
                def _(pe):
                    for i, (w, c) in enumerate(items):
                        pe.wait_ge(scaled, NT * (w + 1))
                        if i >= 8:
                            pe.wait_ge(act_out, i - 7)
                        for t in range(NT):
                            last = nc.tensor.transpose(bank[i % 8][:, t * P:(t + 1) * P], (qtok if w == 0 else ktok)[:, t, c * P:(c + 1) * P], ident)
                        last.then_inc(turned, 1)

                @block.scalar
                def _(act):
                    for i, (w, c) in enumerate(items):
                        act.wait_ge(turned, i + 1)
                        if w == 0:
                            act.activation(bigA[:, c, :], bank[i % 8][:, :], ACT.Copy).then_inc(act_out, 1)
                        else:
                            act.activation(keys_even[0:HD, c, :], bank[i % 8][0:HD, :], ACT.Copy)
                            act.activation(keys_odd[HD:P, c, :], bank[i % 8][HD:P, :], ACT.Copy).then_inc(act_out, 1)
            heads("l3h", lambda h: (keys_even, keys_odd)[h % 2][:, h // 2, :], lambda h: h * HD, False)
            out_proj("l3o", W("l3a", "wo"), bias=W("l3a", "bo"))

        def l3_experts():
            E4 = 4
            PAIRS = ((0, 1), (2, 3))
            lg = v3(tiny[:, 0, :], NT)
            e_t, r_t, d_t = token_value(1), token_value(2), token_value(3)
            made, shifted, exped, weighed, wt, step_s = [bsem(f"l3f_{n}") for n in ("made", "shifted", "exped", "weighed", "wt", "step")]
            up, ubias, ustat, umean, uscale, un, ut, h_done, down = [bsem(f"l3f_{n}") for n in
                ("up", "ubias", "ustat", "umean", "uscale", "un", "ut", "h", "down")]
            dbias, dstat, dmean, dscale, dn = [bsem(f"l3f_{n}") for n in ("dbias", "dstat", "dmean", "dscale", "dn")]
            be_made = bsem("l3f_be")
            wtd = bsem("l3f_wtd")
            hid_n = flat(bigA)[:, 0:2048].rearrange("p (e t d) -> p e t d", e=E4, t=NT)
            out_n = flat(bigA)[:, 2048:4096].rearrange("p (e t d) -> p e t d", e=E4, t=NT)
            offset = newton[:, 64:80]
            hT = [bigC[:, k, 0:512] for k in range(4)]
            w1, w2 = W("l3f", "w1"), W("l3f", "w2")
            b1, b2, g2 = W("l3f", "b1"), W("l3f", "b2"), W("l3f", "g2")
            with nc.Block(no_gpsimd_drain=True) as block:
                @block.tensor
                def _(pe):
                    for t in range(NT):
                        last = nc.tensor.matmul(bank[7][:, t * 8:t * 8 + E4], xT[:, t * P:(t + 1) * P], W("l3f", "gw"), start=True, stop=True)
                    last.then_inc(made, 1)

                    def times(e, xs, w, done):
                        for t in range(NT):
                            last = nc.tensor.matmul(bank[e][:, t * P:(t + 1) * P], xs[:, t * P:(t + 1) * P], w[:, e * P:(e + 1) * P],
                                                    start=True, stop=True)
                        last.then_inc(done, 1)
                    for e in range(E4):
                        times(e, xT, w1, up)
                    pe.wait_ge(weighed, 1)
                    for t in range(NT):
                        last = nc.tensor.transpose(bank[4][0:8, t * P:(t + 1) * P], weights_of[:, t, :], ident)
                    last.then_inc(wt, 1)
                    for pair in PAIRS:
                        for e in pair:
                            pe.wait_ge(un, NT * (e + 1))
                            for t in range(NT):
                                last = nc.tensor.transpose(bank[e][:, t * P:(t + 1) * P], hid_n[:, e, t, :], ident)
                            last.then_inc(ut, 1)
                        for e in pair:
                            pe.wait_ge(h_done, e + 1)
                            times(e, hT[e], w2, down)
                        if pair[0] == 0:
                            pe.wait_ge(wtd, 1)
                            for t in range(NT):
                                last = nc.tensor.matmul(bank[5][:, t * P:(t + 1) * P], weightsT[0:E4, t * P:(t + 1) * P], held["be2"], start=True, stop=True)
                            last.then_inc(be_made, 1)

                @block.scalar
                def _(act):
                    act.wait_ge(shifted, 1)
                    act.activation(e_t, d_t, ACT.Exp).then_inc(exped, 1)
                    act.wait_ge(wt, 1)
                    act.activation(weightsT[:, :], bank[4][0:8, :], ACT.Copy).then_inc(wtd, 1)

                    def normalise(e, y, done):
                        for t in range(NT):
                            k = e * NT + t
                            act.activation(y[:, e, t, :], y[:, e, t, :], ACT.Identity, bias=offset[:, k:k + 1],
                                           scale=rstd[:, k:k + 1]).then_inc(done, 1)
                    for i, pair in enumerate(PAIRS):
                        act.wait_ge(uscale, i + 1)
                        for e in pair:
                            normalise(e, hid_n, un)
                        for e in pair:
                            act.wait_ge(ut, e + 1)
                            act.activation(hT[e], bank[e][:, :], ACT.Relu, bias=W("l3f", "be1")[:, e:e + 1],
                                           scale=W("l3f", "g1")[:, e:e + 1]).then_inc(h_done, 1)
                    for i, pair in enumerate(PAIRS):
                        act.wait_ge(dscale, i + 1)
                        for e in pair:
                            normalise(e, out_n, dn)

                @block.vector
                def _(dve):
                    step = Chain(dve, step_s)
                    step(dve.memset(tiny[:, 0, :], -3.0e38))
                    dve.wait_ge(made, 1)
                    step(dve.tensor_tensor(lg[:, :, 0:E4], v3(bank[7][:, 0:NT * 8], NT)[:, :, 0:E4],
                                           W("l3f", "gb").unsqueeze(1).broadcast_to([P, NT, E4]), ALU.add))
                    mxs, h1, h2 = top2(dve, step, lg, E4)
                    softmax_of_two(dve, (shifted, exped), step, mxs, h1, h2, weights_of, e_t, r_t, d_t)
                    dve.sem_inc(weighed, 1)

                    def moments(pair, src_done, bias, y, sb_, ss, sm_):
                        ks = range(pair[0] * NT, (pair[-1] + 1) * NT)
                        for e in pair:
                            dve.wait_ge(src_done, e + 1)
                            dve.tensor_tensor(y[:, e, :, :], v3(bank[e][:, :], NT),
                                              bias[:, e * P:(e + 1) * P].unsqueeze(1).broadcast_to([P, NT, P]), ALU.add).then_inc(sb_, 1)
                            dve.wait_ge(sb_, e + 1)
                            for t in range(NT):
                                dve.bn_stats(stats[:, e * NT + t, :], y[:, e, t, :]).then_inc(ss, 1)
                        for k in ks:
                            dve.wait_ge(ss, k + 1)
                            dve.bn_aggr(mv[:, k, :], stats[:, k, :]).then_inc(sm_, 1)
                        dve.wait_ge(sm_, ks[-1] + 1)
                        cut = slice(ks[0], ks[-1] + 1)
                        step(dve.tensor_scalar(var_e[:, cut], mv[:, cut, 1], LN_EPS, None, ALU.add))
                        rsqrt(dve, step, var_e[:, cut], rstd[:, cut], newton[:, cut])
                        return cut

                    def offsets(cut, done):
                        dve.scalar_tensor_tensor(out=offset[:, cut], in0=mv[:, cut, 0], scalar=-1.0, in1=rstd[:, cut],
                                                 op0=ALU.mult, op1=ALU.mult).then_inc(done, 1)
                    for pair in PAIRS:
                        offsets(moments(pair, up, b1, hid_n, ubias, ustat, umean), uscale)
                    for i, pair in enumerate(PAIRS):
                        cut = moments(pair, down, b2, out_n, dbias, dstat, dmean)
                        step(dve.tensor_tensor(v3(rstd[:, cut], 2), v3(rstd[:, cut], 2),
                                               weights_of[:, :, pair[0]:pair[-1] + 1].rearrange("p t e -> p e t"), ALU.mult))
                        offsets(cut, dscale)
                        if i == 0:
                            dve.wait_ge(be_made, 1)
                            step(dve.scalar_tensor_tensor(out=r_tok[:, :, :], in0=x_tok[:, :, :], scalar=2.0, in1=v3(bank[5][:, :], NT),
                                                          op0=ALU.mult, op1=ALU.add))
                    for e in range(E4):
                        dve.wait_ge(dn, NT * (e + 1))
                        step(dve.tensor_tensor(out_n[:, e, :, :], out_n[:, e, :, :],
                                               g2[:, e * P:(e + 1) * P].unsqueeze(1).broadcast_to([P, NT, P]), ALU.mult))
                        step(dve.tensor_tensor(r_tok[:, :, :], r_tok[:, :, :], out_n[:, e, :, :], ALU.add))

        def wait_for(eng, pks):
            for pk in pks:
                eng.wait_ge(loaded[pk], 16)

        first_loads()
        put_nothing()
        l0_bias()
        expms()
        l0_bias_table()
        with nc.Block(no_gpsimd_drain=True) as block:
            @block.vector
            def _(dve):
                wait_for(dve, ("first", "const", "l0a"))
                dve.wait_ge(loaded_x, 16)
                dve.wait_ge(zeroed, 32)
        zero_beside_keys()
        with nc.Fori(0, GROUPS) as g:
            take_x("l0x", g)
            l0_attention()
            post_norm("l0n")
            route0(g)
            end_of_body()
        end_of_loop()
        load_early()
        all_put()
        with nc.Fori(0, NE // 2) as pair:
            expert_pair(pair * 2)
            end_of_body()
        end_of_loop()
        fetch_first()
        fold_lora()
        zero_beside_keys1()
        with nc.Fori(0, GROUPS) as g:
            combine0(g)
            post_norm("l0m")
            l1_project(g)
            heads("l1h", lambda h: bigB[:, 2 * (h // 4) + h % 2, :], lambda h: h // 4 * HD, False)
            out_proj("l1o", W("l1a", "wo"))
            post_norm("l1n")
            pre_norm("l1q", W("l1f", "gamma"), W("l1f", "beta"), True, bigC[:, 0, 0:512], bigC[:, 0, 512:1024])
            l1_route()
            l1_experts()
            l1_mix()
            post_norm("l1y")
            keep_x(g)
            end_of_body()
        end_of_loop()
        load_late()
        with nc.Fori(0, GROUPS) as g:
            take_x("l2x", g)
            save_x()
            pre_norm("gn", W("l2a", "n1"), None, False, bigB[:, 0, :], bigB[:, 1, :])
            narrow("g", W("l2a", "g_wq"), held["l2up"], W("l2a", "g_wo"), W("l2a", "g_down"), False)
            pre_norm("ln", W("l2a", "n2"), None, False, bigB[:, 0, :], bigB[:, 1, :])
            narrow("l", W("l2a", "l_wq"), W("l2a", "l_wkv"), W("l2a", "l_wo"), None, True)
            add_saved()
            post_norm("l2n")
            l2_experts()
            post_norm("l2m")
            keep_x(g)
            end_of_body()
        end_of_loop()
        zero_beside_keys()
        with nc.Fori(0, GROUPS) as g:
            take_x("l3x", g)
            l3_attention()
            post_norm("l3n")
            l3_experts()
            post_norm("l3m", True, g)
            end_of_body()
        end_of_loop()
        all_stored()


def kernel(**inputs):
    import numpy as _np
    import concourse.bacc as _bacc
    from concourse import mybir as _mybir
    from concourse.bass_utils import run_bass_kernel_spmd as _run

    w = {n: _np.asarray(a) for n, a in inputs.items()}
    nc = _bacc.Bacc("TRN2", target_bir_lowering=False, num_devices=1)
    f32 = _mybir.dt.float32
    x = _np.ascontiguousarray(w["L0_attn_x"])
    arrays, packs, where = {"in_x": x}, {}, {}
    x_dram = nc.dram_tensor("in_x", x.shape, f32, kind="ExternalInput").ap()
    for pk, parts in layout(w).items():
        at, where[pk] = 0, {}
        for name, a in parts:
            where[pk][name] = (at, at + a.shape[1])
            at += a.shape[1]
        a = _np.ascontiguousarray(_np.concatenate([a for _, a in parts], axis=1))
        arrays[f"in_{pk}"] = a
        packs[pk] = nc.dram_tensor(f"in_{pk}", a.shape, f32, kind="ExternalInput").ap()
    out = nc.dram_tensor("out", (ALL_B, S, P), f32, kind="ExternalOutput").ap()
    dram = {"rpe": nc.dram_tensor("rpe_rows", (NH, S + P), f32, kind="Internal").ap(),
            "slots": nc.dram_tensor("slots", (ALL_T, P), f32, kind="Internal").ap(),
            "results": nc.dram_tensor("results", (ALL_T, P), f32, kind="Internal").ap()}
    program(nc, x_dram, packs, where, out, dram)
    r = _run(nc, [arrays], core_ids=[0])
    return r.results[0]["out"]
```
